# Optimizing a Trainium2 kernel written in Bass

```python
import numpy as np
import jax
import jax.numpy as jnp

def _softmax(x, axis=-1):
    return jax.nn.softmax(x, axis=axis)

def _gelu(x):
    return jax.nn.gelu(x, approximate=True)

def _silu(x):
    return jax.nn.silu(x)

def _sigmoid(x):
    return jax.nn.sigmoid(x)

def _layernorm(x, axis=-1, eps=1e-05):
    m = jnp.mean(x, axis=axis, keepdims=True)
    v = jnp.var(x, axis=axis, keepdims=True)
    return (x - m) / jnp.sqrt(v + eps)

def _scatter_add(tgt, idx, src, axis=0):
    return tgt.at[idx].add(src)

def _segment_sum(src, seg, n):
    return jax.ops.segment_sum(src, seg, n)
kernel_name = 'mk_xattn_ffn_d2_seqx_r4_3944a2'

def setup_inputs(seed: int=0):
    np.random.seed(seed)
    _w = jnp.asarray

    def _rec_inputs():
        import jax
        import jax.numpy as jnp
        _rk = jax.random.key(seed)
        x = -0.0003929 + 0.9999 * jax.random.normal(jax.random.fold_in(_rk, 1), (64, 128, 256), jnp.float32)
        _lenS = 128 - jax.random.randint(jax.random.fold_in(_rk, 7), (64,), 0, max(1, 128 // 4) + 1, jnp.int32)
        _lenS2 = 128 - jax.random.randint(jax.random.fold_in(_rk, 8), (64,), 0, max(1, 128 // 4) + 1, jnp.int32)
        _ctx_768P = jax.random.normal(jax.random.fold_in(_rk, 11), (64, 16, 192), jnp.float32)
        _ctx_768c = jax.random.dirichlet(jax.random.fold_in(_rk, 511), 0.3 * jnp.ones((16,), jnp.float32), (64, 128))
        _ctx_768t = jnp.einsum('bsk,bkd->bsd', _ctx_768c, _ctx_768P)
        _ctx_768t = _ctx_768t * jax.lax.rsqrt(jnp.mean(jnp.square(_ctx_768t)) + 1e-12) * 0.953939
        ctx_768 = 0.00095986 + 0.999812 * (_ctx_768t + 0.3 * jax.random.normal(jax.random.fold_in(_rk, 611), (64, 128, 192), jnp.float32))
        _validS = jnp.arange(128)[None, :] < _lenS[:, None]
        _validS2 = jnp.arange(128)[None, :] < _lenS2[:, None]
        _causal = jnp.tril(jnp.ones((128, 128), dtype=bool))
        mask_BxS2_bf1 = jnp.ones((64, 128), dtype=bool)
        return (x, ctx_768, mask_BxS2_bf1)
    x, ctx_768, mask_BxS2_bf1 = _rec_inputs()

    def _L0_xattn_setup():
        import jax, jax.numpy as jnp
        import numpy as np
        DIM = 256
        CTX_DIM = 192
        HEADS = 16
        key = jax.random.key(seed)
        ks = jax.random.split(key, 7)
        B, N, M = (4, 1024, 64)
        x = jax.random.normal(ks[0], (B, N, DIM), dtype=jnp.float32)
        context = jax.random.normal(ks[1], (B, M, CTX_DIM), dtype=jnp.float32)
        context_mask = jnp.ones((B, M), dtype=bool)
        s_d = 1.0 / np.sqrt(DIM)
        s_c = 1.0 / np.sqrt(CTX_DIM)
        Wq = jax.random.normal(ks[2], (DIM, DIM), dtype=jnp.float32) * s_d
        Wk = jax.random.normal(ks[3], (CTX_DIM, DIM), dtype=jnp.float32) * s_c
        Wv = jax.random.normal(ks[4], (CTX_DIM, DIM), dtype=jnp.float32) * s_c
        Wo = jax.random.normal(ks[5], (DIM, DIM), dtype=jnp.float32) * s_d
        return {'x': x, 'context': context, 'context_mask': context_mask, 'Wq': Wq, 'Wk': Wk, 'Wv': Wv, 'Wo': Wo}
    _L0_xattn_all = _L0_xattn_setup()
    _L0_xattn_in = {k: v for k, v in _L0_xattn_all.items() if k in ('Wq', 'Wk', 'Wv', 'Wo')}
    del _L0_xattn_all

    def _L0_ffn_setup():
        import jax, jax.numpy as jnp
        import numpy as np
        D_MODEL = 256
        EXPERT_DIM = 1024
        N_EXPERTS = 8
        CAP_FACTOR = 0.5
        key = jax.random.key(seed)
        ks = jax.random.split(key, 7)
        inp = {'input': jax.random.normal(ks[0], (4, 1024, D_MODEL), dtype=jnp.float32), 'w_switch': jax.random.normal(ks[1], (D_MODEL, N_EXPERTS), dtype=jnp.float32) * 0.02, 'b_switch': jnp.zeros((N_EXPERTS,), jnp.float32), 'w1': jax.random.normal(ks[2], (N_EXPERTS, D_MODEL, EXPERT_DIM), dtype=jnp.float32) * 0.02, 'b1': jnp.zeros((N_EXPERTS, EXPERT_DIM), jnp.float32), 'w2': jax.random.normal(ks[3], (N_EXPERTS, EXPERT_DIM, D_MODEL), dtype=jnp.float32) * 0.02, 'b2': jnp.zeros((N_EXPERTS, D_MODEL), jnp.float32)}
        return inp
    _L0_ffn_all = _L0_ffn_setup()
    _L0_ffn_in = {k: v for k, v in _L0_ffn_all.items() if k in ('w_switch', 'b_switch', 'w1', 'b1', 'w2', 'b2')}
    del _L0_ffn_all

    def _L1_xattn_setup():
        import jax, jax.numpy as jnp
        import numpy as np
        IMAGE_DIM = 256
        TEXT_DIM = 192
        NUM_HEADS = 16
        HEAD_DIM = IMAGE_DIM // NUM_HEADS
        key = jax.random.key(seed)
        ks = jax.random.split(key, 14)
        B, N, M = (4, 1024, 128)
        s_img = 1.0 / np.sqrt(IMAGE_DIM)
        s_txt = 1.0 / np.sqrt(TEXT_DIM)
        s_ff = 1.0 / np.sqrt(2 * IMAGE_DIM)
        return {'x': jax.random.normal(ks[0], (B, N, IMAGE_DIM), jnp.float32), 'y': jax.random.normal(ks[1], (B, M, TEXT_DIM), jnp.float32), 'Wq': jax.random.normal(ks[2], (IMAGE_DIM, IMAGE_DIM), jnp.float32) * s_img, 'bq': jax.random.normal(ks[3], (IMAGE_DIM,), jnp.float32) * s_img, 'Wk': jax.random.normal(ks[4], (TEXT_DIM, IMAGE_DIM), jnp.float32) * s_txt, 'bk': jax.random.normal(ks[5], (IMAGE_DIM,), jnp.float32) * s_txt, 'Wv': jax.random.normal(ks[6], (TEXT_DIM, IMAGE_DIM), jnp.float32) * s_txt, 'bv': jax.random.normal(ks[7], (IMAGE_DIM,), jnp.float32) * s_txt, 'W1': jax.random.normal(ks[8], (IMAGE_DIM, 2 * IMAGE_DIM), jnp.float32) * s_img, 'b1': jax.random.normal(ks[9], (2 * IMAGE_DIM,), jnp.float32) * s_img, 'W2': jax.random.normal(ks[10], (2 * IMAGE_DIM, IMAGE_DIM), jnp.float32) * s_ff, 'b2': jax.random.normal(ks[11], (IMAGE_DIM,), jnp.float32) * s_ff}
    _L1_xattn_all = _L1_xattn_setup()
    _L1_xattn_in = {k: v for k, v in _L1_xattn_all.items() if k in ('Wq', 'bq', 'Wk', 'bk', 'Wv', 'bv', 'W1', 'b1', 'W2', 'b2')}
    del _L1_xattn_all

    def _L1_ffn_setup():
        import jax, jax.numpy as jnp
        import numpy as np
        NUM_NOD = 6
        MAX_PREV = 5
        NUM_EDGE = 20
        D = 256
        H = 8
        LN_EPS = 1e-06

        def _layernorm(x, g, b):
            mu = jnp.mean(x, axis=-1, keepdims=True)
            var = jnp.mean(jnp.square(x - mu), axis=-1, keepdims=True)
            return (x - mu) * jax.lax.rsqrt(var + LN_EPS) * g + b

        def _mha(q, k, v, wq, wk, wv, wo):
            B, S, d = q.shape
            dh = d // H
            qh = (q @ wq).reshape(B, S, H, dh)
            kh = (k @ wk).reshape(B, S, H, dh)
            vh = (v @ wv).reshape(B, S, H, dh)
            scores = jnp.einsum('bqhd,bkhd->bhqk', qh, kh) / jnp.sqrt(jnp.asarray(dh, q.dtype))
            attn = jax.nn.softmax(scores, axis=-1)
            ctx = jnp.einsum('bhqk,bkhd->bqhd', attn, vh).reshape(B, S, d)
            return ctx @ wo
        key = jax.random.key(seed)
        ks = jax.random.split(key, 12)
        B, S = (8, 256)
        scale = 1.0 / np.sqrt(D)
        return {'inputs': jax.random.normal(ks[0], (B, S, D), jnp.float32), 'ew': jax.random.uniform(ks[1], (NUM_NOD, 3), jnp.float32), 'act_w': jax.random.uniform(ks[2], (NUM_NOD,), jnp.float32), 'We': jax.random.normal(ks[3], (NUM_EDGE, D, D), jnp.float32) * scale, 'be': jnp.zeros((NUM_EDGE, D), jnp.float32), 'Wq': jax.random.normal(ks[4], (NUM_NOD, D, D), jnp.float32) * scale, 'Wk': jax.random.normal(ks[5], (NUM_NOD, D, D), jnp.float32) * scale, 'Wv': jax.random.normal(ks[6], (NUM_NOD, D, D), jnp.float32) * scale, 'Wo': jax.random.normal(ks[7], (NUM_NOD, D, D), jnp.float32) * scale, 'ln_g': jnp.ones((D,), jnp.float32), 'ln_b': jnp.zeros((D,), jnp.float32)}
    _L1_ffn_all = _L1_ffn_setup()
    _L1_ffn_in = {k: v for k, v in _L1_ffn_all.items() if k in ('ew', 'act_w', 'We', 'be', 'Wq', 'Wk', 'Wv', 'Wo', 'ln_g', 'ln_b')}
    del _L1_ffn_all
    return {'x': x, 'ctx_768': ctx_768, 'mask_BxS2_bf1': mask_BxS2_bf1, 'L0_xattn_Wq': _L0_xattn_in['Wq'], 'L0_xattn_Wk': _L0_xattn_in['Wk'], 'L0_xattn_Wv': _L0_xattn_in['Wv'], 'L0_xattn_Wo': _L0_xattn_in['Wo'], 'L0_ffn_w_switch': _L0_ffn_in['w_switch'], 'L0_ffn_b_switch': _L0_ffn_in['b_switch'], 'L0_ffn_w1': _L0_ffn_in['w1'], 'L0_ffn_b1': _L0_ffn_in['b1'], 'L0_ffn_w2': _L0_ffn_in['w2'], 'L0_ffn_b2': _L0_ffn_in['b2'], 'L1_xattn_Wq': _L1_xattn_in['Wq'], 'L1_xattn_bq': _L1_xattn_in['bq'], 'L1_xattn_Wk': _L1_xattn_in['Wk'], 'L1_xattn_bk': _L1_xattn_in['bk'], 'L1_xattn_Wv': _L1_xattn_in['Wv'], 'L1_xattn_bv': _L1_xattn_in['bv'], 'L1_xattn_W1': _L1_xattn_in['W1'], 'L1_xattn_b1': _L1_xattn_in['b1'], 'L1_xattn_W2': _L1_xattn_in['W2'], 'L1_xattn_b2': _L1_xattn_in['b2'], 'L1_ffn_ew': _L1_ffn_in['ew'], 'L1_ffn_act_w': _L1_ffn_in['act_w'], 'L1_ffn_We': _L1_ffn_in['We'], 'L1_ffn_be': _L1_ffn_in['be'], 'L1_ffn_Wq': _L1_ffn_in['Wq'], 'L1_ffn_Wk': _L1_ffn_in['Wk'], 'L1_ffn_Wv': _L1_ffn_in['Wv'], 'L1_ffn_Wo': _L1_ffn_in['Wo'], 'L1_ffn_ln_g': _L1_ffn_in['ln_g'], 'L1_ffn_ln_b': _L1_ffn_in['ln_b']}

def reference(x, ctx_768, mask_BxS2_bf1, L0_xattn_Wq, L0_xattn_Wk, L0_xattn_Wv, L0_xattn_Wo, L0_ffn_w_switch, L0_ffn_b_switch, L0_ffn_w1, L0_ffn_b1, L0_ffn_w2, L0_ffn_b2, L1_xattn_Wq, L1_xattn_bq, L1_xattn_Wk, L1_xattn_bk, L1_xattn_Wv, L1_xattn_bv, L1_xattn_W1, L1_xattn_b1, L1_xattn_W2, L1_xattn_b2, L1_ffn_ew, L1_ffn_act_w, L1_ffn_We, L1_ffn_be, L1_ffn_Wq, L1_ffn_Wk, L1_ffn_Wv, L1_ffn_Wo, L1_ffn_ln_g, L1_ffn_ln_b):
    import jax
    import jax.numpy as jnp

    def _L0_xattn_ref(x, context, context_mask, Wq, Wk, Wv, Wo):
        import jax, jax.numpy as jnp
        import numpy as np
        DIM = 256
        CTX_DIM = 192
        HEADS = 16
        B, N, _ = x.shape
        M = context.shape[1]
        hd = DIM // HEADS
        scale = hd ** (-0.5)
        q = (x @ Wq).reshape(B, N, HEADS, hd).transpose(0, 2, 1, 3)
        k = (context @ Wk).reshape(B, M, HEADS, hd).transpose(0, 2, 1, 3)
        v = (context @ Wv).reshape(B, M, HEADS, hd).transpose(0, 2, 1, 3)
        scores = jnp.einsum('bhid,bhjd->bhij', q, k) * scale
        max_neg = -jnp.finfo(scores.dtype).max
        scores = jnp.where(context_mask[:, None, None, :], scores, max_neg)
        attn = jax.nn.softmax(scores, axis=-1)
        out = jnp.einsum('bhij,bhjd->bhid', attn, v)
        out = out.transpose(0, 2, 1, 3).reshape(B, N, DIM)
        return out @ Wo

    def _L0_ffn_ref(input, w_switch, b_switch, w1, b1, w2, b2):
        import jax, jax.numpy as jnp
        import numpy as np
        D_MODEL = 256
        EXPERT_DIM = 1024
        N_EXPERTS = 8
        CAP_FACTOR = 0.5
        B, S, D = input.shape
        T = B * S
        E = b_switch.shape[0]
        capacity = int(CAP_FACTOR * T / E)
        x = input.reshape(T, D)
        logits = x @ w_switch + b_switch
        probs = jax.nn.softmax(logits, axis=-1)
        pmax = probs.max(axis=-1)
        routes = probs.argmax(axis=-1)
        oh = (routes[:, None] == jnp.arange(E)[None, :]).astype(jnp.int32)
        pos = (jnp.cumsum(oh, axis=0) * oh).sum(-1) - 1
        keep = pos < capacity
        slot = jnp.where(keep, routes * capacity + pos, E * capacity)
        buf = jnp.zeros((E * capacity + 1, D), x.dtype).at[slot].set(x)
        buf_e = buf[:E * capacity].reshape(E, capacity, D)
        h = jax.nn.relu(jnp.einsum('ecd,edh->ech', buf_e, w1) + b1[:, None, :])
        y = jnp.einsum('ech,ehd->ecd', h, w2) + b2[:, None, :]
        y_flat = jnp.concatenate([y.reshape(E * capacity, D), jnp.zeros((1, D), x.dtype)], axis=0)
        out = jnp.where(keep[:, None], y_flat[slot], x)
        scale = pmax / jax.lax.stop_gradient(pmax)
        out = out * scale[:, None]
        return out.reshape(B, S, D)

    def _L1_xattn_ref(x, y, Wq, bq, Wk, bk, Wv, bv, W1, b1, W2, b2):
        import jax, jax.numpy as jnp
        import numpy as np
        IMAGE_DIM = 256
        TEXT_DIM = 192
        NUM_HEADS = 16
        HEAD_DIM = IMAGE_DIM // NUM_HEADS
        B, N, _ = x.shape
        M = y.shape[1]
        q = (x @ Wq + bq).reshape(B, N, NUM_HEADS, HEAD_DIM)
        k = (y @ Wk + bk).reshape(B, M, NUM_HEADS, HEAD_DIM)
        v = (y @ Wv + bv).reshape(B, M, NUM_HEADS, HEAD_DIM)
        scale = 1.0 / np.sqrt(HEAD_DIM)
        scores = jnp.einsum('bnhd,bmhd->bhnm', q, k) * scale
        attn = jax.nn.softmax(scores, axis=-1)
        out = jnp.einsum('bhnm,bmhd->bnhd', attn, v).reshape(B, N, IMAGE_DIM)
        h = jax.nn.relu(out @ W1 + b1)
        return h @ W2 + b2

    def _L1_ffn_ref(inputs, ew, act_w, We, be, Wq, Wk, Wv, Wo, ln_g, ln_b):
        import jax, jax.numpy as jnp
        import numpy as np
        NUM_NOD = 6
        MAX_PREV = 5
        NUM_EDGE = 20
        D = 256
        H = 8
        LN_EPS = 1e-06

        def _layernorm(x, g, b):
            mu = jnp.mean(x, axis=-1, keepdims=True)
            var = jnp.mean(jnp.square(x - mu), axis=-1, keepdims=True)
            return (x - mu) * jax.lax.rsqrt(var + LN_EPS) * g + b

        def _mha(q, k, v, wq, wk, wv, wo):
            B, S, d = q.shape
            dh = d // H
            qh = (q @ wq).reshape(B, S, H, dh)
            kh = (k @ wk).reshape(B, S, H, dh)
            vh = (v @ wv).reshape(B, S, H, dh)
            scores = jnp.einsum('bqhd,bkhd->bhqk', qh, kh) / jnp.sqrt(jnp.asarray(dh, q.dtype))
            attn = jax.nn.softmax(scores, axis=-1)
            ctx = jnp.einsum('bhqk,bkhd->bqhd', attn, vh).reshape(B, S, d)
            return ctx @ wo
        nodes = {-1: inputs}
        lind = 0
        for c in range(NUM_NOD):
            nsrc = min(c + 1, MAX_PREV)
            snode = c - nsrc
            eq, ek, ev = (lind + nsrc - 1, lind, lind + nsrc // 2)
            in_q, in_k, in_v = (c - 1, snode, snode + nsrc // 2)
            q = ew[c, 0] * (nodes[in_q] @ We[eq] + be[eq])
            k = ew[c, 1] * (nodes[in_k] @ We[ek] + be[ek])
            v = ew[c, 2] * (nodes[in_v] @ We[ev] + be[ev])
            o = _mha(q, k, v, Wq[c], Wk[c], Wv[c], Wo[c])
            nodes[c] = act_w[c] * o + q
            lind += nsrc
        out = nodes[NUM_NOD - 1]
        return _layernorm(out, ln_g, ln_b)
    x = x + _L0_xattn_ref(_layernorm(x, axis=-1), ctx_768, mask_BxS2_bf1, L0_xattn_Wq, L0_xattn_Wk, L0_xattn_Wv, L0_xattn_Wo)
    x = x + _L0_ffn_ref(_layernorm(x, axis=-1), L0_ffn_w_switch, L0_ffn_b_switch, L0_ffn_w1, L0_ffn_b1, L0_ffn_w2, L0_ffn_b2)
    x = x + _L1_xattn_ref(_layernorm(x, axis=-1), ctx_768, L1_xattn_Wq, L1_xattn_bq, L1_xattn_Wk, L1_xattn_bk, L1_xattn_Wv, L1_xattn_bv, L1_xattn_W1, L1_xattn_b1, L1_xattn_W2, L1_xattn_b2)
    x = x + _L1_ffn_ref(_layernorm(x, axis=-1), L1_ffn_ew, L1_ffn_act_w, L1_ffn_We, L1_ffn_be, L1_ffn_Wq, L1_ffn_Wk, L1_ffn_Wv, L1_ffn_Wo, L1_ffn_ln_g, L1_ffn_ln_b)
    return x

_drawn_inputs = setup_inputs


def setup_inputs(seed=0):
    import zlib

    import numpy as np

    out = dict(_drawn_inputs(seed))
    spreads = {'L0_ffn_b_switch': (0.0, 0.1),
     'L0_ffn_b1': (0.0, 0.5),
     'L0_ffn_b2': (0.0, 0.1),
     'L1_ffn_be': (0.0, 0.1),
     'L1_ffn_ln_g': (1.0, 0.2),
     'L1_ffn_ln_b': (0.0, 0.1)}
    factors = {'L1_xattn_bq': 8.0,
     'L1_xattn_bk': 200.0,
     'L1_xattn_b1': 2.702,
     'L1_ffn_Wq': 200.0,
     'L1_ffn_Wk': 200.0}
    for name, (base, spread) in spreads.items():
        noise = np.random.default_rng([zlib.crc32(name.encode()), seed]).standard_normal(out[name].shape)
        drawn = base * np.exp(spread * noise) if base else spread * noise
        out[name] = jnp.asarray(drawn.astype(out[name].dtype))
    for name, factor in factors.items():
        out[name] = (out[name] * factor).astype(out[name].dtype)
    return out
```

```python
from contextlib import ExitStack

import numpy as np

import concourse.bass as bass
from concourse import mybir

F32 = mybir.dt.float32
F32R = mybir.dt.float32r
U8 = mybir.dt.uint8
U32 = mybir.dt.uint32
ALU = mybir.AluOpType
ACT = mybir.ActivationFunctionType
AX = mybir.AxisListType

P = 128
PAIR = 2
STREAMS = 2
ROWS = 4
NEG = 2.0 ** 127


class Tally:

    def __init__(self, turn=0, per=0, base=0):
        self.past, self.n = turn * per + base, 0

    def up(self, k=1):
        self.n += k
        return self.past + self.n

    def now(self):
        return self.past + self.n


def consts_array():
    i = np.arange(P)
    parts = [np.eye(P), i[:, None] <= i[None, :], np.ones((P, P)),
             (i % 32 < 16)[:, None], (i % 32 >= 16)[:, None],
             np.broadcast_to(np.arange(8), (P, 8)), np.full((P, 2), -0.5),
             np.full((P, 2), 1e-5), np.full((P, 2), 1e-6)]
    return np.concatenate([np.asarray(a, np.float32) for a in parts], 1)


C_ID, C_TRI, C_ONE, C_EVEN, C_ODD, C_IOTA, C_HALF, C_EPS5, C_EPS6, C_END = \
    0, 128, 256, 384, 385, 386, 394, 396, 398, 400


def phase_first_attention(nc, io, scratch, keep, cst):
    x, ctx, mask = io["x"], io["ctx_768"], io["mask_BxS2_bf1"]
    B, T, D = x.shape
    C = ctx.shape[2]
    C1 = C - P
    TURNS = B // (PAIR * STREAMS)
    E = io["L0_ffn_w_switch"].shape[1]
    W2 = PAIR * T

    def rows(ap, g, p):
        v = ap.rearrange("(g p b) t d -> g p t b d", p=STREAMS, b=PAIR)
        return v[bass.ds(g, 1), p].rearrange("g t b d -> (g t) b d")

    with ExitStack() as es:
        def sb(name, shape, dt=F32):
            return es.enter_context(nc.sbuf_tensor("a_" + name, [P] + shape, dt))

        def sem(name):
            return es.enter_context(nc.semaphore("a_" + name))

        wq, wk, wv, wo = (sb(n, [2, D]) for n in ("wq", "wk", "wv", "wo"))
        wsw = sb("wsw", [2, E])
        xt = sb("x", [STREAMS, PAIR, D])
        ct = sb("ctx", [STREAMS, PAIR, C])
        mku = sb("mask_u8", [STREAMS, PAIR, T], U8)
        mk = sb("mask_add", [STREAMS, PAIR, T])
        stats = sb("stats", [PAIR, 6])
        after_wait = sb("after_wait", [1])
        mv = sb("mean_var", [STREAMS, PAIR, 2])
        veps = sb("var_eps", [STREAMS, PAIR])
        rstd = sb("rstd", [STREAMS, PAIR])
        xn = sb("xn", [STREAMS, PAIR, D])
        x1 = sb("x1", [STREAMS, PAIR, D])
        xn1 = sb("xn1", [STREAMS, PAIR, D])
        xT = sb("xT", [STREAMS, 2, W2])
        cT = sb("cT", [STREAMS, 2, W2])
        qT = sb("qT", [STREAMS, 2, W2])
        kE = sb("kT_even", [STREAMS, 2, W2])
        kO = sb("kT_odd", [STREAMS, 2, W2])
        vE = sb("v_even", [STREAMS, PAIR, D])
        vO = sb("v_odd", [STREAMS, PAIR, D])
        oT = sb("oT", [STREAMS, 2, W2])
        pr = sb("probs", [STREAMS, PAIR, ROWS, 4, T])
        nmax = sb("neg_max", [STREAMS, PAIR, ROWS, 4])
        rsum = sb("row_sum", [STREAMS, PAIR, ROWS, 4])
        rinv = sb("row_inv", [STREAMS, PAIR, ROWS, 4])
        pT = sb("probsT", [PAIR, ROWS, 4, T])
        S = [es.enter_context(nc.psum_tensor(f"a_scores{r}", [P, 4, T], F32)) for r in range(ROWS)]
        TB = [es.enter_context(nc.psum_tensor(f"a_turned{r}", [P, 4, T], F32)) for r in range(2)]
        M = [es.enter_context(nc.psum_tensor(f"a_product{r}", [P, 2, W2], F32)) for r in range(2)]

        w_in = sem("weights_in")
        x_in = [sem(f"x_in{p}") for p in range(STREAMS)]
        c_in = [sem(f"ctx_in{p}") for p in range(STREAMS)]
        mask_in = [sem(f"mask_in{p}") for p in range(STREAMS)]
        x_used, c_used, mask_used = sem("x_used"), sem("ctx_used"), sem("mask_used")
        x1_out = [sem(f"x1_out{p}") for p in range(STREAMS)]
        xn1_out = [sem(f"xn1_out{p}") for p in range(STREAMS)]
        x1_made, xn1_made = sem("x1_made"), sem("xn1_made")
        zeroed = sem("v_zeroed")
        vstep = sem("vector_step")
        var_made, veps_made, rstd_made = sem("var_made"), sem("veps_made"), sem("rstd_made")
        xn_made = sem("xn_made")
        prod, prod_used = sem("product_made"), sem("product_used")
        sco, sco_used = sem("scores_made"), sem("scores_used")
        max_made, exp_made, inv_made, norm_made = sem("max_made"), sem("exp_made"), sem("inv_made"), sem("norm_made")
        turned, pT_made = sem("turned_made"), sem("pT_made")

        STEPS_A = STREAMS * 3
        PRODS = STREAMS * (5 + 4)
        SLOTS = STREAMS * PAIR * ROWS

        block = es.enter_context(nc.Block())

        @block.sync
        def _(sp):
            for n, t in (("Wq", wq), ("Wo", wo)):
                sp.dma_start(t[:], io["L0_xattn_" + n].rearrange("(c p) n -> p c n", p=P)).then_inc(w_in, 16)
            for n, t in (("Wk", wk), ("Wv", wv)):
                w = io["L0_xattn_" + n]
                sp.dma_start(t[:, 0], w[0:P]).then_inc(w_in, 16)
                sp.dma_start(t[0:C1, 1], w[P:C]).then_inc(w_in, 16)
            sp.dma_start(wsw[:], io["L0_ffn_w_switch"].rearrange("(c p) n -> p c n", p=P)).then_inc(w_in, 16)
            with sp.Fori(0, TURNS) as g:
                for p in range(STREAMS):
                    sp.wait_ge(mask_used, g * STREAMS + p + 1)
                    sp.wait_ge(c_used, g * STREAMS + p + 1)
                    sp.dma_start(ct[:, p], rows(ctx, g, p)).then_inc(c_in[p], 16)
                    m = mask.rearrange("(g p b) t -> g p (b t)", p=STREAMS, b=PAIR)
                    m = m[bass.ds(g, 1), p].rearrange("g n -> (g n)").partition_broadcast(P)
                    sp.dma_start(mku[:, p].rearrange("q b t -> q (b t)"), m).then_inc(mask_in[p], 16)
                    sp.wait_ge(x_used, g * STREAMS + p + 1)
                    sp.dma_start(xt[:, p], rows(x, g, p)).then_inc(x_in[p], 16)

        @block.scalar
        def _(act):
            with act.Fori(0, TURNS) as g:
                t_max, t_turn = Tally(g, SLOTS), Tally(g, SLOTS)
                for p in range(STREAMS):
                    for b in range(PAIR):
                        for r in range(ROWS):
                            act.wait_ge(max_made, t_max.up())
                            for j in range(4):
                                e = pr[:, p, b, r, j]
                                i = nc.scalar.activation(e, e, ACT.Exp, bias=nmax[:, p, b, r, j:j + 1],
                                                         accum_out=rsum[:, p, b, r, j:j + 1])
                            i.then_inc(exp_made, 1)
                for p in range(STREAMS):
                    for b in range(PAIR):
                        for r in range(ROWS):
                            act.wait_ge(turned, t_turn.up())
                            nc.scalar.copy(pT[:, b, r], TB[r % 2][:]).then_inc(pT_made, 1)
                    act.wait_ge(x1_made, g * STREAMS + p + 1)
                    act.dma_start(rows(scratch["x1"], g, p), x1[:, p]).then_inc(x1_out[p], 16)
                    act.wait_ge(xn1_made, g * STREAMS + p + 1)
                    act.dma_start(rows(scratch["xn1"], g, p), xn1[:, p]).then_inc(xn1_out[p], 16)
            for p in range(STREAMS):
                act.wait_ge(x1_out[p], 16 * TURNS + 16)
                act.wait_ge(xn1_out[p], 16 * TURNS + 16)

        @block.gpsimd
        def _(pool):
            nc.gpsimd.memset(vE[:], 0.0).then_inc(zeroed, 1)
            nc.gpsimd.memset(vO[:], 0.0).then_inc(zeroed, 1)
            with pool.Fori(0, TURNS) as g:
                t_var, t_inv = Tally(g, 2 * STREAMS), Tally(g, SLOTS)

                def rsqrt(p):
                    n = t_var.up()
                    pool.wait_ge(var_made, n)
                    nc.gpsimd.tensor_tensor(veps[:, p], mv[:, p, :, 1], cst[:, C_EPS5:C_EPS5 + 2], ALU.add).then_inc(veps_made, 1)
                    pool.wait_ge(veps_made, n)
                    nc.gpsimd.tensor_tensor(rstd[:, p], veps[:, p], cst[:, C_HALF:C_HALF + 2], ALU.pow).then_inc(rstd_made, 1)

                for p in range(STREAMS):
                    rsqrt(p)
                    for b in range(PAIR):
                        for r in range(ROWS):
                            pool.wait_ge(inv_made, t_inv.up())
                            e = pr[:, p, b, r]
                            nc.gpsimd.tensor_tensor(e, e, rinv[:, p, b, r].unsqueeze(2).broadcast_to([P, 4, T]),
                                                    ALU.mult).then_inc(norm_made, 1)
                for p in range(STREAMS):
                    rsqrt(p)

        @block.vector
        def _(dve):
            for s, k in ((x_used, STREAMS), (c_used, STREAMS), (mask_used, STREAMS), (prod_used, 2),
                         (sco_used, ROWS), (pT_made, 2), *((m, 16) for m in x1_out + xn1_out)):
                dve.sem_inc(s, k)
            dve.wait_ge(zeroed, 2)
            with dve.Fori(0, TURNS) as g:
                t_step, t_prod, t_sco = Tally(g, STEPS_A), Tally(g, PRODS), Tally(g, SLOTS)
                t_rstd, t_exp = Tally(g, 2 * STREAMS), Tally(g, SLOTS)

                def chain(i):
                    i.then_inc(vstep, 1)
                    dve.wait_ge(vstep, t_step.up())

                def layer_norm(src, dst, p, made):
                    for b in range(PAIR):
                        i = nc.vector.bn_stats(stats[:, b], src[:, b])
                    chain(i)
                    nc.vector.memset(after_wait[:], 0.0)
                    for b in range(PAIR):
                        i = nc.vector.bn_aggr(mv[:, p, b], stats[:, b])
                    i.then_inc(var_made, 1)
                    dve.wait_ge(rstd_made, t_rstd.up())
                    for b in range(PAIR):
                        i = nc.vector.tensor_scalar(dst[:, b], src[:, b], mv[:, p, b, 0:1], rstd[:, p, b:b + 1],
                                                    ALU.subtract, ALU.mult)
                    i.then_inc(made, 1)

                def product():
                    dve.wait_ge(prod, t_prod.up())
                    return M[(t_prod.n - 1) % 2]

                for p in range(STREAMS):
                    dve.wait_ge(x_in[p], g * 16 + 16)
                    layer_norm(xt[:, p], xn[:, p], p, xn_made)
                    m = product()
                    nc.vector.tensor_copy(xT[:, p], m[:]).then_inc(prod_used, 1)
                    m = product()
                    nc.vector.tensor_copy(cT[:, p, 0], m[:, 0])
                    nc.vector.tensor_copy(cT[0:C1, p, 1], m[0:C1, 1]).then_inc(prod_used, 1)
                    m = product()
                    nc.vector.tensor_scalar(qT[:, p], m[:], 0.25, None, ALU.mult).then_inc(prod_used, 1)
                    m = product()
                    nc.vector.tensor_scalar(kE[:, p], m[:], cst[:, C_EVEN:C_EVEN + 1], None, ALU.mult)
                    nc.vector.tensor_scalar(kO[:, p], m[:], cst[:, C_ODD:C_ODD + 1], None, ALU.mult).then_inc(prod_used, 1)
                    m = product()
                    for v, o in ((vE, 0), (vO, 16)):
                        i = nc.vector.tensor_copy(
                            v[:, p].rearrange("t b (h f) -> t (b h) f", f=32)[:, :, o:o + 16],
                            m[:].rearrange("t b (h f) -> t (b h) f", f=32)[:, :, o:o + 16])
                    i.then_inc(prod_used, 1)
                    dve.wait_ge(mask_in[p], g * 16 + 16)
                    chain(nc.vector.tensor_scalar(mk[:, p], mku[:, p], 1.0, NEG, ALU.subtract, ALU.mult))
                    dve.sem_inc(mask_used, 1)
                    for b in range(PAIR):
                        for r in range(ROWS):
                            dve.wait_ge(sco, t_sco.up())
                            i = nc.vector.tensor_tensor(pr[:, p, b, r], S[r][:],
                                                        mk[:, p, b].unsqueeze(1).broadcast_to([P, 4, T]), ALU.add)
                            i.then_inc(sco_used, 1)
                            dve.wait_ge(sco_used, ROWS + t_sco.now())
                            nc.vector.tensor_reduce(nmax[:, p, b, r], pr[:, p, b, r], AX.X, ALU.max,
                                                    negate=True).then_inc(max_made, 1)
                    for b in range(PAIR):
                        for r in range(ROWS):
                            dve.wait_ge(exp_made, t_exp.up())
                            nc.vector.reciprocal(rinv[:, p, b, r], rsum[:, p, b, r]).then_inc(inv_made, 1)
                for p in range(STREAMS):
                    m = product()
                    nc.vector.tensor_copy(oT[:, p], m[:]).then_inc(prod_used, 1)
                    m = product()
                    dve.wait_ge(x1_out[p], g * 16 + 16)
                    i = nc.vector.tensor_tensor(x1[:, p], m[:], xt[:, p], ALU.add)
                    i.then_inc(prod_used, 1)
                    dve.wait_ge(prod_used, 2 + t_prod.now())
                    dve.sem_inc(x1_made, 1)
                    dve.sem_inc(x_used, 1)
                    dve.wait_ge(xn1_out[p], g * 16 + 16)
                    layer_norm(x1[:, p], xn1[:, p], p, xn1_made)
                    m = product()
                    nc.vector.tensor_copy(xT[:, p], m[:]).then_inc(prod_used, 1)
                    m = product()
                    nc.vector.tensor_copy(keep["logits"][:, bass.ds(g * 4 + p * 2, 2)],
                                          m[:, :, 0:E]).then_inc(prod_used, 1)
                assert t_step.n == STEPS_A, t_step.n
                assert t_prod.n == PRODS

        @block.tensor
        def _(pe):
            ident = cst[:, C_ID:C_ID + P]
            pe.wait_ge(w_in, 16 * 7)
            with pe.Fori(0, TURNS) as g:
                t_free, t_made = Tally(g, PRODS), Tally(g, PRODS)
                t_sfree, t_norm, t_pt = Tally(g, SLOTS), Tally(g, SLOTS), Tally(g, SLOTS)
                t_tfree = Tally(g, SLOTS)

                def bank():
                    pe.wait_ge(prod_used, t_free.up())
                    return M[(t_free.n - 1) % 2]

                def turn_rows(dst, src):
                    for b in range(PAIR):
                        for u in range(2):
                            w = min(P, src.shape[2] - u * P)
                            i = nc.tensor.transpose(dst[0:w, u, b * T:(b + 1) * T], src[:, b, u * P:u * P + w], ident)
                    i.then_inc(prod, 1)
                    t_made.up()

                def project(w, src, K1=P):
                    m = bank()
                    for u in range(2):
                        nc.tensor.matmul(m[:, u], w[:, 0, u * P:(u + 1) * P], src[:, 0], start=True, stop=False)
                        i = nc.tensor.matmul(m[:, u], w[0:K1, 1, u * P:(u + 1) * P], src[0:K1, 1], start=False, stop=True)
                    i.then_inc(prod, 1)
                    t_made.up()

                def project_rows(w, src, K1=P):
                    m = bank()
                    for b in range(PAIR):
                        n = w.shape[2]
                        nc.tensor.matmul(m[:, b, 0:n], src[:, 0, b * T:(b + 1) * T], w[:, 0], start=True, stop=False)
                        i = nc.tensor.matmul(m[:, b, 0:n], src[0:K1, 1, b * T:(b + 1) * T], w[0:K1, 1], start=False, stop=True)
                    i.then_inc(prod, 1)
                    t_made.up()

                for p in range(STREAMS):
                    pe.wait_ge(xn_made, g * STREAMS + p + 1)
                    turn_rows(bank(), xn[:, p])
                    pe.wait_ge(c_in[p], g * 16 + 16)
                    turn_rows(bank(), ct[:, p])
                    n_x, n_c = 2 + t_made.now() - 1, 2 + t_made.now()
                    pe.wait_ge(prod_used, n_x)
                    project(wq, xT[:, p])
                    pe.wait_ge(prod_used, n_c)
                    pe.sem_inc(c_used, 1)
                    project(wk, cT[:, p], C1)
                    project_rows(wv, cT[:, p], C1)
                    pe.wait_ge(prod_used, 2 + t_made.now() - 1)
                    for b in range(PAIR):
                        for j in range(4):
                            u, k = j // 2, (kE, kO)[j % 2]
                            for r in range(ROWS):
                                if j == 0:
                                    pe.wait_ge(sco_used, t_sfree.up())
                                s = slice(32 * r, 32 * r + 32)
                                i = nc.tensor.matmul(S[r][:, j], qT[s, p, u, b * T:(b + 1) * T],
                                                     k[s, p, u, b * T:(b + 1) * T], start=True, stop=True)
                                if j == 3:
                                    i.then_inc(sco, 1)
                for p in range(STREAMS):
                    for b in range(PAIR):
                        for r in range(ROWS):
                            pe.wait_ge(norm_made, t_norm.up())
                            pe.wait_ge(pT_made, t_tfree.up())
                            for j in range(4):
                                i = nc.tensor.transpose(TB[r % 2][:, j], pr[:, p, b, r, j], ident)
                            i.then_inc(turned, 1)
                    m = bank()
                    for b in range(PAIR):
                        pe.wait_ge(pT_made, 2 + t_pt.up(ROWS))
                        for j in range(4):
                            u, v = j // 2, (vE, vO)[j % 2]
                            for r in range(ROWS):
                                h = 32 * (4 * u + r)
                                i = nc.tensor.matmul(m[32 * r:32 * r + 32, u, b * T:(b + 1) * T],
                                                     v[:, p, b, h:h + 32], pT[:, b, r, j],
                                                     start=j % 2 == 0, stop=j % 2 == 1)
                    i.then_inc(prod, 1)
                    t_made.up()
                    pe.wait_ge(prod_used, 2 + t_made.now())
                    project_rows(wo, oT[:, p])
                    pe.wait_ge(xn1_made, g * STREAMS + p + 1)
                    turn_rows(bank(), xn1[:, p])
                    pe.wait_ge(prod_used, 2 + t_made.now())
                    project_rows(wsw, xT[:, p])

CAP_FACTOR = 0.5
OUT_OF_BOUNDS = 65536.0


def phase_route(nc, io, scratch, keep, cst):
    NT, T, D = io["x"].shape
    E = io["L0_ffn_b_switch"].shape[0]
    CAP = int(CAP_FACTOR * NT * T / E)
    LOADS = 4
    HALVES = 2
    TURNS = NT // (LOADS * HALVES)
    buf = scratch["buf"]

    with ExitStack() as es:
        def sb(name, shape, dt=F32):
            return es.enter_context(nc.sbuf_tensor("r_" + name, [P] + shape, dt))

        def sem(name):
            return es.enter_context(nc.semaphore("r_" + name))

        bsw = sb("b_switch", [E])
        lg, e, pb = keep["logits"], sb("exp", [NT, E]), sb("probs", [NT, E])
        oh = sb("one_hot", [NT, E])
        i8 = sb("iota_less_E", [E])
        tot = sb("tile_totals", [NT, E])
        run = [sb(f"running{n}", [NT, E]) for n in range(2)]
        mx, sm, pm, route, pos, kept, slot = (sb(n, [NT]) for n in ("mx", "sm", "pm", "route", "pos", "kept", "slotf"))
        zero = sb("zero", [2048])
        rows = sb("rows", [HALVES, LOADS, D])
        idx = sb("idx", [HALVES, LOADS], U32)
        after_wait = sb("after_wait", [1])
        cum = es.enter_context(nc.psum_tensor("r_cum", [P, NT, E], F32))
        all_ = es.enter_context(nc.psum_tensor("r_all", [P, NT, E], F32))

        b_in, zero_made, zeroed, pad_made = sem("b_in"), sem("zero_made"), sem("buf_zeroed"), sem("pad_made")
        step = sem("vector_step")
        shifted, exped, hot, counted = sem("shifted"), sem("exped"), sem("one_hot"), sem("counted")
        slots_made = sem("slots_made")
        rows_in = [sem(f"rows_in{h}") for h in range(HALVES)]
        sent = [sem(f"sent{h}") for h in range(HALVES)]
        idx_made, rows_free = sem("idx_made"), sem("rows_free")
        block = es.enter_context(nc.Block())

        @block.vector
        def _(dve):
            t = Tally()

            def chain(i):
                i.then_inc(step, 1)
                dve.wait_ge(step, t.up())

            def over_e(a):
                return a.unsqueeze(2).broadcast_to([P, NT, E])

            def over_t(a):
                return a.unsqueeze(1).broadcast_to([P, NT, E])

            V = nc.vector
            V.memset(zero[:], 0.0).then_inc(zero_made, 1)
            V.memset(keep["gate"][:, NT:], 0.0)
            V.memset(keep["slots"][:, NT:], 0)
            chain(V.tensor_scalar(i8[:], cst[:, C_IOTA:C_IOTA + E], float(E), None, ALU.subtract))
            dve.wait_ge(b_in, 16)
            chain(V.tensor_tensor(e[:], lg[:], over_t(bsw[:]), ALU.add))
            chain(V.tensor_reduce(mx[:], e[:], AX.X, ALU.max))
            V.tensor_tensor(pb[:], e[:], over_e(mx[:]), ALU.subtract).then_inc(shifted, 1)
            dve.wait_ge(exped, 1)
            chain(V.tensor_reduce(sm[:], e[:], AX.X, ALU.add))
            chain(V.reciprocal(mx[:], sm[:]))
            chain(V.tensor_tensor(pb[:], e[:], over_e(mx[:]), ALU.mult))
            chain(V.tensor_reduce(pm[:], pb[:], AX.X, ALU.max))
            chain(V.reciprocal(mx[:], pm[:]))
            V.tensor_tensor(keep["gate"][:, 0:NT], pm[:], mx[:], ALU.mult)
            chain(V.tensor_tensor(oh[:], pb[:], over_e(pm[:]), ALU.is_equal))
            chain(V.tensor_tensor(e[:], oh[:], over_t(i8[:]), ALU.mult))
            chain(V.tensor_reduce(route[:], e[:], AX.X, ALU.min))
            V.tensor_tensor(oh[:], over_t(i8[:]), over_e(route[:]), ALU.is_equal).then_inc(hot, 1)
            dve.wait_ge(counted, 1)
            chain(V.tensor_copy(tot[:], all_[:]))
            src, n, s = tot, 0, 1
            while s < NT:
                dst = run[n % 2]
                V.tensor_copy(dst[:, 0:s], src[:, 0:s])
                chain(V.tensor_tensor(dst[:, s:NT], src[:, s:NT], src[:, 0:NT - s], ALU.add))
                src, n, s = dst, n + 1, s * 2
            chain(V.tensor_tensor(e[:], src[:], tot[:], ALU.subtract))
            chain(V.tensor_tensor(pb[:], e[:], cum[:], ALU.add))
            chain(V.tensor_tensor(e[:], pb[:], oh[:], ALU.mult))
            chain(V.tensor_reduce(pos[:], e[:], AX.X, ALU.add))
            chain(V.tensor_scalar(kept[:], pos[:], float(CAP), OUT_OF_BOUNDS, ALU.is_gt, ALU.mult))
            chain(V.tensor_scalar(route[:], route[:], float(CAP), float(E * CAP - 1), ALU.mult, ALU.add))
            chain(V.tensor_tensor(slot[:], route[:], pos[:], ALU.add))
            V.tensor_tensor(keep["slots"][:, 0:NT], slot[:], kept[:], ALU.add).then_inc(slots_made, 1)

        @block.scalar
        def _(act):
            act.wait_ge(shifted, 1)
            nc.scalar.activation(e[:], pb[:], ACT.Exp).then_inc(exped, 1)

        @block.tensor
        def _(pe):
            pe.wait_ge(hot, 1)
            nc.tensor.matmul(cum[:], cst[:, C_TRI:C_TRI + P], oh[:], start=True, stop=True)
            nc.tensor.matmul(all_[:], cst[:, C_ONE:C_ONE + P], oh[:], start=True, stop=True).then_inc(counted, 1)

        @block.sync
        def _(sp):
            sp.dma_start(bsw[:], io["L0_ffn_b_switch"].partition_broadcast(P)).then_inc(b_in, 16)
            sp.wait_ge(zero_made, 1)
            parts = buf.rearrange("(n p r) d -> n p (r d)", p=P, r=2048 // D)
            for n in range(parts.shape[0]):
                sp.dma_start(parts[n], zero[:]).then_inc(zeroed, 16)
            src = scratch["xn1"][0:NT].rearrange("(g h n) t d -> g h t n d", h=HALVES, n=LOADS)
            pad = scratch["xn1"].shape[0] - NT
            if pad:
                spare = scratch["xn1"][NT:NT + pad].rearrange("n t d -> (n t d)").rearrange("(p r) -> p r", p=P)
                sp.dma_start(spare, zero[:, 0:pad * T * D // P]).then_inc(pad_made, 16)
                sp.wait_ge(pad_made, 16)
            with sp.Fori(0, TURNS) as g:
                for h in range(HALVES):
                    sp.wait_ge(rows_free, g * HALVES + h + 1)
                    sp.dma_start(rows[:, h], src[bass.ds(g, 1), h].rearrange("g t n d -> (g t) n d")).then_inc(rows_in[h], 16)

        @block.gpsimd
        def _(pool):
            last_slot = pool.to_reg(E * CAP - 1)
            pool.sem_inc(rows_free, HALVES)
            pool.wait_ge(slots_made, 1)
            pool.wait_ge(zeroed, 16 * (E * CAP * D // (2048 * P)))
            with pool.Fori(0, TURNS) as g:
                for h in range(HALVES):
                    nc.gpsimd.tensor_copy(idx[:, h], keep["slots"][:, bass.ds((g * HALVES + h) * LOADS, LOADS)]).then_inc(idx_made, 1)
                    pool.wait_ge(idx_made, g * HALVES + h + 1)
                    pool.wait_ge(rows_in[h], g * 16 + 16)
                    nc.gpsimd.tensor_tensor(after_wait[:], cst[:, 0:1], cst[:, 0:1], ALU.add)
                    for n in range(LOADS):
                        nc.gpsimd.indirect_dma_start(
                            out=buf, out_offset=bass.IndirectOffsetOnAxis(ap=idx[:, h, n:n + 1], axis=0),
                            in_=rows[:, h, n], in_offset=None, bounds_check=last_slot, oob_is_err=False,
                        ).then_inc(sent[h], 16)
                for h in range(HALVES):
                    pool.wait_ge(sent[h], (g + 1) * 16 * LOADS)
                    pool.sem_inc(rows_free, 1)


def phase_experts(nc, io, scratch, cst):
    w1, w2, b2 = io["L0_ffn_w1"], io["L0_ffn_w2"], io["L0_ffn_b2"]
    E, D, H = w1.shape
    CAP = scratch["buf"].shape[0] // E
    NR = CAP // P
    HC = H // P
    SIDES = 2
    TURNS = E // SIDES
    YB = NR // 2

    with ExitStack() as es:
        def sb(name, shape, dt=F32):
            return es.enter_context(nc.sbuf_tensor("e_" + name, [P] + shape, dt))

        def sem(name):
            return es.enter_context(nc.semaphore("e_" + name))

        w1t = sb("w1", [SIDES, 2, H])
        w2t = sb("w2", [SIDES, HC, D])
        b1t = sb("b1", [SIDES, HC])
        b2t = sb("b2", [SIDES, D])
        xr = sb("rows", [SIDES, NR, D])
        xT = sb("rowsT", [2, CAP])
        hT = sb("hidden", [HC, CAP])
        y = sb("y", [YB, 2, D])
        TB = [es.enter_context(nc.psum_tensor(f"e_turned{r}", [P, CAP], F32)) for r in range(2)]
        HB = [es.enter_context(nc.psum_tensor(f"e_hidden{r}", [P, CAP], F32)) for r in range(4)]
        Y = [es.enter_context(nc.psum_tensor(f"e_out{r}", [P, 2, D], F32)) for r in range(2)]
        got = [sem(f"loaded{s}") for s in range(SIDES)]
        turned, xT_made, done = sem("turned"), sem("xT_made"), sem("expert_done")
        hid, hid_made = sem("hidden"), sem("hidden_made")
        out, y_made = sem("out"), sem("y_made")
        y_out = [sem(f"y_out{i}") for i in range(2)]
        block = es.enter_context(nc.Block())

        def of(ap, g, s):
            v = ap.rearrange("(g s) a n -> g s a n", s=SIDES)[bass.ds(g, 1), s]
            return v.rearrange("g (c p) n -> p (g c) n", p=P)

        @block.sync
        def _(sp):
            buf = scratch["buf"].rearrange("(e r) d -> e r d", e=E)
            with sp.Fori(0, TURNS) as g:
                for s in range(SIDES):
                    sp.wait_ge(done, g * SIDES + s + 1)
                    sp.dma_start(xr[:, s], of(buf, g, s)).then_inc(got[s], 16)
                    sp.dma_start(w1t[:, s], of(w1, g, s)).then_inc(got[s], 16)
                    sp.dma_start(w2t[:, s], of(w2, g, s)).then_inc(got[s], 16)
                    b1 = io["b1_cols"].rearrange("(g s) p c -> g s p c", s=SIDES)[bass.ds(g, 1), s]
                    sp.dma_start(b1t[:, s], b1.rearrange("g p c -> (g p) c")).then_inc(got[s], 16)
                    b = b2.rearrange("(g s) n -> g s n", s=SIDES)[bass.ds(g, 1), s]
                    sp.dma_start(b2t[:, s], b.rearrange("g n -> (g n)").partition_broadcast(P)).then_inc(got[s], 16)

        @block.tensor
        def _(pe):
            with pe.Fori(0, TURNS) as g:
                t_x, t_h, t_y = Tally(g, 2 * SIDES), Tally(g, HC * SIDES), Tally(g, YB * SIDES)
                for s in range(SIDES):
                    pe.wait_ge(got[s], g * 80 + 80)
                    for u in range(2):
                        pe.wait_ge(xT_made, t_x.up())
                        for n in range(NR):
                            i = nc.tensor.transpose(TB[u][:, n * P:(n + 1) * P], xr[:, s, n, u * P:(u + 1) * P],
                                                    cst[:, C_ID:C_ID + P])
                        i.then_inc(turned, 1)
                    pe.wait_ge(xT_made, 2 + t_x.now())
                    for c in range(HC):
                        pe.wait_ge(hid_made, t_h.up())
                        b = HB[c % 4]
                        for u in range(2):
                            i = nc.tensor.matmul(b[:], w1t[:, s, u, c * P:(c + 1) * P], xT[:, u], start=u == 0, stop=u == 1)
                        i.then_inc(hid, 1)
                    for q in range(YB):
                        pe.wait_ge(y_made, t_y.up())
                        for n in range(2):
                            r = (2 * q + n) * P
                            for c in range(HC):
                                if q == 0 and n == 0:
                                    pe.wait_ge(hid_made, 4 + t_h.now() - HC + c + 1)
                                i = nc.tensor.matmul(Y[q % 2][:, n], hT[:, c, r:r + P], w2t[:, s, c],
                                                     start=c == 0, stop=c == HC - 1)
                        i.then_inc(out, 1)

        @block.scalar
        def _(act):
            with act.Fori(0, TURNS) as g:
                t_h, t_y = Tally(g, HC * SIDES), Tally(g, YB * SIDES, YB)
                for s in range(SIDES):
                    act.wait_ge(got[s], g * 80 + 80)
                    for c in range(HC):
                        act.wait_ge(hid, t_h.up())
                        nc.scalar.activation(hT[:, c], HB[c % 4][:], ACT.Relu,
                                             bias=b1t[:, s, c:c + 1]).then_inc(hid_made, 1)
                    dst = scratch["y"].rearrange("(g s q n p) d -> g s q p n d", s=SIDES, q=YB, n=2, p=P)
                    for q in range(YB):
                        act.wait_ge(y_made, t_y.up())
                        act.dma_start(dst[bass.ds(g, 1), s, q].rearrange("g p n d -> (g p) n d"), y[:, q]).then_inc(y_out[q], 16)
            for q in range(YB):
                act.wait_ge(y_out[q], 16 * E + 16)

        @block.vector
        def _(dve):
            for m, k in ((xT_made, 2), (hid_made, 4), (y_made, YB), (done, SIDES), *((m, 16) for m in y_out)):
                dve.sem_inc(m, k)
            with dve.Fori(0, TURNS) as g:
                t_x, t_y = Tally(g, 2 * SIDES), Tally(g, YB * SIDES)
                for s in range(SIDES):
                    for u in range(2):
                        dve.wait_ge(turned, t_x.up())
                        nc.vector.tensor_copy(xT[:, u], TB[u][:]).then_inc(xT_made, 1)
                    dve.wait_ge(got[s], g * 80 + 80)
                    for q in range(YB):
                        dve.wait_ge(out, t_y.up())
                        dve.wait_ge(y_out[q], (g * SIDES + s + 1) * 16)
                        nc.vector.tensor_tensor(y[:, q], Y[q][:], b2t[:, s].unsqueeze(1).broadcast_to([P, 2, D]),
                                                ALU.add).then_inc(y_made, 1)
                    dve.wait_ge(y_made, YB + t_y.now())
                    dve.sem_inc(done, 1)



NODES, MAX_PREV, CELL_HEADS = 6, 5, 8
KINDS = 5
TO_Q, TO_K, TO_V, EDGE, OUT = range(KINDS)


def cell_plan():
    plan, at = [], 0
    for c in range(NODES):
        n = min(c + 1, MAX_PREV)
        plan.append(dict(edge=(at + n - 1, at, at + n // 2), src=(c - 1, c - n, c - n + n // 2)))
        at += n
    return plan


def phase_fuse(nc, io, fw, fb, row5, cst):
    plan = cell_plan()
    D = io["L1_ffn_Wq"].shape[1]
    SCALE = 1.0 / np.sqrt(D // CELL_HEADS)
    NE = io["L1_ffn_We"].shape[0]
    RING = 3
    jobs = [(c, k) for c in range(NODES) for k in (TO_Q, TO_K, TO_V)]
    W = [io["L1_ffn_" + n] for n in ("Wq", "Wk", "Wv")]

    with ExitStack() as es:
        def sb(name, shape, dt=F32):
            return es.enter_context(nc.sbuf_tensor("f_" + name, [P] + shape, dt))

        def sem(name):
            return es.enter_context(nc.semaphore("f_" + name))

        weT = sb("edgeT", [RING, 2, D])
        w = sb("w", [RING, 2, D])
        ew = sb("ew", [NODES, 3])
        aw = sb("act_w", [NODES])
        be = sb("be", [2, NE])
        M = [es.enter_context(nc.psum_tensor(f"f_product{r}", [P, 2, D], F32)) for r in range(2)]
        MB = es.enter_context(nc.psum_tensor("f_biases", [P, NODES, 3, 2], F32))
        small_in, plain_in = sem("small_in"), sem("plain_in")
        job_in = [sem(f"job_in{r}") for r in range(RING)]
        made, used, bias_made = sem("made"), sem("used"), sem("bias_made")
        block = es.enter_context(nc.Block())

        def halves(a):
            return a.rearrange("(c p) n -> p c n", p=P)

        @block.sync
        def _(sp):
            sp.dma_start(ew[:], io["L1_ffn_ew"].rearrange("c k -> (c k)").partition_broadcast(P)
                         .rearrange("p (c k) -> p c k", k=3)).then_inc(small_in, 16)
            sp.dma_start(aw[:], io["L1_ffn_act_w"].partition_broadcast(P)).then_inc(small_in, 16)
            sp.dma_start(be[:], io["be_cols"]).then_inc(small_in, 16)
            last = plan[-1]["edge"][0]
            sp.dma_start(row5[:], io["L1_ffn_be"][last].partition_broadcast(P)).then_inc(small_in, 16)
            for n, (c, k) in enumerate(jobs):
                if n >= RING:
                    sp.wait_ge(made, n - RING + 1)
                sp.dma_start(weT[:, n % RING], halves(io["edgesT"][plan[c]["edge"][k]])).then_inc(job_in[n % RING], 16)
                sp.dma_start(w[:, n % RING], halves(W[k][c])).then_inc(job_in[n % RING], 16)

        @block.scalar
        def _(act):
            for c in range(NODES):
                act.dma_start(fw[:, c, EDGE], halves(io["L1_ffn_We"][plan[c]["edge"][0]])).then_inc(plain_in, 16)
                act.dma_start(fw[:, c, OUT], halves(io["L1_ffn_Wo"][c])).then_inc(plain_in, 16)

        @block.tensor
        def _(pe):
            pe.wait_ge(small_in, 64)
            for n, (c, k) in enumerate(jobs):
                pe.wait_ge(job_in[n % RING], 32 * (n // RING + 1))
                if n >= 2:
                    pe.wait_ge(used, n - 1)
                e = plan[c]["edge"][k]
                for o in range(2):
                    for h in range(2):
                        nc.tensor.matmul(MB[:, c, k, o:o + 1], w[:, n % RING, h, o * P:(o + 1) * P],
                                         be[:, h, e:e + 1], start=h == 0, stop=h == 1)
                for u in range(2):
                    for h in range(2):
                        i = nc.tensor.matmul(M[n % 2][:, u], weT[:, n % RING, h, u * P:(u + 1) * P],
                                             w[:, n % RING, h], start=h == 0, stop=h == 1)
                i.then_inc(made, 1)

        @block.vector
        def _(dve):
            dve.wait_ge(small_in, 64)
            for n, (c, k) in enumerate(jobs):
                dve.wait_ge(made, n + 1)
                nc.vector.tensor_scalar(fw[:, c, k], M[n % 2][:], ew[:, c, k:k + 1], SCALE if k == TO_Q else 1.0,
                                        ALU.mult, ALU.mult).then_inc(used, 1)
            for c, k in jobs:
                nc.vector.tensor_scalar(fb[:, c, k], MB[:, c, k], ew[:, c, k:k + 1], SCALE if k == TO_Q else 1.0,
                                        ALU.mult, ALU.mult)
            dve.wait_ge(plain_in, 32 * NODES)
            for c in range(NODES):
                q = ew[:, c, TO_Q:TO_Q + 1]
                nc.vector.tensor_scalar(fw[:, c, EDGE], fw[:, c, EDGE], q, None, ALU.mult)
                nc.vector.tensor_scalar(fb[:, c, EDGE], be[:, :, plan[c]["edge"][0]], q, None, ALU.mult)
                nc.vector.tensor_scalar(fw[:, c, OUT], fw[:, c, OUT], aw[:, c:c + 1], None, ALU.mult)
            nc.vector.tensor_scalar(row5[:], row5[:], ew[:, NODES - 1, TO_Q:TO_Q + 1], None, ALU.mult)



def phase_second_layer(nc, io, scratch, keep, fw, fb, row5, cst, out):
    ctx = io["ctx_768"]
    B, T, D = io["x"].shape
    C = ctx.shape[2]
    C1 = C - P
    TURNS = B // (PAIR * STREAMS)
    W2 = PAIR * T
    HID = io["L1_xattn_W1"].shape[1] // P
    plan = cell_plan()
    RT = PAIR * STREAMS
    SLOT_OF = {-1: 0, 0: 1, 1: 2, 2: 3, 3: 0, 4: 1}
    STAGES = NODES + 2
    FILL = [[(TO_V, c)] * (c < 2) + [(TO_K, c + 1)] * (c < NODES - 1) + [(TO_V, c + 1)] * (0 < c < NODES - 1)
            for c in range(NODES)]

    def rows(ap, g, p):
        v = ap.rearrange("(g p b) t d -> g p t b d", p=STREAMS, b=PAIR)
        return v[bass.ds(g, 1), p].rearrange("g t b d -> (g t) b d")

    with ExitStack() as es:
        def sb(name, shape, dt=F32):
            return es.enter_context(nc.sbuf_tensor("c_" + name, [P] + shape, dt))

        def sem(name):
            return es.enter_context(nc.semaphore("c_" + name))

        wq, wk, wv = (sb(n, [2, D]) for n in ("wq", "wk", "wv"))
        w1, w2 = sb("w1", [2, HID * P]), sb("w2", [HID, D])
        bq, bk, bv, b1 = sb("bq", [2]), sb("bk", [2]), sb("bv", [2]), sb("b1", [HID])
        b2, ln_g, ln_b = sb("b2", [D]), sb("ln_g", [D]), sb("ln_b", [D])
        x1 = sb("x1", [STREAMS, PAIR, D])
        xg = sb("routed", [STREAMS, PAIR, D])
        ct = sb("ctx", [STREAMS, PAIR, C])
        idx = sb("idx", [STREAMS, PAIR], U32)
        gate = sb("gate", [STREAMS, PAIR])
        x2 = sb("x2", [STREAMS, PAIR, D])
        xn = sb("xn", [STREAMS, PAIR, D])
        fin = sb("fin", [STREAMS, PAIR, D])
        stats = sb("stats", [PAIR, 6])
        after_wait = sb("after_wait", [1])
        after_wait_pool = sb("after_wait_pool", [1])
        mv = sb("mean_var", [STREAMS, PAIR, 2])
        veps = sb("var_eps", [STREAMS, PAIR])
        rstd = sb("rstd", [STREAMS, PAIR])
        nd = sb("nodes", [STREAMS, 4, 2, W2])
        hid = sb("hidden", [STREAMS, HID, W2])
        qT = sb("qT", [STREAMS, 2, W2])
        kT = sb("kT", [STREAMS, 2, W2])
        oT = sb("oT", [STREAMS, 2, W2])
        vE = sb("v_even", [STREAMS, PAIR, D])
        vO = sb("v_odd", [STREAMS, PAIR, D])
        va = sb("v", [STREAMS, 2, PAIR, D])
        pr = sb("probs", [STREAMS, PAIR, ROWS, 4, T])
        nmax = sb("neg_max", [STREAMS, PAIR, ROWS, 4])
        rsum = sb("row_sum", [STREAMS, PAIR, ROWS, 4])
        rinv = sb("row_inv", [STREAMS, PAIR, ROWS, 4])
        pT = sb("probsT", [PAIR, ROWS, 4, T])
        kO = oT
        cT = hid

        S = [es.enter_context(nc.psum_tensor(f"c_scores{r}", [P, 4, T], F32)) for r in range(ROWS)]
        TB = [es.enter_context(nc.psum_tensor(f"c_turned{r}", [P, 4, T], F32)) for r in range(2)]
        M = [es.enter_context(nc.psum_tensor(f"c_product{r}", [P, 2, W2], F32)) for r in range(2)]

        w_in = sem("weights_in")
        x_in = [sem(f"x_in{p}") for p in range(STREAMS)]
        c_in = [sem(f"ctx_in{p}") for p in range(STREAMS)]
        r_in = [sem(f"routed_in{p}") for p in range(STREAMS)]
        gathered = [sem(f"gathered{p}") for p in range(STREAMS)]
        idx_made, x2_made, c_used = sem("idx_made"), sem("x2_made"), sem("ctx_used")
        zeroed, x3b_made, x3n_made = sem("v_zeroed"), sem("x3_ln_b_made"), sem("x3_normed")
        vstep, pstep = sem("vector_step"), sem("pool_step")
        var_made, veps_made, rstd_made, xn_made = sem("var_made"), sem("veps_made"), sem("rstd_made"), sem("xn_made")
        normed = sem("cell_normed")
        stored = [sem(f"stored{p}") for p in range(STREAMS)]
        prod, prod_used = sem("product_made"), sem("product_used")
        sco, sco_used = sem("scores_made"), sem("scores_used")
        max_made, inv_made, norm_made = sem("max_made"), sem("inv_made"), sem("norm_made")
        turned, pT_made = sem("turned_made"), sem("pT_made")

        def banks(s):
            return [(b, r) for b in range(PAIR if s == 0 else 1 if s < STAGES - 1 else 0) for r in range(ROWS)]

        SLOTS = STREAMS * sum(len(banks(s)) for s in range(STAGES))
        PRODS = STREAMS * (5 + 7 + len(FILL[0]) + sum(3 + len(FILL[c]) for c in range(1, NODES)) + 2)
        LNS = 3 * STREAMS
        VSTEPS = STREAMS * (1 + 1 + 3)
        block = es.enter_context(nc.Block())
        order = [(s, p) for s in range(STAGES) for p in range(STREAMS)]

        @block.sync
        def _(sp):
            def halves(a):
                return a.rearrange("(c p) n -> p c n", p=P)

            for t, a in ((wq[:], halves(io["L1_xattn_Wq"])), (w1[:], halves(io["L1_xattn_W1"])),
                         (w2[:], halves(io["L1_xattn_W2"])), (wk[:, 0], io["L1_xattn_Wk"][0:P]),
                         (wk[0:C1, 1], io["L1_xattn_Wk"][P:C]), (wv[:, 0], io["L1_xattn_Wv"][0:P]),
                         (wv[0:C1, 1], io["L1_xattn_Wv"][P:C]), (bq[:], io["L1_xattn_bq_cols"]),
                         (bk[:], io["L1_xattn_bk_cols"]), (bv[:], io["L1_xattn_bv_cols"]),
                         (b1[:], io["L1_xattn_b1_cols"]), (b2[:], io["L1_xattn_b2"].partition_broadcast(P)),
                         (ln_g[:], io["L1_ffn_ln_g"].partition_broadcast(P)),
                         (ln_b[:], io["L1_ffn_ln_b"].partition_broadcast(P))):
                sp.dma_start(t, a).then_inc(w_in, 16)
            for p in range(STREAMS):
                sp.dma_start(xg[:, p], rows(scratch["xn1"], 0, p)).then_inc(r_in[p], 16)
            with sp.Fori(0, TURNS) as g:
                for p in range(STREAMS):
                    sp.wait_ge(x2_made, g * STREAMS + p + 1)
                    sp.dma_start(x1[:, p], rows(scratch["x1"], g, p)).then_inc(x_in[p], 16)
                    sp.wait_ge(c_used, g * STREAMS + p + 1)
                    sp.dma_start(ct[:, p], rows(ctx, g, p)).then_inc(c_in[p], 16)
                for p in range(STREAMS):
                    sp.wait_ge(x2_made, STREAMS + g * STREAMS + p + 1)
                    sp.dma_start(xg[:, p], rows(scratch["xn1"][RT:], g, p)).then_inc(r_in[p], 16)

        @block.gpsimd
        def _(pool):
            def gather(g, p):
                at = bass.ds(g * RT + p * PAIR, PAIR)
                nc.gpsimd.tensor_copy(idx[:, p], keep["slots"][:, at]).then_inc(idx_made, 1)
                pool.wait_ge(idx_made, g * 2 * STREAMS + 2 * p + 1)
                nc.gpsimd.tensor_copy(gate[:, p], keep["gate"][:, at]).then_inc(idx_made, 1)
                pool.wait_ge(idx_made, g * 2 * STREAMS + 2 * p + 2)
                pool.wait_ge(r_in[p], g * 16 + 16)
                nc.gpsimd.tensor_tensor(after_wait_pool[:], cst[:, 0:1], cst[:, 0:1], ALU.add)
                for b in range(PAIR):
                    nc.gpsimd.indirect_dma_start(
                        out=xg[:, p, b], out_offset=None, in_=scratch["y"],
                        in_offset=bass.IndirectOffsetOnAxis(ap=idx[:, p, b:b + 1], axis=0),
                        bounds_check=last_slot, oob_is_err=False).then_inc(gathered[p], 16)

            last_slot = pool.to_reg(scratch["y"].shape[0] - 1)
            nc.gpsimd.memset(vE[:], 0.0).then_inc(zeroed, 1)
            nc.gpsimd.memset(vO[:], 0.0).then_inc(zeroed, 1)
            for p in range(STREAMS):
                gather(0, p)
            pool.wait_ge(w_in, 16 * 14)
            with pool.Fori(0, TURNS) as g:
                t_var, t_inv = Tally(g, LNS), Tally(g, SLOTS)

                def rsqrt(p, eps):
                    n = t_var.up()
                    pool.wait_ge(var_made, n)
                    nc.gpsimd.tensor_tensor(veps[:, p], mv[:, p, :, 1], cst[:, eps:eps + 2], ALU.add).then_inc(veps_made, 1)
                    pool.wait_ge(veps_made, n)
                    nc.gpsimd.tensor_tensor(rstd[:, p], veps[:, p], cst[:, C_HALF:C_HALF + 2], ALU.pow).then_inc(rstd_made, 1)

                def wide(a):
                    return a.unsqueeze(1).broadcast_to([P, PAIR, D])

                for s, p in order:
                    if s in (0, 1):
                        rsqrt(p, C_EPS5)
                    if s == 3:
                        pool.wait_ge(x3n_made, g * STREAMS + p + 1)
                        nc.gpsimd.tensor_tensor(x2[:, p], x2[:, p], wide(ln_b[:]), ALU.add).then_inc(x3b_made, 1)
                    if s == 5:
                        gather(g + 1, p)
                    if s == STAGES - 1:
                        rsqrt(p, C_EPS6)
                        pool.wait_ge(normed, g * STREAMS + p + 1)
                        pool.wait_ge(stored[p], g * 16 + 16)
                        nc.gpsimd.tensor_tensor(fin[:, p], xn[:, p], wide(ln_g[:]), ALU.mult).then_inc(pstep, 1)
                        pool.wait_ge(pstep, 2 * STREAMS + g * 2 * STREAMS + 2 * p + 1)
                        pool.wait_ge(x3b_made, g * STREAMS + p + 1)
                        nc.gpsimd.tensor_tensor(fin[:, p], fin[:, p], x2[:, p], ALU.add).then_inc(pstep, 1)
                        pool.wait_ge(pstep, 2 * STREAMS + g * 2 * STREAMS + 2 * p + 2)
                    for b, r in banks(s):
                        pool.wait_ge(inv_made, t_inv.up())
                        e = pr[:, p, b, r]
                        nc.gpsimd.tensor_tensor(e, e, rinv[:, p, b, r].unsqueeze(2).broadcast_to([P, 4, T]),
                                                ALU.mult).then_inc(norm_made, 1)
            for p in range(STREAMS):
                pool.wait_ge(gathered[p], 16 * PAIR * (TURNS + 1))

        @block.scalar
        def _(act):
            with act.Fori(0, TURNS) as g:
                t_max, t_turn = Tally(g, SLOTS), Tally(g, SLOTS)
                for s, p in order:
                    for b, r in (banks(s - 1) if s else []):
                        act.wait_ge(turned, t_turn.up())
                        nc.scalar.copy(pT[:, b, r], TB[r % 2][:]).then_inc(pT_made, 1)
                    for b, r in banks(s):
                        act.wait_ge(max_made, t_max.up())
                        for j in range(4):
                            i = nc.scalar.activation(pr[:, p, b, r, j], S[r][:, j], ACT.Exp,
                                                     bias=nmax[:, p, b, r, j:j + 1],
                                                     accum_out=rsum[:, p, b, r, j:j + 1])
                        i.then_inc(sco_used, 1)
                for p in range(STREAMS):
                    act.wait_ge(pstep, 2 * STREAMS + g * 2 * STREAMS + 2 * p + 2)
                    act.dma_start(rows(out, g, p), fin[:, p]).then_inc(stored[p], 16)
            for p in range(STREAMS):
                act.wait_ge(stored[p], 16 * TURNS + 16)

        @block.vector
        def _(dve):
            for m, k in ((x2_made, STREAMS), (c_used, STREAMS), (prod_used, 2), (sco_used, ROWS), (pT_made, 2),
                         (pstep, 2 * STREAMS), *((m, 16) for m in stored)):
                dve.sem_inc(m, k)
            dve.wait_ge(zeroed, 2)
            dve.wait_ge(w_in, 16 * 14)
            V = nc.vector
            with dve.Fori(0, TURNS) as g:
                t_step, t_prod, t_sco, t_exp = Tally(g, VSTEPS), Tally(g, PRODS), Tally(g, SLOTS), Tally(g, SLOTS)
                t_rstd = Tally(g, LNS)

                def chain(i):
                    i.then_inc(vstep, 1)
                    dve.wait_ge(vstep, t_step.up())

                def product():
                    dve.wait_ge(prod, t_prod.up())
                    return M[(t_prod.n - 1) % 2]

                def layer_norm(src, dst, p, made):
                    for b in range(PAIR):
                        i = V.bn_stats(stats[:, b], src[:, b])
                    chain(i)
                    V.memset(after_wait[:], 0.0)
                    for b in range(PAIR):
                        i = V.bn_aggr(mv[:, p, b], stats[:, b])
                    i.then_inc(var_made, 1)
                    dve.wait_ge(rstd_made, t_rstd.up())
                    for b in range(PAIR):
                        i = V.tensor_scalar(dst[:, b], src[:, b], mv[:, p, b, 0:1], rstd[:, p, b:b + 1],
                                            ALU.subtract, ALU.mult)
                    i.then_inc(made, 1)

                def biased(dst, bias, then=None, scalar=None):
                    m = product()
                    for u in range(2):
                        i = V.tensor_scalar(dst[:, u], m[:, u], bias[:, u:u + 1], scalar,
                                            ALU.add, *([then] if then else []))
                    i.then_inc(prod_used, 1)

                def copied(dst):
                    m = product()
                    V.tensor_copy(dst, m[:]).then_inc(prod_used, 1)

                def maxima(p, some):
                    for b, r in some:
                        dve.wait_ge(sco, t_sco.up())
                        V.tensor_reduce(nmax[:, p, b, r], S[r][:], AX.X, ALU.max, negate=True).then_inc(max_made, 1)

                def inverses(p, s):
                    for b, r in banks(s):
                        dve.wait_ge(sco_used, ROWS + t_exp.up())
                        V.reciprocal(rinv[:, p, b, r], rsum[:, p, b, r]).then_inc(inv_made, 1)

                def wide(a):
                    return a.unsqueeze(1).broadcast_to([P, PAIR, D])

                def into_node(p, c):
                    biased(qT[:, p], fb[:, c, TO_Q])
                    if c == 0:
                        biased(kT[:, p], fb[:, c, TO_K])
                    maxima(p, banks(c + 1))
                    for kind, to in FILL[c]:
                        if kind == TO_K:
                            biased(kT[:, p], fb[:, to, TO_K])
                        else:
                            copied(va[:, p, to % 2])
                    inverses(p, c + 1)

                for s, p in order:
                    if s == 0:
                        dve.wait_ge(x_in[p], g * 16 + 16)
                        dve.wait_ge(gathered[p], g * 16 * PAIR + 16 * PAIR)
                        dve.wait_ge(pstep, g * 2 * STREAMS + 2 * p + 2)
                        for b in range(PAIR):
                            i = V.scalar_tensor_tensor(out=x2[:, p, b], in0=xg[:, p, b], scalar=gate[:, p, b:b + 1],
                                                       in1=x1[:, p, b], op0=ALU.mult, op1=ALU.add)
                        chain(i)
                        dve.sem_inc(x2_made, 1)
                        layer_norm(x2[:, p], xn[:, p], p, xn_made)
                        copied(nd[:, p, 1])
                        m = product()
                        V.tensor_copy(cT[:, p, 0], m[:, 0])
                        V.tensor_copy(cT[0:C1, p, 1], m[0:C1, 1]).then_inc(prod_used, 1)
                        biased(qT[:, p], bq, ALU.mult, 0.25)
                        m = product()
                        for u in range(2):
                            V.tensor_scalar(kT[:, p, u], m[:, u], bk[:, u:u + 1], cst[:, C_EVEN:C_EVEN + 1], ALU.add, ALU.mult)
                            i = V.tensor_scalar(kO[:, p, u], m[:, u], bk[:, u:u + 1], cst[:, C_ODD:C_ODD + 1], ALU.add, ALU.mult)
                        i.then_inc(prod_used, 1)
                        maxima(p, banks(0)[:ROWS])
                        m = product()
                        for v, o in ((vE, 0), (vO, 16)):
                            i = V.tensor_copy(v[:, p].rearrange("t b (h f) -> t (b h) f", f=32)[:, :, o:o + 16],
                                              m[:].rearrange("t b (h f) -> t (b h) f", f=32)[:, :, o:o + 16])
                        i.then_inc(prod_used, 1)
                        maxima(p, banks(0)[ROWS:])
                        inverses(p, 0)
                    elif s == 1:
                        biased(oT[:, p], bv)
                        for h in range(HID // 2):
                            m = product()
                            for u in range(2):
                                i = V.tensor_scalar(hid[:, p, 2 * h + u], m[:, u], b1[:, 2 * h + u:2 * h + u + 1], 0.0,
                                                    ALU.add, ALU.max)
                            i.then_inc(prod_used, 1)
                        m = product()
                        V.tensor_tensor(xn[:, p], m[:], wide(b2[:]), ALU.add).then_inc(prod_used, 1)
                        dve.wait_ge(prod_used, 2 + t_prod.now())
                        chain(V.tensor_tensor(x2[:, p], xn[:, p], x2[:, p], ALU.add))
                        layer_norm(x2[:, p], xn[:, p], p, xn_made)
                        dve.wait_ge(xn_made, g * 2 * STREAMS + STREAMS + p + 1)
                        dve.sem_inc(x3n_made, 1)
                        copied(nd[:, p, SLOT_OF[-1]])
                        into_node(p, 0)
                    elif s < STAGES - 1:
                        c = s - 1
                        biased(oT[:, p], fb[:, c - 1, TO_V])
                        biased(nd[:, p, SLOT_OF[c - 1]], fb[:, c - 1, EDGE])
                        into_node(p, c)
                    else:
                        biased(oT[:, p], fb[:, NODES - 1, TO_V])
                        m = product()
                        i = V.tensor_tensor(xn[:, p], m[:], wide(row5[:]), ALU.add)
                        i.then_inc(prod_used, 1)
                        dve.wait_ge(prod_used, 2 + t_prod.now())
                        layer_norm(xn[:, p], xn[:, p], p, normed)
                assert (t_step.n, t_prod.n, t_sco.n, t_rstd.n) == (VSTEPS, PRODS, SLOTS, LNS), (t_step.n, t_prod.n, t_sco.n)

        @block.tensor
        def _(pe):
            ident = cst[:, C_ID:C_ID + P]
            T_ = nc.tensor
            pe.wait_ge(w_in, 16 * 14)
            with pe.Fori(0, TURNS) as g:
                t_free, t_sfree, t_norm = Tally(g, PRODS), Tally(g, SLOTS), Tally(g, SLOTS)
                t_tfree, t_pt = Tally(g, SLOTS), Tally(g, SLOTS)

                def bank():
                    pe.wait_ge(prod_used, t_free.up())
                    return M[(t_free.n - 1) % 2]

                def landed(back=0):
                    pe.wait_ge(prod_used, 2 + t_free.now() - back)

                def turn_rows(src):
                    m = bank()
                    for b in range(PAIR):
                        for u in range(2):
                            w = min(P, src.shape[2] - u * P)
                            i = T_.transpose(m[0:w, u, b * T:(b + 1) * T], src[:, b, u * P:u * P + w], ident)
                    i.then_inc(prod, 1)

                def project(*terms, K1=P):
                    m = bank()
                    last = len(terms) * 2 - 1
                    for u in range(2):
                        n = 0
                        for w, src in terms:
                            for k in range(2):
                                K = K1 if k else P
                                i = T_.matmul(m[:, u], w[0:K, k, u * P:(u + 1) * P], src[0:K, k], start=n == 0, stop=n == last)
                                n += 1
                    i.then_inc(prod, 1)

                def project_rows(*terms, K1=P):
                    m = bank()
                    for b in range(PAIR):
                        steps = [(w, src, k) for w, src in terms for k in range(w.shape[1])]
                        for n, (w, src, k) in enumerate(steps):
                            K = K1 if k == 1 else P
                            i = T_.matmul(m[:, b], src[0:K, k, b * T:(b + 1) * T], w[0:K, k], start=n == 0, stop=n == len(steps) - 1)
                    i.then_inc(prod, 1)

                def scores(p, pairs):
                    for j, (u, b, k) in enumerate(pairs):
                        for r in range(ROWS):
                            if j == 0:
                                pe.wait_ge(sco_used, t_sfree.up())
                            q = slice(32 * r, 32 * r + 32)
                            i = T_.matmul(S[r][:, j], qT[q, p, u, b * T:(b + 1) * T], k[q, p, u, b * T:(b + 1) * T],
                                          start=True, stop=True)
                            if j == 3:
                                i.then_inc(sco, 1)

                def turn_probs(p, some):
                    for b, r in some:
                        pe.wait_ge(norm_made, t_norm.up())
                        pe.wait_ge(pT_made, t_tfree.up())
                        for j in range(4):
                            i = T_.transpose(TB[r % 2][:, j], pr[:, p, b, r, j], ident)
                        i.then_inc(turned, 1)

                def into_node(p, c):
                    project((fw[:, c, TO_Q], nd[:, p, SLOT_OF[c - 1]]))
                    if c == 0:
                        project((fw[:, c, TO_K], nd[:, p, SLOT_OF[-1]]))
                    landed()
                    scores(p, [(j % 2, j // 2, kT) for j in range(4)])
                    for kind, to in FILL[c]:
                        src = nd[:, p, SLOT_OF[plan[to]["src"][kind]]]
                        (project if kind == TO_K else project_rows)((fw[:, to, kind], src))

                def attended(p, c):
                    turn_probs(p, banks(c + 1))
                    m = bank()
                    pe.wait_ge(pT_made, 2 + t_pt.up(ROWS))
                    for j in range(4):
                        u, b = j % 2, j // 2
                        for r in range(ROWS):
                            h = 32 * (4 * u + r)
                            i = T_.matmul(m[32 * r:32 * r + 32, u, b * T:(b + 1) * T], va[:, p, c % 2, b, h:h + 32],
                                          pT[:, 0, r, j], start=True, stop=True)
                    i.then_inc(prod, 1)
                    landed()

                for s, p in order:
                    if s == 0:
                        pe.wait_ge(xn_made, g * 2 * STREAMS + p + 1)
                        turn_rows(xn[:, p])
                        pe.wait_ge(c_in[p], g * 16 + 16)
                        turn_rows(ct[:, p])
                        landed(1)
                        project((wq, nd[:, p, 1]))
                        landed(1)
                        pe.sem_inc(c_used, 1)
                        project((wk, cT[:, p]), K1=C1)
                        landed()
                        scores(p, [(j // 2, 0, (kT, kO)[j % 2]) for j in range(4)])
                        project_rows((wv, cT[:, p]), K1=C1)
                        scores(p, [(j // 2, 1, (kT, kO)[j % 2]) for j in range(4)])
                    elif s == 1:
                        turn_probs(p, banks(0))
                        m = bank()
                        for b in range(PAIR):
                            pe.wait_ge(pT_made, 2 + t_pt.up(ROWS))
                            for j in range(4):
                                u, v = j // 2, (vE, vO)[j % 2]
                                for r in range(ROWS):
                                    h = 32 * (4 * u + r)
                                    i = T_.matmul(m[32 * r:32 * r + 32, u, b * T:(b + 1) * T], v[:, p, b, h:h + 32],
                                                  pT[:, b, r, j], start=j % 2 == 0, stop=j % 2 == 1)
                        i.then_inc(prod, 1)
                        landed()
                        for h in range(HID // 2):
                            project((w1[:, :, 2 * h * P:(2 * h + 2) * P], oT[:, p]))
                        landed()
                        project_rows((w2, hid[:, p]))
                        pe.wait_ge(xn_made, g * 2 * STREAMS + STREAMS + p + 1)
                        turn_rows(xn[:, p])
                        landed()
                        into_node(p, 0)
                    elif s < STAGES - 1:
                        c = s - 1
                        attended(p, c - 1)
                        project((fw[:, c - 1, OUT], oT[:, p]), (fw[:, c - 1, EDGE], nd[:, p, SLOT_OF[c - 2]]))
                        landed()
                        into_node(p, c)
                    else:
                        attended(p, NODES - 1)
                        last = NODES - 1
                        project_rows((fw[:, last, OUT], oT[:, p]), (fw[:, last, EDGE], nd[:, p, SLOT_OF[last - 1]]))

def build(nc, io, out):
    B, T, D = io["x"].shape
    E = io["L0_ffn_w_switch"].shape[1]
    CAP = int(CAP_FACTOR * B * T / E)
    AHEAD = PAIR * STREAMS
    scratch = {n: nc.dram_tensor(n, s, F32, kind="Internal").ap() for n, s in (
        ("x1", (B, T, D)), ("xn1", (B + AHEAD, T, D)), ("buf", (E * CAP, D)), ("y", (E * CAP, D)))}
    with ExitStack() as es:
        def sb(name, shape, dt=F32):
            return es.enter_context(nc.sbuf_tensor(name, [P] + shape, dt))

        cst = sb("consts_sb", [C_END])
        keep = {"logits": sb("logits", [B, E]), "gate": sb("gates", [B + AHEAD]), "slots": sb("slots", [B + AHEAD], U32)}
        consts_in = es.enter_context(nc.semaphore("consts_in"))
        with nc.Block() as block:
            @block.sync
            def _(sp):
                sp.dma_start(cst[:], io["consts"]).then_inc(consts_in, 16)
                sp.wait_ge(consts_in, 16)
        phase_first_attention(nc, io, scratch, keep, cst)
        phase_route(nc, io, scratch, keep, cst)
        phase_experts(nc, io, scratch, cst)
        fw = sb("cell_w", [NODES, KINDS, 2, D])
        fb = sb("cell_b", [NODES, KINDS - 1, 2])
        row5 = sb("last_edge_b", [D])
        phase_fuse(nc, io, fw, fb, row5, cst)
        phase_second_layer(nc, io, scratch, keep, fw, fb, row5, cst, out)


_PLAIN = ["x", "ctx_768", "L0_xattn_Wq", "L0_xattn_Wk", "L0_xattn_Wv", "L0_xattn_Wo", "L0_ffn_w_switch",
          "L0_ffn_b_switch", "L0_ffn_w1", "L0_ffn_w2", "L0_ffn_b2",
          "L1_xattn_Wq", "L1_xattn_Wk", "L1_xattn_Wv", "L1_xattn_W1", "L1_xattn_W2", "L1_xattn_b2",
          "L1_ffn_ew", "L1_ffn_act_w", "L1_ffn_We", "L1_ffn_be", "L1_ffn_Wq", "L1_ffn_Wk", "L1_ffn_Wv",
          "L1_ffn_Wo", "L1_ffn_ln_g", "L1_ffn_ln_b"]


def lay_out(inputs):
    arrays = {n: np.ascontiguousarray(inputs[n]) for n in _PLAIN}
    arrays["mask_BxS2_bf1"] = np.ascontiguousarray(inputs["mask_BxS2_bf1"]).view(np.uint8)
    b1 = np.asarray(inputs["L0_ffn_b1"])
    arrays["b1_cols"] = np.ascontiguousarray(b1.reshape(b1.shape[0], -1, P).transpose(0, 2, 1))
    for n in ("bq", "bk", "bv", "b1"):
        arrays[f"L1_xattn_{n}_cols"] = np.ascontiguousarray(np.asarray(inputs[f"L1_xattn_{n}"]).reshape(-1, P).T)
    be = np.asarray(inputs["L1_ffn_be"])
    arrays["be_cols"] = np.ascontiguousarray(be.reshape(be.shape[0], -1, P).transpose(2, 1, 0))
    arrays["edgesT"] = np.ascontiguousarray(np.asarray(inputs["L1_ffn_We"]).transpose(0, 2, 1))
    arrays["consts"] = consts_array()
    return arrays


def kernel(**inputs):
    import concourse.bacc as bacc
    from concourse.bass_utils import run_bass_kernel_spmd

    nc = bacc.Bacc("TRN2", target_bir_lowering=False, num_devices=1)
    arrays = {f"in_{n}": a for n, a in lay_out(inputs).items()}
    io = {n[3:]: nc.dram_tensor(n, a.shape, mybir.dt.from_np(a.dtype), kind="ExternalInput").ap()
          for n, a in arrays.items()}
    out = nc.dram_tensor("out", io["x"].shape, F32, kind="ExternalOutput").ap()
    build(nc, io, out)
    return run_bass_kernel_spmd(nc, [arrays], core_ids=[0]).results[0]["out"]
```

```python
from contextlib import ExitStack

import numpy as np

import concourse.bass as bass
from concourse import mybir

F32 = mybir.dt.float32
F32R = mybir.dt.float32r
U8 = mybir.dt.uint8
U32 = mybir.dt.uint32
ALU = mybir.AluOpType
ACT = mybir.ActivationFunctionType
AX = mybir.AxisListType

P = 128
PAIR = 2
STREAMS = 2
ROWS = 4
NEG = 2.0 ** 127


class Tally:

    def __init__(self, turn=0, per=0, base=0):
        self.past, self.n = turn * per + base, 0

    def up(self, k=1):
        self.n += k
        return self.past + self.n

    def now(self):
        return self.past + self.n


def consts_array():
    i = np.arange(P)
    parts = [np.eye(P), i[:, None] <= i[None, :], np.ones((P, P)),
             (i % 32 < 16)[:, None], (i % 32 >= 16)[:, None],
             np.broadcast_to(np.arange(8), (P, 8)), np.full((P, 2), -0.5),
             np.full((P, 2), 1e-5), np.full((P, 2), 1e-6)]
    return np.concatenate([np.asarray(a, np.float32) for a in parts], 1)


C_ID, C_TRI, C_ONE, C_EVEN, C_ODD, C_IOTA, C_HALF, C_EPS5, C_EPS6, C_END = \
    0, 128, 256, 384, 385, 386, 394, 396, 398, 400


def phase_first_attention(nc, io, scratch, keep, cst):
    x, ctx, mask = io["x"], io["ctx_768"], io["mask_BxS2_bf1"]
    B, T, D = x.shape
    C = ctx.shape[2]
    C1 = C - P
    TURNS = B // (PAIR * STREAMS)
    E = io["L0_ffn_w_switch"].shape[1]
    W2 = PAIR * T

    def rows(ap, g, p):
        v = ap.rearrange("(g p b) t d -> g p t b d", p=STREAMS, b=PAIR)
        return v[bass.ds(g, 1), p].rearrange("g t b d -> (g t) b d")

    with ExitStack() as es:
        def sb(name, shape, dt=F32):
            return es.enter_context(nc.sbuf_tensor("a_" + name, [P] + shape, dt))

        def sem(name):
            return es.enter_context(nc.semaphore("a_" + name))

        wq, wk, wv, wo = (sb(n, [2, D]) for n in ("wq", "wk", "wv", "wo"))
        wsw = sb("wsw", [2, E])
        xt = sb("x", [STREAMS, PAIR, D])
        ct = sb("ctx", [STREAMS, PAIR, C])
        mku = sb("mask_u8", [STREAMS, PAIR, T], U8)
        mk = sb("mask_add", [STREAMS, PAIR, T])
        stats = sb("stats", [PAIR, 6])
        after_wait = sb("after_wait", [1])
        mv = sb("mean_var", [STREAMS, PAIR, 2])
        veps = sb("var_eps", [STREAMS, PAIR])
        rstd = sb("rstd", [STREAMS, PAIR])
        xn = sb("xn", [STREAMS, PAIR, D])
        x1 = sb("x1", [STREAMS, PAIR, D])
        xn1 = sb("xn1", [STREAMS, PAIR, D])
        xT = sb("xT", [STREAMS, 2, W2])
        cT = sb("cT", [STREAMS, 2, W2])
        qT = sb("qT", [STREAMS, 2, W2])
        kE = sb("kT_even", [STREAMS, 2, W2])
        kO = sb("kT_odd", [STREAMS, 2, W2])
        vE = sb("v_even", [STREAMS, PAIR, D])
        vO = sb("v_odd", [STREAMS, PAIR, D])
        oT = sb("oT", [STREAMS, 2, W2])
        pr = sb("probs", [STREAMS, PAIR, ROWS, 4, T])
        nmax = sb("neg_max", [STREAMS, PAIR, ROWS, 4])
        rsum = sb("row_sum", [STREAMS, PAIR, ROWS, 4])
        rinv = sb("row_inv", [STREAMS, PAIR, ROWS, 4])
        pT = sb("probsT", [PAIR, ROWS, 4, T])
        S = [es.enter_context(nc.psum_tensor(f"a_scores{r}", [P, 4, T], F32)) for r in range(ROWS)]
        TB = [es.enter_context(nc.psum_tensor(f"a_turned{r}", [P, 4, T], F32)) for r in range(2)]
        M = [es.enter_context(nc.psum_tensor(f"a_product{r}", [P, 2, W2], F32)) for r in range(2)]

        w_in = sem("weights_in")
        x_in = [sem(f"x_in{p}") for p in range(STREAMS)]
        c_in = [sem(f"ctx_in{p}") for p in range(STREAMS)]
        mask_in = [sem(f"mask_in{p}") for p in range(STREAMS)]
        x_used, c_used, mask_used = sem("x_used"), sem("ctx_used"), sem("mask_used")
        x1_out = [sem(f"x1_out{p}") for p in range(STREAMS)]
        xn1_out = [sem(f"xn1_out{p}") for p in range(STREAMS)]
        x1_made, xn1_made = sem("x1_made"), sem("xn1_made")
        zeroed = sem("v_zeroed")
        vstep = sem("vector_step")
        var_made, veps_made, rstd_made = sem("var_made"), sem("veps_made"), sem("rstd_made")
        xn_made = sem("xn_made")
        prod, prod_used = sem("product_made"), sem("product_used")
        sco, sco_used = sem("scores_made"), sem("scores_used")
        max_made, exp_made, inv_made, norm_made = sem("max_made"), sem("exp_made"), sem("inv_made"), sem("norm_made")
        turned, pT_made = sem("turned_made"), sem("pT_made")

        STEPS_A = STREAMS * 3
        PRODS = STREAMS * (5 + 4)
        SLOTS = STREAMS * PAIR * ROWS

        block = es.enter_context(nc.Block())

        @block.sync
        def _(sp):
            for n, t in (("Wq", wq), ("Wo", wo)):
                sp.dma_start(t[:], io["L0_xattn_" + n].rearrange("(c p) n -> p c n", p=P)).then_inc(w_in, 16)
            for n, t in (("Wk", wk), ("Wv", wv)):
                w = io["L0_xattn_" + n]
                sp.dma_start(t[:, 0], w[0:P]).then_inc(w_in, 16)
                sp.dma_start(t[0:C1, 1], w[P:C]).then_inc(w_in, 16)
            sp.dma_start(wsw[:], io["L0_ffn_w_switch"].rearrange("(c p) n -> p c n", p=P)).then_inc(w_in, 16)
            with sp.Fori(0, TURNS) as g:
                for p in range(STREAMS):
                    sp.wait_ge(mask_used, g * STREAMS + p + 1)
                    sp.wait_ge(c_used, g * STREAMS + p + 1)
                    sp.dma_start(ct[:, p], rows(ctx, g, p)).then_inc(c_in[p], 16)
                    m = mask.rearrange("(g p b) t -> g p (b t)", p=STREAMS, b=PAIR)
                    m = m[bass.ds(g, 1), p].rearrange("g n -> (g n)").partition_broadcast(P)
                    sp.dma_start(mku[:, p].rearrange("q b t -> q (b t)"), m).then_inc(mask_in[p], 16)
                    sp.wait_ge(x_used, g * STREAMS + p + 1)
                    sp.dma_start(xt[:, p], rows(x, g, p)).then_inc(x_in[p], 16)

        @block.scalar
        def _(act):
            with act.Fori(0, TURNS) as g:
                t_max, t_turn = Tally(g, SLOTS), Tally(g, SLOTS)
                for p in range(STREAMS):
                    for b in range(PAIR):
                        for r in range(ROWS):
                            act.wait_ge(max_made, t_max.up())
                            for j in range(4):
                                e = pr[:, p, b, r, j]
                                i = nc.scalar.activation(e, e, ACT.Exp, bias=nmax[:, p, b, r, j:j + 1],
                                                         accum_out=rsum[:, p, b, r, j:j + 1])
                            i.then_inc(exp_made, 1)
                for p in range(STREAMS):
                    for b in range(PAIR):
                        for r in range(ROWS):
                            act.wait_ge(turned, t_turn.up())
                            nc.scalar.copy(pT[:, b, r], TB[r % 2][:]).then_inc(pT_made, 1)
                    act.wait_ge(x1_made, g * STREAMS + p + 1)
                    act.dma_start(rows(scratch["x1"], g, p), x1[:, p]).then_inc(x1_out[p], 16)
                    act.wait_ge(xn1_made, g * STREAMS + p + 1)
                    act.dma_start(rows(scratch["xn1"], g, p), xn1[:, p]).then_inc(xn1_out[p], 16)
            for p in range(STREAMS):
                act.wait_ge(x1_out[p], 16 * TURNS + 16)
                act.wait_ge(xn1_out[p], 16 * TURNS + 16)

        @block.gpsimd
        def _(pool):
            nc.gpsimd.memset(vE[:], 0.0).then_inc(zeroed, 1)
            nc.gpsimd.memset(vO[:], 0.0).then_inc(zeroed, 1)
            with pool.Fori(0, TURNS) as g:
                t_var, t_inv = Tally(g, 2 * STREAMS), Tally(g, SLOTS)

                def rsqrt(p):
                    n = t_var.up()
                    pool.wait_ge(var_made, n)
                    nc.gpsimd.tensor_tensor(veps[:, p], mv[:, p, :, 1], cst[:, C_EPS5:C_EPS5 + 2], ALU.add).then_inc(veps_made, 1)
                    pool.wait_ge(veps_made, n)
                    nc.gpsimd.tensor_tensor(rstd[:, p], veps[:, p], cst[:, C_HALF:C_HALF + 2], ALU.pow).then_inc(rstd_made, 1)

                for p in range(STREAMS):
                    rsqrt(p)
                    for b in range(PAIR):
                        for r in range(ROWS):
                            pool.wait_ge(inv_made, t_inv.up())
                            e = pr[:, p, b, r]
                            nc.gpsimd.tensor_tensor(e, e, rinv[:, p, b, r].unsqueeze(2).broadcast_to([P, 4, T]),
                                                    ALU.mult).then_inc(norm_made, 1)
                for p in range(STREAMS):
                    rsqrt(p)

        @block.vector
        def _(dve):
            for s, k in ((x_used, STREAMS), (c_used, STREAMS), (mask_used, STREAMS), (prod_used, 2),
                         (sco_used, ROWS), (pT_made, 2), *((m, 16) for m in x1_out + xn1_out)):
                dve.sem_inc(s, k)
            dve.wait_ge(zeroed, 2)
            with dve.Fori(0, TURNS) as g:
                t_step, t_prod, t_sco = Tally(g, STEPS_A), Tally(g, PRODS), Tally(g, SLOTS)
                t_rstd, t_exp = Tally(g, 2 * STREAMS), Tally(g, SLOTS)

                def chain(i):
                    i.then_inc(vstep, 1)
                    dve.wait_ge(vstep, t_step.up())

                def layer_norm(src, dst, p, made):
                    for b in range(PAIR):
                        i = nc.vector.bn_stats(stats[:, b], src[:, b])
                    chain(i)
                    nc.vector.memset(after_wait[:], 0.0)
                    for b in range(PAIR):
                        i = nc.vector.bn_aggr(mv[:, p, b], stats[:, b])
                    i.then_inc(var_made, 1)
                    dve.wait_ge(rstd_made, t_rstd.up())
                    for b in range(PAIR):
                        i = nc.vector.tensor_scalar(dst[:, b], src[:, b], mv[:, p, b, 0:1], rstd[:, p, b:b + 1],
                                                    ALU.subtract, ALU.mult)
                    i.then_inc(made, 1)

                def product():
                    dve.wait_ge(prod, t_prod.up())
                    return M[(t_prod.n - 1) % 2]

                for p in range(STREAMS):
                    dve.wait_ge(x_in[p], g * 16 + 16)
                    layer_norm(xt[:, p], xn[:, p], p, xn_made)
                    m = product()
                    nc.vector.tensor_copy(xT[:, p], m[:]).then_inc(prod_used, 1)
                    m = product()
                    nc.vector.tensor_copy(cT[:, p, 0], m[:, 0])
                    nc.vector.tensor_copy(cT[0:C1, p, 1], m[0:C1, 1]).then_inc(prod_used, 1)
                    m = product()
                    nc.vector.tensor_scalar(qT[:, p], m[:], 0.25, None, ALU.mult).then_inc(prod_used, 1)
                    m = product()
                    nc.vector.tensor_scalar(kE[:, p], m[:], cst[:, C_EVEN:C_EVEN + 1], None, ALU.mult)
                    nc.vector.tensor_scalar(kO[:, p], m[:], cst[:, C_ODD:C_ODD + 1], None, ALU.mult).then_inc(prod_used, 1)
                    m = product()
                    for v, o in ((vE, 0), (vO, 16)):
                        i = nc.vector.tensor_copy(
                            v[:, p].rearrange("t b (h f) -> t (b h) f", f=32)[:, :, o:o + 16],
                            m[:].rearrange("t b (h f) -> t (b h) f", f=32)[:, :, o:o + 16])
                    i.then_inc(prod_used, 1)
                    dve.wait_ge(mask_in[p], g * 16 + 16)
                    chain(nc.vector.tensor_scalar(mk[:, p], mku[:, p], 1.0, NEG, ALU.subtract, ALU.mult))
                    dve.sem_inc(mask_used, 1)
                    for b in range(PAIR):
                        for r in range(ROWS):
                            dve.wait_ge(sco, t_sco.up())
                            i = nc.vector.tensor_tensor(pr[:, p, b, r], S[r][:],
                                                        mk[:, p, b].unsqueeze(1).broadcast_to([P, 4, T]), ALU.add)
                            i.then_inc(sco_used, 1)
                            dve.wait_ge(sco_used, ROWS + t_sco.now())
                            nc.vector.tensor_reduce(nmax[:, p, b, r], pr[:, p, b, r], AX.X, ALU.max,
                                                    negate=True).then_inc(max_made, 1)
                    for b in range(PAIR):
                        for r in range(ROWS):
                            dve.wait_ge(exp_made, t_exp.up())
                            nc.vector.reciprocal(rinv[:, p, b, r], rsum[:, p, b, r]).then_inc(inv_made, 1)
                for p in range(STREAMS):
                    m = product()
                    nc.vector.tensor_copy(oT[:, p], m[:]).then_inc(prod_used, 1)
                    m = product()
                    dve.wait_ge(x1_out[p], g * 16 + 16)
                    i = nc.vector.tensor_tensor(x1[:, p], m[:], xt[:, p], ALU.add)
                    i.then_inc(prod_used, 1)
                    dve.wait_ge(prod_used, 2 + t_prod.now())
                    dve.sem_inc(x1_made, 1)
                    dve.sem_inc(x_used, 1)
                    dve.wait_ge(xn1_out[p], g * 16 + 16)
                    layer_norm(x1[:, p], xn1[:, p], p, xn1_made)
                    m = product()
                    nc.vector.tensor_copy(xT[:, p], m[:]).then_inc(prod_used, 1)
                    m = product()
                    nc.vector.tensor_copy(keep["logits"][:, bass.ds(g * 4 + p * 2, 2)],
                                          m[:, :, 0:E]).then_inc(prod_used, 1)
                assert t_step.n == STEPS_A, t_step.n
                assert t_prod.n == PRODS

        @block.tensor
        def _(pe):
            ident = cst[:, C_ID:C_ID + P]
            pe.wait_ge(w_in, 16 * 7)
            with pe.Fori(0, TURNS) as g:
                t_free, t_made = Tally(g, PRODS), Tally(g, PRODS)
                t_sfree, t_norm, t_pt = Tally(g, SLOTS), Tally(g, SLOTS), Tally(g, SLOTS)
                t_tfree = Tally(g, SLOTS)

                def bank():
                    pe.wait_ge(prod_used, t_free.up())
                    return M[(t_free.n - 1) % 2]

                def turn_rows(dst, src):
                    for b in range(PAIR):
                        for u in range(2):
                            w = min(P, src.shape[2] - u * P)
                            i = nc.tensor.transpose(dst[0:w, u, b * T:(b + 1) * T], src[:, b, u * P:u * P + w], ident)
                    i.then_inc(prod, 1)
                    t_made.up()

                def project(w, src, K1=P):
                    m = bank()
                    for u in range(2):
                        nc.tensor.matmul(m[:, u], w[:, 0, u * P:(u + 1) * P], src[:, 0], start=True, stop=False)
                        i = nc.tensor.matmul(m[:, u], w[0:K1, 1, u * P:(u + 1) * P], src[0:K1, 1], start=False, stop=True)
                    i.then_inc(prod, 1)
                    t_made.up()

                def project_rows(w, src, K1=P):
                    m = bank()
                    for b in range(PAIR):
                        n = w.shape[2]
                        nc.tensor.matmul(m[:, b, 0:n], src[:, 0, b * T:(b + 1) * T], w[:, 0], start=True, stop=False)
                        i = nc.tensor.matmul(m[:, b, 0:n], src[0:K1, 1, b * T:(b + 1) * T], w[0:K1, 1], start=False, stop=True)
                    i.then_inc(prod, 1)
                    t_made.up()

                for p in range(STREAMS):
                    pe.wait_ge(xn_made, g * STREAMS + p + 1)
                    turn_rows(bank(), xn[:, p])
                    pe.wait_ge(c_in[p], g * 16 + 16)
                    turn_rows(bank(), ct[:, p])
                    n_x, n_c = 2 + t_made.now() - 1, 2 + t_made.now()
                    pe.wait_ge(prod_used, n_x)
                    project(wq, xT[:, p])
                    pe.wait_ge(prod_used, n_c)
                    pe.sem_inc(c_used, 1)
                    project(wk, cT[:, p], C1)
                    project_rows(wv, cT[:, p], C1)
                    pe.wait_ge(prod_used, 2 + t_made.now() - 1)
                    for b in range(PAIR):
                        for j in range(4):
                            u, k = j // 2, (kE, kO)[j % 2]
                            for r in range(ROWS):
                                if j == 0:
                                    pe.wait_ge(sco_used, t_sfree.up())
                                s = slice(32 * r, 32 * r + 32)
                                i = nc.tensor.matmul(S[r][:, j], qT[s, p, u, b * T:(b + 1) * T],
                                                     k[s, p, u, b * T:(b + 1) * T], start=True, stop=True)
                                if j == 3:
                                    i.then_inc(sco, 1)
                for p in range(STREAMS):
                    for b in range(PAIR):
                        for r in range(ROWS):
                            pe.wait_ge(norm_made, t_norm.up())
                            pe.wait_ge(pT_made, t_tfree.up())
                            for j in range(4):
                                i = nc.tensor.transpose(TB[r % 2][:, j], pr[:, p, b, r, j], ident)
                            i.then_inc(turned, 1)
                    m = bank()
                    for b in range(PAIR):
                        pe.wait_ge(pT_made, 2 + t_pt.up(ROWS))
                        for j in range(4):
                            u, v = j // 2, (vE, vO)[j % 2]
                            for r in range(ROWS):
                                h = 32 * (4 * u + r)
                                i = nc.tensor.matmul(m[32 * r:32 * r + 32, u, b * T:(b + 1) * T],
                                                     v[:, p, b, h:h + 32], pT[:, b, r, j],
                                                     start=j % 2 == 0, stop=j % 2 == 1)
                    i.then_inc(prod, 1)
                    t_made.up()
                    pe.wait_ge(prod_used, 2 + t_made.now())
                    project_rows(wo, oT[:, p])
                    pe.wait_ge(xn1_made, g * STREAMS + p + 1)
                    turn_rows(bank(), xn1[:, p])
                    pe.wait_ge(prod_used, 2 + t_made.now())
                    project_rows(wsw, xT[:, p])

CAP_FACTOR = 0.5
OUT_OF_BOUNDS = 65536.0


def phase_route(nc, io, scratch, keep, cst):
    NT, T, D = io["x"].shape
    E = io["L0_ffn_b_switch"].shape[0]
    CAP = int(CAP_FACTOR * NT * T / E)
    LOADS = 4
    HALVES = 2
    TURNS = NT // (LOADS * HALVES)
    buf = scratch["buf"]

    with ExitStack() as es:
        def sb(name, shape, dt=F32):
            return es.enter_context(nc.sbuf_tensor("r_" + name, [P] + shape, dt))

        def sem(name):
            return es.enter_context(nc.semaphore("r_" + name))

        bsw = sb("b_switch", [E])
        lg, e, pb = keep["logits"], sb("exp", [NT, E]), sb("probs", [NT, E])
        oh = sb("one_hot", [NT, E])
        i8 = sb("iota_less_E", [E])
        tot = sb("tile_totals", [NT, E])
        run = [sb(f"running{n}", [NT, E]) for n in range(2)]
        mx, sm, pm, route, pos, kept, slot = (sb(n, [NT]) for n in ("mx", "sm", "pm", "route", "pos", "kept", "slotf"))
        zero = sb("zero", [2048])
        rows = sb("rows", [HALVES, LOADS, D])
        idx = sb("idx", [HALVES, LOADS], U32)
        after_wait = sb("after_wait", [1])
        cum = es.enter_context(nc.psum_tensor("r_cum", [P, NT, E], F32))
        all_ = es.enter_context(nc.psum_tensor("r_all", [P, NT, E], F32))

        b_in, zero_made, zeroed, pad_made = sem("b_in"), sem("zero_made"), sem("buf_zeroed"), sem("pad_made")
        step = sem("vector_step")
        shifted, exped, hot, counted = sem("shifted"), sem("exped"), sem("one_hot"), sem("counted")
        slots_made = sem("slots_made")
        rows_in = [sem(f"rows_in{h}") for h in range(HALVES)]
        sent = [sem(f"sent{h}") for h in range(HALVES)]
        idx_made, rows_free = sem("idx_made"), sem("rows_free")
        block = es.enter_context(nc.Block())

        @block.vector
        def _(dve):
            t = Tally()

            def chain(i):
                i.then_inc(step, 1)
                dve.wait_ge(step, t.up())

            def over_e(a):
                return a.unsqueeze(2).broadcast_to([P, NT, E])

            def over_t(a):
                return a.unsqueeze(1).broadcast_to([P, NT, E])

            V = nc.vector
            V.memset(zero[:], 0.0).then_inc(zero_made, 1)
            V.memset(keep["gate"][:, NT:], 0.0)
            V.memset(keep["slots"][:, NT:], 0)
            chain(V.tensor_scalar(i8[:], cst[:, C_IOTA:C_IOTA + E], float(E), None, ALU.subtract))
            dve.wait_ge(b_in, 16)
            chain(V.tensor_tensor(e[:], lg[:], over_t(bsw[:]), ALU.add))
            chain(V.tensor_reduce(mx[:], e[:], AX.X, ALU.max))
            V.tensor_tensor(pb[:], e[:], over_e(mx[:]), ALU.subtract).then_inc(shifted, 1)
            dve.wait_ge(exped, 1)
            chain(V.tensor_reduce(sm[:], e[:], AX.X, ALU.add))
            chain(V.reciprocal(mx[:], sm[:]))
            chain(V.tensor_tensor(pb[:], e[:], over_e(mx[:]), ALU.mult))
            chain(V.tensor_reduce(pm[:], pb[:], AX.X, ALU.max))
            chain(V.reciprocal(mx[:], pm[:]))
            V.tensor_tensor(keep["gate"][:, 0:NT], pm[:], mx[:], ALU.mult)
            chain(V.tensor_tensor(oh[:], pb[:], over_e(pm[:]), ALU.is_equal))
            chain(V.tensor_tensor(e[:], oh[:], over_t(i8[:]), ALU.mult))
            chain(V.tensor_reduce(route[:], e[:], AX.X, ALU.min))
            V.tensor_tensor(oh[:], over_t(i8[:]), over_e(route[:]), ALU.is_equal).then_inc(hot, 1)
            dve.wait_ge(counted, 1)
            chain(V.tensor_copy(tot[:], all_[:]))
            src, n, s = tot, 0, 1
            while s < NT:
                dst = run[n % 2]
                V.tensor_copy(dst[:, 0:s], src[:, 0:s])
                chain(V.tensor_tensor(dst[:, s:NT], src[:, s:NT], src[:, 0:NT - s], ALU.add))
                src, n, s = dst, n + 1, s * 2
            chain(V.tensor_tensor(e[:], src[:], tot[:], ALU.subtract))
            chain(V.tensor_tensor(pb[:], e[:], cum[:], ALU.add))
            chain(V.tensor_tensor(e[:], pb[:], oh[:], ALU.mult))
            chain(V.tensor_reduce(pos[:], e[:], AX.X, ALU.add))
            chain(V.tensor_scalar(kept[:], pos[:], float(CAP), OUT_OF_BOUNDS, ALU.is_gt, ALU.mult))
            chain(V.tensor_scalar(route[:], route[:], float(CAP), float(E * CAP - 1), ALU.mult, ALU.add))
            chain(V.tensor_tensor(slot[:], route[:], pos[:], ALU.add))
            V.tensor_tensor(keep["slots"][:, 0:NT], slot[:], kept[:], ALU.add).then_inc(slots_made, 1)

        @block.scalar
        def _(act):
            act.wait_ge(shifted, 1)
            nc.scalar.activation(e[:], pb[:], ACT.Exp).then_inc(exped, 1)

        @block.tensor
        def _(pe):
            pe.wait_ge(hot, 1)
            nc.tensor.matmul(cum[:], cst[:, C_TRI:C_TRI + P], oh[:], start=True, stop=True)
            nc.tensor.matmul(all_[:], cst[:, C_ONE:C_ONE + P], oh[:], start=True, stop=True).then_inc(counted, 1)

        @block.sync
        def _(sp):
            sp.dma_start(bsw[:], io["L0_ffn_b_switch"].partition_broadcast(P)).then_inc(b_in, 16)
            sp.wait_ge(zero_made, 1)
            parts = buf.rearrange("(n p r) d -> n p (r d)", p=P, r=2048 // D)
            for n in range(parts.shape[0]):
                sp.dma_start(parts[n], zero[:]).then_inc(zeroed, 16)
            src = scratch["xn1"][0:NT].rearrange("(g h n) t d -> g h t n d", h=HALVES, n=LOADS)
            pad = scratch["xn1"].shape[0] - NT
            for n in ("x1", "xn1"):
                spare = scratch[n][NT:NT + pad].rearrange("n t d -> (n t d)").rearrange("(p r) -> p r", p=P)
                sp.dma_start(spare, zero[:, 0:pad * T * D // P]).then_inc(pad_made, 16)
            sp.wait_ge(pad_made, 32)
            with sp.Fori(0, TURNS) as g:
                for h in range(HALVES):
                    sp.wait_ge(rows_free, g * HALVES + h + 1)
                    sp.dma_start(rows[:, h], src[bass.ds(g, 1), h].rearrange("g t n d -> (g t) n d")).then_inc(rows_in[h], 16)

        @block.gpsimd
        def _(pool):
            last_slot = pool.to_reg(E * CAP - 1)
            pool.sem_inc(rows_free, HALVES)
            pool.wait_ge(slots_made, 1)
            pool.wait_ge(zeroed, 16 * (E * CAP * D // (2048 * P)))
            with pool.Fori(0, TURNS) as g:
                for h in range(HALVES):
                    nc.gpsimd.tensor_copy(idx[:, h], keep["slots"][:, bass.ds((g * HALVES + h) * LOADS, LOADS)]).then_inc(idx_made, 1)
                    pool.wait_ge(idx_made, g * HALVES + h + 1)
                    pool.wait_ge(rows_in[h], g * 16 + 16)
                    nc.gpsimd.tensor_tensor(after_wait[:], cst[:, 0:1], cst[:, 0:1], ALU.add)
                    for n in range(LOADS):
                        nc.gpsimd.indirect_dma_start(
                            out=buf, out_offset=bass.IndirectOffsetOnAxis(ap=idx[:, h, n:n + 1], axis=0),
                            in_=rows[:, h, n], in_offset=None, bounds_check=last_slot, oob_is_err=False,
                        ).then_inc(sent[h], 16)
                for h in range(HALVES):
                    pool.wait_ge(sent[h], (g + 1) * 16 * LOADS)
                    pool.sem_inc(rows_free, 1)


def phase_experts(nc, io, scratch, cst):
    w1, w2, b2 = io["L0_ffn_w1"], io["L0_ffn_w2"], io["L0_ffn_b2"]
    E, D, H = w1.shape
    CAP = scratch["buf"].shape[0] // E
    NR = CAP // P
    HC = H // P
    SIDES = 2
    TURNS = E // SIDES
    YB = NR // 2

    with ExitStack() as es:
        def sb(name, shape, dt=F32):
            return es.enter_context(nc.sbuf_tensor("e_" + name, [P] + shape, dt))

        def sem(name):
            return es.enter_context(nc.semaphore("e_" + name))

        w1t = sb("w1", [SIDES, 2, H])
        w2t = sb("w2", [SIDES, HC, D])
        b1t = sb("b1", [SIDES, HC])
        b2t = sb("b2", [SIDES, D])
        xr = sb("rows", [SIDES, NR, D])
        xT = sb("rowsT", [2, CAP])
        hT = sb("hidden", [HC, CAP])
        y = sb("y", [YB, 2, D])
        TB = [es.enter_context(nc.psum_tensor(f"e_turned{r}", [P, CAP], F32)) for r in range(2)]
        HB = [es.enter_context(nc.psum_tensor(f"e_hidden{r}", [P, CAP], F32)) for r in range(4)]
        Y = [es.enter_context(nc.psum_tensor(f"e_out{r}", [P, 2, D], F32)) for r in range(2)]
        got = [sem(f"loaded{s}") for s in range(SIDES)]
        turned, xT_made, done = sem("turned"), sem("xT_made"), sem("expert_done")
        hid, hid_made = sem("hidden"), sem("hidden_made")
        out, y_made = sem("out"), sem("y_made")
        y_out = [sem(f"y_out{i}") for i in range(2)]
        block = es.enter_context(nc.Block())

        def of(ap, g, s):
            v = ap.rearrange("(g s) a n -> g s a n", s=SIDES)[bass.ds(g, 1), s]
            return v.rearrange("g (c p) n -> p (g c) n", p=P)

        @block.sync
        def _(sp):
            buf = scratch["buf"].rearrange("(e r) d -> e r d", e=E)
            with sp.Fori(0, TURNS) as g:
                for s in range(SIDES):
                    sp.wait_ge(done, g * SIDES + s + 1)
                    sp.dma_start(xr[:, s], of(buf, g, s)).then_inc(got[s], 16)
                    sp.dma_start(w1t[:, s], of(w1, g, s)).then_inc(got[s], 16)
                    sp.dma_start(w2t[:, s], of(w2, g, s)).then_inc(got[s], 16)
                    b1 = io["b1_cols"].rearrange("(g s) p c -> g s p c", s=SIDES)[bass.ds(g, 1), s]
                    sp.dma_start(b1t[:, s], b1.rearrange("g p c -> (g p) c")).then_inc(got[s], 16)
                    b = b2.rearrange("(g s) n -> g s n", s=SIDES)[bass.ds(g, 1), s]
                    sp.dma_start(b2t[:, s], b.rearrange("g n -> (g n)").partition_broadcast(P)).then_inc(got[s], 16)

        @block.tensor
        def _(pe):
            with pe.Fori(0, TURNS) as g:
                t_x, t_h, t_y = Tally(g, 2 * SIDES), Tally(g, HC * SIDES), Tally(g, YB * SIDES)
                for s in range(SIDES):
                    pe.wait_ge(got[s], g * 80 + 80)
                    for u in range(2):
                        pe.wait_ge(xT_made, t_x.up())
                        for n in range(NR):
                            i = nc.tensor.transpose(TB[u][:, n * P:(n + 1) * P], xr[:, s, n, u * P:(u + 1) * P],
                                                    cst[:, C_ID:C_ID + P])
                        i.then_inc(turned, 1)
                    pe.wait_ge(xT_made, 2 + t_x.now())
                    for c in range(HC):
                        pe.wait_ge(hid_made, t_h.up())
                        b = HB[c % 4]
                        for u in range(2):
                            i = nc.tensor.matmul(b[:], w1t[:, s, u, c * P:(c + 1) * P], xT[:, u], start=u == 0, stop=u == 1)
                        i.then_inc(hid, 1)
                    for q in range(YB):
                        pe.wait_ge(y_made, t_y.up())
                        for n in range(2):
                            r = (2 * q + n) * P
                            for c in range(HC):
                                if q == 0 and n == 0:
                                    pe.wait_ge(hid_made, 4 + t_h.now() - HC + c + 1)
                                i = nc.tensor.matmul(Y[q % 2][:, n], hT[:, c, r:r + P], w2t[:, s, c],
                                                     start=c == 0, stop=c == HC - 1)
                        i.then_inc(out, 1)

        @block.scalar
        def _(act):
            with act.Fori(0, TURNS) as g:
                t_h, t_y = Tally(g, HC * SIDES), Tally(g, YB * SIDES, YB)
                for s in range(SIDES):
                    act.wait_ge(got[s], g * 80 + 80)
                    for c in range(HC):
                        act.wait_ge(hid, t_h.up())
                        nc.scalar.activation(hT[:, c], HB[c % 4][:], ACT.Relu,
                                             bias=b1t[:, s, c:c + 1]).then_inc(hid_made, 1)
                    dst = scratch["y"].rearrange("(g s q n p) d -> g s q p n d", s=SIDES, q=YB, n=2, p=P)
                    for q in range(YB):
                        act.wait_ge(y_made, t_y.up())
                        act.dma_start(dst[bass.ds(g, 1), s, q].rearrange("g p n d -> (g p) n d"), y[:, q]).then_inc(y_out[q], 16)
            for q in range(YB):
                act.wait_ge(y_out[q], 16 * E + 16)

        @block.vector
        def _(dve):
            for m, k in ((xT_made, 2), (hid_made, 4), (y_made, YB), (done, SIDES), *((m, 16) for m in y_out)):
                dve.sem_inc(m, k)
            with dve.Fori(0, TURNS) as g:
                t_x, t_y = Tally(g, 2 * SIDES), Tally(g, YB * SIDES)
                for s in range(SIDES):
                    for u in range(2):
                        dve.wait_ge(turned, t_x.up())
                        nc.vector.tensor_copy(xT[:, u], TB[u][:]).then_inc(xT_made, 1)
                    dve.wait_ge(got[s], g * 80 + 80)
                    for q in range(YB):
                        dve.wait_ge(out, t_y.up())
                        dve.wait_ge(y_out[q], (g * SIDES + s + 1) * 16)
                        nc.vector.tensor_tensor(y[:, q], Y[q][:], b2t[:, s].unsqueeze(1).broadcast_to([P, 2, D]),
                                                ALU.add).then_inc(y_made, 1)
                    dve.wait_ge(y_made, YB + t_y.now())
                    dve.sem_inc(done, 1)



NODES, MAX_PREV, CELL_HEADS = 6, 5, 8
KINDS = 5
TO_Q, TO_K, TO_V, EDGE, OUT = range(KINDS)


def cell_plan():
    plan, at = [], 0
    for c in range(NODES):
        n = min(c + 1, MAX_PREV)
        plan.append(dict(edge=(at + n - 1, at, at + n // 2), src=(c - 1, c - n, c - n + n // 2)))
        at += n
    return plan


def phase_fuse(nc, io, fw, fb, row5, cst):
    plan = cell_plan()
    D = io["L1_ffn_Wq"].shape[1]
    SCALE = 1.0 / np.sqrt(D // CELL_HEADS)
    NE = io["L1_ffn_We"].shape[0]
    RING = 3
    jobs = [(c, k) for c in range(NODES) for k in (TO_Q, TO_K, TO_V)]
    W = [io["L1_ffn_" + n] for n in ("Wq", "Wk", "Wv")]

    with ExitStack() as es:
        def sb(name, shape, dt=F32):
            return es.enter_context(nc.sbuf_tensor("f_" + name, [P] + shape, dt))

        def sem(name):
            return es.enter_context(nc.semaphore("f_" + name))

        weT = sb("edgeT", [RING, 2, D])
        w = sb("w", [RING, 2, D])
        ew = sb("ew", [NODES, 3])
        aw = sb("act_w", [NODES])
        be = sb("be", [2, NE])
        M = [es.enter_context(nc.psum_tensor(f"f_product{r}", [P, 2, D], F32)) for r in range(2)]
        MB = es.enter_context(nc.psum_tensor("f_biases", [P, NODES, 3, 2], F32))
        small_in, plain_in = sem("small_in"), sem("plain_in")
        job_in = [sem(f"job_in{r}") for r in range(RING)]
        made, used, bias_made = sem("made"), sem("used"), sem("bias_made")
        block = es.enter_context(nc.Block())

        def halves(a):
            return a.rearrange("(c p) n -> p c n", p=P)

        @block.sync
        def _(sp):
            sp.dma_start(ew[:], io["L1_ffn_ew"].rearrange("c k -> (c k)").partition_broadcast(P)
                         .rearrange("p (c k) -> p c k", k=3)).then_inc(small_in, 16)
            sp.dma_start(aw[:], io["L1_ffn_act_w"].partition_broadcast(P)).then_inc(small_in, 16)
            sp.dma_start(be[:], io["be_cols"]).then_inc(small_in, 16)
            last = plan[-1]["edge"][0]
            sp.dma_start(row5[:], io["L1_ffn_be"][last].partition_broadcast(P)).then_inc(small_in, 16)
            for n, (c, k) in enumerate(jobs):
                if n >= RING:
                    sp.wait_ge(made, n - RING + 1)
                sp.dma_start(weT[:, n % RING], halves(io["edgesT"][plan[c]["edge"][k]])).then_inc(job_in[n % RING], 16)
                sp.dma_start(w[:, n % RING], halves(W[k][c])).then_inc(job_in[n % RING], 16)

        @block.scalar
        def _(act):
            for c in range(NODES):
                act.dma_start(fw[:, c, EDGE], halves(io["L1_ffn_We"][plan[c]["edge"][0]])).then_inc(plain_in, 16)
                act.dma_start(fw[:, c, OUT], halves(io["L1_ffn_Wo"][c])).then_inc(plain_in, 16)

        @block.tensor
        def _(pe):
            pe.wait_ge(small_in, 64)
            for n, (c, k) in enumerate(jobs):
                pe.wait_ge(job_in[n % RING], 32 * (n // RING + 1))
                if n >= 2:
                    pe.wait_ge(used, n - 1)
                e = plan[c]["edge"][k]
                for o in range(2):
                    for h in range(2):
                        nc.tensor.matmul(MB[:, c, k, o:o + 1], w[:, n % RING, h, o * P:(o + 1) * P],
                                         be[:, h, e:e + 1], start=h == 0, stop=h == 1)
                for u in range(2):
                    for h in range(2):
                        i = nc.tensor.matmul(M[n % 2][:, u], weT[:, n % RING, h, u * P:(u + 1) * P],
                                             w[:, n % RING, h], start=h == 0, stop=h == 1)
                i.then_inc(made, 1)

        @block.vector
        def _(dve):
            dve.wait_ge(small_in, 64)
            for n, (c, k) in enumerate(jobs):
                dve.wait_ge(made, n + 1)
                nc.vector.tensor_scalar(fw[:, c, k], M[n % 2][:], ew[:, c, k:k + 1], SCALE if k == TO_Q else 1.0,
                                        ALU.mult, ALU.mult).then_inc(used, 1)
            for c, k in jobs:
                nc.vector.tensor_scalar(fb[:, c, k], MB[:, c, k], ew[:, c, k:k + 1], SCALE if k == TO_Q else 1.0,
                                        ALU.mult, ALU.mult)
            dve.wait_ge(plain_in, 32 * NODES)
            for c in range(NODES):
                q = ew[:, c, TO_Q:TO_Q + 1]
                nc.vector.tensor_scalar(fw[:, c, EDGE], fw[:, c, EDGE], q, None, ALU.mult)
                nc.vector.tensor_scalar(fb[:, c, EDGE], be[:, :, plan[c]["edge"][0]], q, None, ALU.mult)
                nc.vector.tensor_scalar(fw[:, c, OUT], fw[:, c, OUT], aw[:, c:c + 1], None, ALU.mult)
            nc.vector.tensor_scalar(row5[:], row5[:], ew[:, NODES - 1, TO_Q:TO_Q + 1], None, ALU.mult)



def phase_second_layer(nc, io, scratch, keep, fw, fb, row5, cst, out):
    ctx = io["ctx_768"]
    B, T, D = io["x"].shape
    C = ctx.shape[2]
    C1 = C - P
    TURNS = B // (PAIR * STREAMS)
    W2 = PAIR * T
    HID = io["L1_xattn_W1"].shape[1] // P
    plan = cell_plan()
    RT = PAIR * STREAMS
    SLOT_OF = {-1: 0, 0: 1, 1: 2, 2: 3, 3: 0, 4: 1}
    STAGES = NODES + 2

    def rows(ap, g, p):
        v = ap.rearrange("(g p b) t d -> g p t b d", p=STREAMS, b=PAIR)
        return v[bass.ds(g, 1), p].rearrange("g t b d -> (g t) b d")

    with ExitStack() as es:
        def sb(name, shape, dt=F32):
            return es.enter_context(nc.sbuf_tensor("c_" + name, [P] + shape, dt))

        def sem(name):
            return es.enter_context(nc.semaphore("c_" + name))

        wq, wk, wv = (sb(n, [2, D]) for n in ("wq", "wk", "wv"))
        w1, w2 = sb("w1", [2, HID * P]), sb("w2", [HID, D])
        bq, bk, bv, b1 = sb("bq", [2]), sb("bk", [2]), sb("bv", [2]), sb("b1", [HID])
        b2, ln_g, ln_b = sb("b2", [D]), sb("ln_g", [D]), sb("ln_b", [D])
        x2 = sb("x2", [STREAMS, PAIR, D])
        xg = sb("routed", [STREAMS, PAIR, D])
        ct = sb("ctx", [STREAMS, PAIR, C])
        mvf = sb("front_mean_var", [STREAMS, PAIR, 2])
        vepsf = sb("front_var_eps", [STREAMS, PAIR])
        rstdf = sb("front_rstd", [STREAMS, PAIR])
        idx = sb("idx", [STREAMS, PAIR], U32)
        gate = sb("gate", [STREAMS, PAIR])
        x3 = sb("x3", [STREAMS, PAIR, D])
        xn = sb("xn", [STREAMS, PAIR, D])
        fin = sb("fin", [STREAMS, PAIR, D])
        stats = sb("stats", [PAIR, 6])
        after_wait = sb("after_wait", [1])
        after_wait_pool = sb("after_wait_pool", [1])
        mv = sb("mean_var", [STREAMS, PAIR, 2])
        veps = sb("var_eps", [STREAMS, PAIR])
        rstd = sb("rstd", [STREAMS, PAIR])
        nd = sb("nodes", [STREAMS, 4, 2, W2])
        hid = sb("hidden", [STREAMS, HID, W2])
        qT = sb("qT", [STREAMS, 2, W2])
        kT = sb("kT", [STREAMS, 2, W2])
        oT = sb("oT", [STREAMS, 2, W2])
        vE = sb("v_even", [STREAMS, PAIR, D])
        vO = sb("v_odd", [STREAMS, PAIR, D])
        va = sb("v", [STREAMS, PAIR, D])
        pr = sb("probs", [STREAMS, PAIR, ROWS, 4, T])
        nmax = sb("neg_max", [STREAMS, PAIR, ROWS, 4])
        rsum = sb("row_sum", [STREAMS, PAIR, ROWS, 4])
        rinv = sb("row_inv", [STREAMS, PAIR, ROWS, 4])
        pT = sb("probsT", [PAIR, ROWS, 4, T])
        kO = oT
        cT = hid

        S = [es.enter_context(nc.psum_tensor(f"c_scores{r}", [P, 4, T], F32)) for r in range(ROWS)]
        TB = [es.enter_context(nc.psum_tensor(f"c_turned{r}", [P, 4, T], F32)) for r in range(2)]
        M = [es.enter_context(nc.psum_tensor(f"c_product{r}", [P, 2, W2], F32)) for r in range(2)]

        w_in = sem("weights_in")
        x_in = [sem(f"x_in{p}") for p in range(STREAMS)]
        c_in = [sem(f"ctx_in{p}") for p in range(STREAMS)]
        r_in = [sem(f"routed_in{p}") for p in range(STREAMS)]
        gathered = [sem(f"gathered{p}") for p in range(STREAMS)]
        idx_made, c_used, xg_used, x2_used = sem("idx_made"), sem("ctx_used"), sem("routed_used"), sem("x2_used")
        zeroed, x3b_made, x3n_made = sem("v_zeroed"), sem("x3_ln_b_made"), sem("x3_normed")
        vstep, pstep = sem("vector_step"), sem("pool_step")
        var_made, veps_made, rstd_made, xn_made = sem("var_made"), sem("veps_made"), sem("rstd_made"), sem("xn_made")
        fvar_made, fveps_made, frstd_made, front_made = \
            sem("front_var_made"), sem("front_veps_made"), sem("front_rstd_made"), sem("front_made")
        normed = sem("cell_normed")
        stored = [sem(f"stored{p}") for p in range(STREAMS)]
        prod, prod_used = sem("product_made"), sem("product_used")
        sco, sco_used = sem("scores_made"), sem("scores_used")
        max_made, inv_made, norm_made = sem("max_made"), sem("inv_made"), sem("norm_made")
        turned, turned_used = sem("turned_made"), sem("turned_used")

        def banks(s):
            return [(b, r) for b in range((2, 1, 1, 1, 1, 1, 1, 0)[s]) for r in range(ROWS)]

        order = [(s, p) for s in range(1, STAGES) for p in range(STREAMS)]
        SLOTS = STREAMS * sum(len(banks(s)) for s in range(STAGES))
        PRODS = STREAMS * (5 + 7 + 4 * (NODES - 1) + 2)
        TURNED = SLOTS + STREAMS * NODES
        LNS = 2 * STREAMS
        VSTEPS = STREAMS * (3 + 2)
        assert PRODS % 2 == 0 and TURNED % 2 == 0

        def left_over(n):
            return [(1, (1, r)) for r in range(ROWS)] if n == 0 else \
                [(order[n - 1][1], k) for k in banks(order[n - 1][0])]

        def ahead(n):
            return [(order[n + 1][1], k) for k in banks(order[n + 1][0] - 1)] if n + 1 < len(order) else []

        block = es.enter_context(nc.Block())

        @block.sync
        def _(sp):
            def halves(a):
                return a.rearrange("(c p) n -> p c n", p=P)

            for t, a in ((wq[:], halves(io["L1_xattn_Wq"])), (w1[:], halves(io["L1_xattn_W1"])),
                         (w2[:], halves(io["L1_xattn_W2"])), (wk[:, 0], io["L1_xattn_Wk"][0:P]),
                         (wk[0:C1, 1], io["L1_xattn_Wk"][P:C]), (wv[:, 0], io["L1_xattn_Wv"][0:P]),
                         (wv[0:C1, 1], io["L1_xattn_Wv"][P:C]), (bq[:], io["L1_xattn_bq_cols"]),
                         (bk[:], io["L1_xattn_bk_cols"]), (bv[:], io["L1_xattn_bv_cols"]),
                         (b1[:], io["L1_xattn_b1_cols"]), (b2[:], io["L1_xattn_b2"].partition_broadcast(P)),
                         (ln_g[:], io["L1_ffn_ln_g"].partition_broadcast(P)),
                         (ln_b[:], io["L1_ffn_ln_b"].partition_broadcast(P))):
                sp.dma_start(t, a).then_inc(w_in, 16)
            for p in range(STREAMS):
                sp.dma_start(xg[:, p], rows(scratch["xn1"], 0, p)).then_inc(r_in[p], 16)
                sp.dma_start(x2[:, p], rows(scratch["x1"], 0, p)).then_inc(x_in[p], 16)
            with sp.Fori(0, TURNS) as g:
                for p in range(STREAMS):
                    sp.wait_ge(c_used, g * STREAMS + p + 1)
                    sp.dma_start(ct[:, p], rows(ctx, g, p)).then_inc(c_in[p], 16)
                for p in range(STREAMS):
                    sp.wait_ge(xg_used, g * STREAMS + p + 1)
                    sp.dma_start(xg[:, p], rows(scratch["xn1"][RT:], g, p)).then_inc(r_in[p], 16)
                for p in range(STREAMS):
                    sp.wait_ge(x2_used, g * STREAMS + p + 1)
                    sp.dma_start(x2[:, p], rows(scratch["x1"][RT:], g, p)).then_inc(x_in[p], 16)

        @block.gpsimd
        def _(pool):
            def gather(g, p):
                at = bass.ds(g * RT + p * PAIR, PAIR)
                nc.gpsimd.tensor_copy(idx[:, p], keep["slots"][:, at]).then_inc(idx_made, 1)
                pool.wait_ge(idx_made, g * 2 * STREAMS + 2 * p + 1)
                nc.gpsimd.tensor_copy(gate[:, p], keep["gate"][:, at]).then_inc(idx_made, 1)
                pool.wait_ge(idx_made, g * 2 * STREAMS + 2 * p + 2)
                pool.wait_ge(r_in[p], g * 16 + 16)
                nc.gpsimd.tensor_tensor(after_wait_pool[:], cst[:, 0:1], cst[:, 0:1], ALU.add)
                for b in range(PAIR):
                    nc.gpsimd.indirect_dma_start(
                        out=xg[:, p, b], out_offset=None, in_=scratch["y"],
                        in_offset=bass.IndirectOffsetOnAxis(ap=idx[:, p, b:b + 1], axis=0),
                        bounds_check=last_slot, oob_is_err=False).then_inc(gathered[p], 16)

            last_slot = pool.to_reg(scratch["y"].shape[0] - 1)
            nc.gpsimd.memset(vE[:], 0.0).then_inc(zeroed, 1)
            nc.gpsimd.memset(vO[:], 0.0).then_inc(zeroed, 1)
            for p in range(STREAMS):
                gather(0, p)
            pool.wait_ge(w_in, 16 * 14)

            def rsqrt_front(g, p):
                pool.wait_ge(fvar_made, g * STREAMS + p + 1)
                nc.gpsimd.tensor_tensor(vepsf[:, p], mvf[:, p, :, 1], cst[:, C_EPS5:C_EPS5 + 2], ALU.add).then_inc(fveps_made, 1)
                pool.wait_ge(fveps_made, g * STREAMS + p + 1)
                nc.gpsimd.tensor_tensor(rstdf[:, p], vepsf[:, p], cst[:, C_HALF:C_HALF + 2], ALU.pow).then_inc(frstd_made, 1)

            for p in range(STREAMS):
                rsqrt_front(0, p)
            with pool.Fori(0, TURNS) as g:
                t_var, t_inv = Tally(g, LNS), Tally(g, SLOTS)

                def rsqrt(p, eps):
                    n = t_var.up()
                    pool.wait_ge(var_made, n)
                    nc.gpsimd.tensor_tensor(veps[:, p], mv[:, p, :, 1], cst[:, eps:eps + 2], ALU.add).then_inc(veps_made, 1)
                    pool.wait_ge(veps_made, n)
                    nc.gpsimd.tensor_tensor(rstd[:, p], veps[:, p], cst[:, C_HALF:C_HALF + 2], ALU.pow).then_inc(rstd_made, 1)

                def wide(a):
                    return a.unsqueeze(1).broadcast_to([P, PAIR, D])

                def norms(some):
                    for p, (b, r) in some:
                        pool.wait_ge(inv_made, t_inv.up())
                        e = pr[:, p, b, r]
                        nc.gpsimd.tensor_tensor(e, e, rinv[:, p, b, r].unsqueeze(2).broadcast_to([P, 4, T]),
                                                ALU.mult).then_inc(norm_made, 1)

                norms([(p, k) for p in range(STREAMS) for k in banks(0)][:-ROWS])
                for n, (s, p) in enumerate(order):
                    norms(left_over(n))
                    if s == 1:
                        rsqrt(p, C_EPS5)
                    if s == 2:
                        pool.wait_ge(x3n_made, g * STREAMS + p + 1)
                        nc.gpsimd.tensor_tensor(x3[:, p], x3[:, p], wide(ln_b[:]), ALU.add).then_inc(x3b_made, 1)
                    if s == 3:
                        gather(g + 1, p)
                    if s == 5:
                        rsqrt_front(g + 1, p)
                    if s == STAGES - 1:
                        rsqrt(p, C_EPS6)
                        pool.wait_ge(normed, g * STREAMS + p + 1)
                        pool.wait_ge(stored[p], g * 16 + 16)
                        nc.gpsimd.tensor_tensor(fin[:, p], xn[:, p], wide(ln_g[:]), ALU.mult).then_inc(pstep, 1)
                        pool.wait_ge(pstep, 2 * STREAMS + g * 2 * STREAMS + 2 * p + 1)
                        pool.wait_ge(x3b_made, g * STREAMS + p + 1)
                        nc.gpsimd.tensor_tensor(fin[:, p], fin[:, p], x3[:, p], ALU.add).then_inc(pstep, 1)
            for p in range(STREAMS):
                pool.wait_ge(gathered[p], 16 * PAIR * (TURNS + 1))

        @block.scalar
        def _(act):
            with act.Fori(0, TURNS) as g:
                t_max, t_turn = Tally(g, SLOTS), Tally(g, TURNED)

                def evacuate(dst):
                    act.wait_ge(turned, t_turn.up())
                    nc.scalar.copy(dst, TB[(t_turn.n - 1) % 2][:]).then_inc(turned_used, 1)

                def turned_probs(some):
                    for _, (b, r) in some:
                        evacuate(pT[:, b, r])

                def exponentials(p, some):
                    for b, r in some:
                        act.wait_ge(max_made, t_max.up())
                        for j in range(4):
                            i = nc.scalar.activation(pr[:, p, b, r, j], S[r][:, j], ACT.Exp,
                                                     bias=nmax[:, p, b, r, j:j + 1],
                                                     accum_out=rsum[:, p, b, r, j:j + 1])
                        i.then_inc(sco_used, 1)

                def v(p):
                    evacuate(va[:, p].rearrange("t b (h f) -> t (b h) f", f=T))

                exponentials(0, banks(0))
                first = [(0, k) for k in banks(0)]
                turned_probs(first[:ROWS])
                exponentials(1, banks(0)[:ROWS])
                turned_probs(first[ROWS:])
                exponentials(1, banks(0)[ROWS:])
                for n, (s, p) in enumerate(order):
                    if s == 1:
                        turned_probs(ahead(n))
                        v(p)
                    elif s < STAGES - 1:
                        v(p)
                        turned_probs(ahead(n))
                    else:
                        turned_probs(ahead(n))
                    exponentials(p, banks(s))
                for p in range(STREAMS):
                    act.wait_ge(pstep, 2 * STREAMS + g * 2 * STREAMS + 2 * p + 2)
                    act.dma_start(rows(out, g, p), fin[:, p]).then_inc(stored[p], 16)
            for p in range(STREAMS):
                act.wait_ge(stored[p], 16 * TURNS + 16)

        @block.vector
        def _(dve):
            V = nc.vector
            for m, k in ((c_used, STREAMS), (prod_used, 2), (sco_used, ROWS), (turned_used, 2), (pstep, 2 * STREAMS),
                         *((m, 16) for m in stored)):
                dve.sem_inc(m, k)
            dve.wait_ge(zeroed, 2)
            dve.wait_ge(w_in, 16 * 14)

            def statistics(src, dst, made, stepped):
                for b in range(PAIR):
                    i = V.bn_stats(stats[:, b], src[:, b])
                i.then_inc(vstep, 1)
                dve.wait_ge(vstep, stepped)
                V.memset(after_wait[:], 0.0)
                for b in range(PAIR):
                    i = V.bn_aggr(dst[:, b], stats[:, b])
                i.then_inc(made, 1)

            def front_statistics(g, p, step):
                dve.wait_ge(x_in[p], g * 16 + 16)
                dve.wait_ge(gathered[p], g * 16 * PAIR + 16 * PAIR)
                for b in range(PAIR):
                    i = V.scalar_tensor_tensor(out=x2[:, p, b], in0=xg[:, p, b], scalar=gate[:, p, b:b + 1],
                                               in1=x2[:, p, b], op0=ALU.mult, op1=ALU.add)
                i.then_inc(vstep, 1)
                dve.wait_ge(vstep, step())
                statistics(x2[:, p], mvf[:, p], fvar_made, step())

            def front_norm(g, p):
                dve.wait_ge(frstd_made, g * STREAMS + p + 1)
                for b in range(PAIR):
                    i = V.tensor_scalar(xg[:, p, b], x2[:, p, b], mvf[:, p, b, 0:1], rstdf[:, p, b:b + 1],
                                        ALU.subtract, ALU.mult)
                i.then_inc(front_made, 1)

            before = Tally()
            for p in range(STREAMS):
                front_statistics(0, p, before.up)
            for p in range(STREAMS):
                front_norm(0, p)
            with dve.Fori(0, TURNS) as g:
                t_step, t_prod, t_sco = Tally(g, VSTEPS, 2 * STREAMS), Tally(g, PRODS), Tally(g, SLOTS)
                t_exp, t_rstd = Tally(g, SLOTS), Tally(g, LNS)

                def product():
                    dve.wait_ge(prod, t_prod.up())
                    return M[(t_prod.n - 1) % 2]

                def layer_norm(src, dst, p, made):
                    statistics(src, mv[:, p], var_made, t_step.up())
                    dve.wait_ge(rstd_made, t_rstd.up())
                    for b in range(PAIR):
                        i = V.tensor_scalar(dst[:, b], src[:, b], mv[:, p, b, 0:1], rstd[:, p, b:b + 1],
                                            ALU.subtract, ALU.mult)
                    i.then_inc(made, 1)

                def biased(dst, bias, then=None, scalar=None):
                    m = product()
                    for u in range(2):
                        i = V.tensor_scalar(dst[:, u], m[:, u], bias[:, u:u + 1], scalar,
                                            ALU.add, *([then] if then else []))
                    i.then_inc(prod_used, 1)

                def copied(dst):
                    m = product()
                    V.tensor_copy(dst, m[:]).then_inc(prod_used, 1)

                def maxima(p, some):
                    for b, r in some:
                        dve.wait_ge(sco, t_sco.up())
                        V.tensor_reduce(nmax[:, p, b, r], S[r][:], AX.X, ALU.max, negate=True).then_inc(max_made, 1)

                def inverses(some):
                    for p, (b, r) in some:
                        dve.wait_ge(sco_used, ROWS + t_exp.up())
                        V.reciprocal(rinv[:, p, b, r], rsum[:, p, b, r]).then_inc(inv_made, 1)

                def wide(a):
                    return a.unsqueeze(1).broadcast_to([P, PAIR, D])

                def front(p):
                    copied(nd[:, p, 1])
                    dve.sem_inc(xg_used, 1)
                    m = product()
                    V.tensor_copy(cT[:, p, 0], m[:, 0])
                    V.tensor_copy(cT[0:C1, p, 1], m[0:C1, 1]).then_inc(prod_used, 1)
                    biased(qT[:, p], bq, ALU.mult, 0.25)
                    m = product()
                    for u in range(2):
                        V.tensor_scalar(kT[:, p, u], m[:, u], bk[:, u:u + 1], cst[:, C_EVEN:C_EVEN + 1], ALU.add, ALU.mult)
                        i = V.tensor_scalar(kO[:, p, u], m[:, u], bk[:, u:u + 1], cst[:, C_ODD:C_ODD + 1], ALU.add, ALU.mult)
                    i.then_inc(prod_used, 1)
                    m = product()
                    for v, o in ((vE, 0), (vO, 16)):
                        i = V.tensor_copy(v[:, p].rearrange("t b (h f) -> t (b h) f", f=32)[:, :, o:o + 16],
                                          m[:].rearrange("t b (h f) -> t (b h) f", f=32)[:, :, o:o + 16])
                    i.then_inc(prod_used, 1)

                rounds = [(p, banks(0)[b * ROWS:(b + 1) * ROWS]) for p in range(STREAMS) for b in range(PAIR)]
                front(0)
                maxima(*rounds[0])
                front(1)
                for n in range(1, len(rounds)):
                    inverses([(rounds[n - 1][0], k) for k in rounds[n - 1][1]])
                    maxima(*rounds[n])
                for n, (s, p) in enumerate(order):
                    late = left_over(n)
                    if s == 1:
                        biased(oT[:, p], bv)
                        for h in range(HID // 2):
                            m = product()
                            for u in range(2):
                                i = V.tensor_scalar(hid[:, p, 2 * h + u], m[:, u], b1[:, 2 * h + u:2 * h + u + 1], 0.0,
                                                    ALU.add, ALU.max)
                            i.then_inc(prod_used, 1)
                            if h == 0:
                                inverses(late)
                        m = product()
                        V.tensor_tensor(xn[:, p], m[:], wide(b2[:]), ALU.add).then_inc(prod_used, 1)
                        dve.wait_ge(prod_used, 2 + t_prod.now())
                        dve.wait_ge(pstep, g * 2 * STREAMS + 2 * p + 2)
                        V.tensor_tensor(x3[:, p], xn[:, p], x2[:, p], ALU.add).then_inc(vstep, 1)
                        dve.wait_ge(vstep, t_step.up())
                        dve.sem_inc(x2_used, 1)
                        layer_norm(x3[:, p], xn[:, p], p, xn_made)
                        dve.wait_ge(xn_made, g * STREAMS + p + 1)
                        dve.sem_inc(x3n_made, 1)
                        copied(nd[:, p, SLOT_OF[-1]])
                        biased(qT[:, p], fb[:, 0, TO_Q])
                        biased(kT[:, p], fb[:, 0, TO_K])
                        maxima(p, banks(s))
                    elif s < STAGES - 1:
                        c = s - 1
                        biased(oT[:, p], fb[:, c - 1, TO_V])
                        biased(kT[:, p], fb[:, c, TO_K])
                        inverses(late[:2])
                        biased(nd[:, p, SLOT_OF[c - 1]], fb[:, c - 1, EDGE])
                        inverses(late[2:])
                        biased(qT[:, p], fb[:, c, TO_Q])
                        maxima(p, banks(s))
                        if s == 4:
                            front_statistics(g + 1, p, t_step.up)
                        if s == 5:
                            front_norm(g + 1, p)
                    else:
                        biased(oT[:, p], fb[:, NODES - 1, TO_V])
                        inverses(late)
                        m = product()
                        V.tensor_tensor(xn[:, p], m[:], wide(row5[:]), ALU.add).then_inc(prod_used, 1)
                        dve.wait_ge(prod_used, 2 + t_prod.now())
                        layer_norm(xn[:, p], xn[:, p], p, normed)
                assert (t_step.n, t_prod.n, t_sco.n, t_rstd.n) == (VSTEPS, PRODS, SLOTS, LNS), (t_step.n, t_prod.n, t_sco.n, t_rstd.n)

        @block.tensor
        def _(pe):
            ident = cst[:, C_ID:C_ID + P]
            T_ = nc.tensor
            pe.wait_ge(w_in, 16 * 14)
            with pe.Fori(0, TURNS) as g:
                t_free, t_sfree, t_norm = Tally(g, PRODS), Tally(g, SLOTS), Tally(g, SLOTS)
                t_turn = Tally(g, TURNED)

                def bank():
                    pe.wait_ge(prod_used, t_free.up())
                    return M[(t_free.n - 1) % 2]

                def turn_bank():
                    pe.wait_ge(turned_used, t_turn.up())
                    return TB[(t_turn.n - 1) % 2]

                def landed(back=0):
                    pe.wait_ge(prod_used, 2 + t_free.now() - back)

                def turn_rows(src):
                    m = bank()
                    for b in range(PAIR):
                        for u in range(2):
                            w = min(P, src.shape[2] - u * P)
                            i = T_.transpose(m[0:w, u, b * T:(b + 1) * T], src[:, b, u * P:u * P + w], ident)
                    i.then_inc(prod, 1)

                def project(*terms, K1=P):
                    m = bank()
                    last = len(terms) * 2 - 1
                    for u in range(2):
                        n = 0
                        for w, src in terms:
                            for k in range(2):
                                K = K1 if k else P
                                i = T_.matmul(m[:, u], w[0:K, k, u * P:(u + 1) * P], src[0:K, k], start=n == 0, stop=n == last)
                                n += 1
                    i.then_inc(prod, 1)

                def rows_of(m, b, terms, K1=P):
                    steps = [(w, src, k) for w, src in terms for k in range(w.shape[1])]
                    for n, (w, src, k) in enumerate(steps):
                        K = K1 if k == 1 else P
                        i = T_.matmul(m, src[0:K, k, b * T:(b + 1) * T], w[0:K, k], start=n == 0, stop=n == len(steps) - 1)
                    return i

                def project_rows(*terms, K1=P):
                    m = bank()
                    for b in range(PAIR):
                        i = rows_of(m[:, b], b, terms, K1)
                    i.then_inc(prod, 1)

                def scores(p, j, u, b, k):
                    for r in range(ROWS):
                        if j == 0:
                            pe.wait_ge(sco_used, t_sfree.up())
                        q = slice(32 * r, 32 * r + 32)
                        i = T_.matmul(S[r][:, j], qT[q, p, u, b * T:(b + 1) * T], k[q, p, u, b * T:(b + 1) * T],
                                      start=True, stop=True)
                        if j == 3:
                            i.then_inc(sco, 1)

                def turn_probs(some):
                    for p, (b, r) in some:
                        pe.wait_ge(norm_made, t_norm.up())
                        m = turn_bank()
                        for j in range(4):
                            i = T_.transpose(m[:, j], pr[:, p, b, r, j], ident)
                        i.then_inc(turned, 1)

                def v_of(p, c, between=lambda: None):
                    m = turn_bank()
                    src = nd[:, p, SLOT_OF[plan[c]["src"][TO_V]]]
                    for b in range(PAIR):
                        i = rows_of(m[:, 2 * b:2 * b + 2].rearrange("t a f -> t (a f)"), b, [(fw[:, c, TO_V], src)])
                        if b == 0:
                            between()
                    i.then_inc(turned, 1)

                def node_scores(p, js):
                    for j in js:
                        scores(p, j, j % 2, j // 2, kT)

                def attend(p, pairs):
                    pe.wait_ge(turned_used, 2 + t_turn.now())
                    m = bank()
                    for b, u, v, start, stop, row, j in pairs:
                        for r in range(ROWS):
                            h = 32 * (4 * u + r)
                            i = T_.matmul(m[32 * r:32 * r + 32, u, b * T:(b + 1) * T], v[:, p, b, h:h + 32],
                                          pT[:, row, r, j], start=start, stop=stop)
                    i.then_inc(prod, 1)

                def front(p):
                    pe.wait_ge(front_made, g * STREAMS + p + 1)
                    turn_rows(xg[:, p])
                    pe.wait_ge(c_in[p], g * 16 + 16)
                    turn_rows(ct[:, p])
                    landed(1)
                    project((wq, nd[:, p, 1]))
                    landed(1)
                    pe.sem_inc(c_used, 1)
                    project((wk, cT[:, p]), K1=C1)
                    project_rows((wv, cT[:, p]), K1=C1)
                    landed(1)

                def layer_scores(p, b):
                    for j in range(4):
                        scores(p, j, j // 2, b, (kT, kO)[j % 2])

                front(0)
                layer_scores(0, 0)
                front(1)
                layer_scores(0, 1)
                first = [(0, k) for k in banks(0)]
                turn_probs(first[:ROWS])
                layer_scores(1, 0)
                turn_probs(first[ROWS:])
                layer_scores(1, 1)
                for n, (s, p) in enumerate(order):
                    some = ahead(n)
                    if s == 1:
                        attend(p, [(b, j // 2, (vE, vO)[j % 2], j % 2 == 0, j % 2 == 1, b, j)
                                         for b in range(PAIR) for j in range(4)])
                        turn_probs(some[:-ROWS])
                        landed()
                        for h in range(HID // 2):
                            project((w1[:, :, 2 * h * P:(2 * h + 2) * P], oT[:, p]))
                        landed()
                        project_rows((w2, hid[:, p]))
                        turn_probs(some[-ROWS:])
                        pe.wait_ge(xn_made, g * STREAMS + p + 1)
                        turn_rows(xn[:, p])
                        landed()
                        project((fw[:, 0, TO_Q], nd[:, p, SLOT_OF[-1]]))
                        project((fw[:, 0, TO_K], nd[:, p, SLOT_OF[-1]]))

                        def half():
                            landed()
                            node_scores(p, (0, 1))

                        v_of(p, 0, half)
                        node_scores(p, (2, 3))
                    elif s < STAGES - 1:
                        c = s - 1
                        attend(p, [(j // 2, j % 2, va, True, True, 0, j) for j in range(4)])
                        project((fw[:, c, TO_K], nd[:, p, SLOT_OF[plan[c]["src"][TO_K]]]))
                        landed(1)
                        project((fw[:, c - 1, OUT], oT[:, p]), (fw[:, c - 1, EDGE], nd[:, p, SLOT_OF[c - 2]]))
                        if c >= 2:
                            v_of(p, c)
                        landed()
                        project((fw[:, c, TO_Q], nd[:, p, SLOT_OF[c - 1]]))
                        if c == 1:
                            v_of(p, c)
                        turn_probs(some[:2])
                        landed()
                        node_scores(p, (0, 1))
                        turn_probs(some[2:])
                        node_scores(p, (2, 3))
                    else:
                        last = NODES - 1
                        attend(p, [(j // 2, j % 2, va, True, True, 0, j) for j in range(4)])
                        landed()
                        project_rows((fw[:, last, OUT], oT[:, p]), (fw[:, last, EDGE], nd[:, p, SLOT_OF[last - 1]]))
                        turn_probs(some)

def build(nc, io, out):
    B, T, D = io["x"].shape
    E = io["L0_ffn_w_switch"].shape[1]
    CAP = int(CAP_FACTOR * B * T / E)
    AHEAD = PAIR * STREAMS
    scratch = {n: nc.dram_tensor(n, s, F32, kind="Internal").ap() for n, s in (
        ("x1", (B + AHEAD, T, D)), ("xn1", (B + AHEAD, T, D)), ("buf", (E * CAP, D)), ("y", (E * CAP, D)))}
    with ExitStack() as es:
        def sb(name, shape, dt=F32):
            return es.enter_context(nc.sbuf_tensor(name, [P] + shape, dt))

        cst = sb("consts_sb", [C_END])
        keep = {"logits": sb("logits", [B, E]), "gate": sb("gates", [B + AHEAD]), "slots": sb("slots", [B + AHEAD], U32)}
        consts_in = es.enter_context(nc.semaphore("consts_in"))
        with nc.Block() as block:
            @block.sync
            def _(sp):
                sp.dma_start(cst[:], io["consts"]).then_inc(consts_in, 16)
                sp.wait_ge(consts_in, 16)
        phase_first_attention(nc, io, scratch, keep, cst)
        phase_route(nc, io, scratch, keep, cst)
        phase_experts(nc, io, scratch, cst)
        fw = sb("cell_w", [NODES, KINDS, 2, D])
        fb = sb("cell_b", [NODES, KINDS - 1, 2])
        row5 = sb("last_edge_b", [D])
        phase_fuse(nc, io, fw, fb, row5, cst)
        phase_second_layer(nc, io, scratch, keep, fw, fb, row5, cst, out)


_PLAIN = ["x", "ctx_768", "L0_xattn_Wq", "L0_xattn_Wk", "L0_xattn_Wv", "L0_xattn_Wo", "L0_ffn_w_switch",
          "L0_ffn_b_switch", "L0_ffn_w1", "L0_ffn_w2", "L0_ffn_b2",
          "L1_xattn_Wq", "L1_xattn_Wk", "L1_xattn_Wv", "L1_xattn_W1", "L1_xattn_W2", "L1_xattn_b2",
          "L1_ffn_ew", "L1_ffn_act_w", "L1_ffn_We", "L1_ffn_be", "L1_ffn_Wq", "L1_ffn_Wk", "L1_ffn_Wv",
          "L1_ffn_Wo", "L1_ffn_ln_g", "L1_ffn_ln_b"]


def lay_out(inputs):
    arrays = {n: np.ascontiguousarray(inputs[n]) for n in _PLAIN}
    arrays["mask_BxS2_bf1"] = np.ascontiguousarray(inputs["mask_BxS2_bf1"]).view(np.uint8)
    b1 = np.asarray(inputs["L0_ffn_b1"])
    arrays["b1_cols"] = np.ascontiguousarray(b1.reshape(b1.shape[0], -1, P).transpose(0, 2, 1))
    for n in ("bq", "bk", "bv", "b1"):
        arrays[f"L1_xattn_{n}_cols"] = np.ascontiguousarray(np.asarray(inputs[f"L1_xattn_{n}"]).reshape(-1, P).T)
    be = np.asarray(inputs["L1_ffn_be"])
    arrays["be_cols"] = np.ascontiguousarray(be.reshape(be.shape[0], -1, P).transpose(2, 1, 0))
    arrays["edgesT"] = np.ascontiguousarray(np.asarray(inputs["L1_ffn_We"]).transpose(0, 2, 1))
    arrays["consts"] = consts_array()
    return arrays


def kernel(**inputs):
    import concourse.bacc as bacc
    from concourse.bass_utils import run_bass_kernel_spmd

    nc = bacc.Bacc("TRN2", target_bir_lowering=False, num_devices=1)
    arrays = {f"in_{n}": a for n, a in lay_out(inputs).items()}
    io = {n[3:]: nc.dram_tensor(n, a.shape, mybir.dt.from_np(a.dtype), kind="ExternalInput").ap()
          for n, a in arrays.items()}
    out = nc.dram_tensor("out", io["x"].shape, F32, kind="ExternalOutput").ap()
    build(nc, io, out)
    return run_bass_kernel_spmd(nc, [arrays], core_ids=[0]).results[0]["out"]
```

```python
from contextlib import ExitStack

import numpy as np

import concourse.bass as bass
from concourse import mybir

F32 = mybir.dt.float32
F32R = mybir.dt.float32r
U8 = mybir.dt.uint8
U32 = mybir.dt.uint32
ALU = mybir.AluOpType
ACT = mybir.ActivationFunctionType
AX = mybir.AxisListType

P = 128
PAIR = 2
STREAMS = 2
ROWS = 4
NEG = 2.0 ** 127


class Tally:

    def __init__(self, turn=0, per=0, base=0):
        self.past, self.n = turn * per + base, 0

    def up(self, k=1):
        self.n += k
        return self.past + self.n

    def now(self):
        return self.past + self.n


def consts_array():
    i = np.arange(P)
    parts = [np.eye(P), i[:, None] <= i[None, :], np.ones((P, P)),
             (i % 32 < 16)[:, None], (i % 32 >= 16)[:, None],
             np.broadcast_to(np.arange(8), (P, 8)), np.full((P, 2), -0.5),
             np.full((P, 2), 1e-5), np.full((P, 2), 1e-6)]
    return np.concatenate([np.asarray(a, np.float32) for a in parts], 1)


C_ID, C_TRI, C_ONE, C_EVEN, C_ODD, C_IOTA, C_HALF, C_EPS5, C_EPS6, C_END = \
    0, 128, 256, 384, 385, 386, 394, 396, 398, 400


def phase_first_attention(nc, io, scratch, keep, cst):
    x, ctx, mask = io["x"], io["ctx_768"], io["mask_BxS2_bf1"]
    B, T, D = x.shape
    C = ctx.shape[2]
    C1 = C - P
    TURNS = B // (PAIR * STREAMS)
    E = io["L0_ffn_w_switch"].shape[1]
    W2 = PAIR * T

    def rows(ap, g, p):
        v = ap.rearrange("(g p b) t d -> g p t b d", p=STREAMS, b=PAIR)
        return v[bass.ds(g, 1), p].rearrange("g t b d -> (g t) b d")

    with ExitStack() as es:
        def sb(name, shape, dt=F32):
            return es.enter_context(nc.sbuf_tensor("a_" + name, [P] + shape, dt))

        def sem(name):
            return es.enter_context(nc.semaphore("a_" + name))

        wq, wk, wv, wo = (sb(n, [2, D]) for n in ("wq", "wk", "wv", "wo"))
        wsw = sb("wsw", [2, E])
        xt = sb("x", [STREAMS, PAIR, D])
        xr = sb("x_residual", [STREAMS, PAIR, D])
        ct = sb("ctx", [STREAMS, PAIR, C])
        mku = sb("mask_u8", [STREAMS, PAIR, T], U8)
        mk = sb("mask_add", [STREAMS, PAIR, T])
        stats = sb("stats", [PAIR, 6])
        after_wait = sb("after_wait", [1])
        mv = sb("mean_var", [STREAMS, PAIR, 2])
        veps = sb("var_eps", [STREAMS, PAIR])
        rstd = sb("rstd", [STREAMS, PAIR])
        xn = sb("xn", [STREAMS, PAIR, D])
        x1 = sb("x1", [STREAMS, PAIR, D])
        xn1 = sb("xn1", [STREAMS, PAIR, D])
        xT = sb("xT", [STREAMS, 2, W2])
        cT = sb("cT", [STREAMS, 2, W2])
        qT = sb("qT", [STREAMS, 2, W2])
        kE = sb("kT_even", [STREAMS, 2, W2])
        kO = sb("kT_odd", [STREAMS, 2, W2])
        vE = sb("v_even", [STREAMS, PAIR, D])
        vO = sb("v_odd", [STREAMS, PAIR, D])
        oT = sb("oT", [2, W2])
        xn1T = sb("xn1T", [2, W2])
        pr = sb("probs", [STREAMS, PAIR, ROWS, 4, T])
        nmax = sb("neg_max", [STREAMS, PAIR, ROWS, 4])
        rsum = sb("row_sum", [STREAMS, PAIR, ROWS, 4])
        rinv = sb("row_inv", [STREAMS, PAIR, ROWS, 4])
        pT = sb("probsT", [PAIR, ROWS, 4, T])
        S = [es.enter_context(nc.psum_tensor(f"a_scores{r}", [P, 4, T], F32)) for r in range(ROWS)]
        TB = [es.enter_context(nc.psum_tensor(f"a_turned{r}", [P, 4, T], F32)) for r in range(2)]
        M = [es.enter_context(nc.psum_tensor(f"a_product{r}", [P, 2, W2], F32)) for r in range(2)]

        w_in = sem("weights_in")
        x_in = [sem(f"x_in{p}") for p in range(STREAMS)]
        c_in = [sem(f"ctx_in{p}") for p in range(STREAMS)]
        mask_in = [sem(f"mask_in{p}") for p in range(STREAMS)]
        x_used, c_used, mask_used = sem("x_used"), sem("ctx_used"), sem("mask_used")
        x1_out = [sem(f"x1_out{p}") for p in range(STREAMS)]
        xn1_out = [sem(f"xn1_out{p}") for p in range(STREAMS)]
        x1_made, xn1_made = sem("x1_made"), sem("xn1_made")
        zeroed = sem("v_zeroed")
        kept = sem("x_kept")
        vstep = sem("vector_step")
        var_made, veps_made, rstd_made = sem("var_made"), sem("veps_made"), sem("rstd_made")
        xn_made = sem("xn_made")
        prod, prod_used = sem("product_made"), sem("product_used")
        sco, sco_used = sem("scores_made"), sem("scores_used")
        max_made, exp_made, inv_made, norm_made = sem("max_made"), sem("exp_made"), sem("inv_made"), sem("norm_made")
        turned, pT_made = sem("turned_made"), sem("pT_made")

        FRONT, BACK = 5, 4
        PRODS = STREAMS * (FRONT + BACK)
        SLOTS = PAIR * ROWS

        def all_steps(eng, run):
            run(0, 0, [((0, 0), None, (0, 1))])
            with eng.Fori(0, TURNS - 1) as g:
                run(g, 1, [((g, 1), (g, 0), (g + 1, 0)), ((g + 1, 0), (g, 1), (g + 1, 1))])
            last = TURNS - 1
            run(last, 1, [((last, 1), (last, 0), None), (None, (last, 1), None)])

        block = es.enter_context(nc.Block())

        @block.sync
        def _(sp):
            for n, t in (("Wq", wq), ("Wo", wo)):
                sp.dma_start(t[:], io["L0_xattn_" + n].rearrange("(c p) n -> p c n", p=P)).then_inc(w_in, 16)
            for n, t in (("Wk", wk), ("Wv", wv)):
                w = io["L0_xattn_" + n]
                sp.dma_start(t[:, 0], w[0:P]).then_inc(w_in, 16)
                sp.dma_start(t[0:C1, 1], w[P:C]).then_inc(w_in, 16)
            sp.dma_start(wsw[:], io["L0_ffn_w_switch"].rearrange("(c p) n -> p c n", p=P)).then_inc(w_in, 16)
            with sp.Fori(0, TURNS) as g:
                for p in range(STREAMS):
                    sp.wait_ge(x_used, g * STREAMS + p + 1)
                    sp.dma_start(xt[:, p], rows(x, g, p)).then_inc(x_in[p], 16)
                    sp.wait_ge(mask_used, g * STREAMS + p + 1)
                    sp.wait_ge(c_used, g * STREAMS + p + 1)
                    sp.dma_start(ct[:, p], rows(ctx, g, p)).then_inc(c_in[p], 16)
                    m = mask.rearrange("(g p b) t -> g p (b t)", p=STREAMS, b=PAIR)
                    m = m[bass.ds(g, 1), p].rearrange("g n -> (g n)").partition_broadcast(P)
                    sp.dma_start(mku[:, p].rearrange("q b t -> q (b t)"), m).then_inc(mask_in[p], 16)

        @block.scalar
        def _(act):
            def keep_x(k, p):
                act.wait_ge(x_in[p], k * 16 + 16)
                nc.scalar.copy(xr[:, p], xt[:, p]).then_inc(kept, 1)

            def run(g, started, steps):
                t_xn = Tally(g, STREAMS, 1 + started)
                t_max = Tally(g, STREAMS * SLOTS, started * SLOTS)
                t_turn, t_out = Tally(g, STREAMS * SLOTS), Tally(g, STREAMS)
                for front, back, ahead in steps:
                    if back:
                        for b in range(PAIR):
                            for r in range(ROWS):
                                act.wait_ge(turned, t_turn.up())
                                nc.scalar.copy(pT[:, b, r], TB[r % 2][:]).then_inc(pT_made, 1)
                    if front:
                        p = front[1]
                        for b in range(PAIR):
                            for r in range(ROWS):
                                act.wait_ge(max_made, t_max.up())
                                for j in range(4):
                                    e = pr[:, p, b, r, j]
                                    i = nc.scalar.activation(e, e, ACT.Exp, bias=nmax[:, p, b, r, j:j + 1],
                                                             accum_out=rsum[:, p, b, r, j:j + 1])
                                i.then_inc(exp_made, 1)
                    if back:
                        k, p = back
                        n = t_out.up()
                        act.wait_ge(x1_made, n)
                        act.dma_start(rows(scratch["x1"], k, p), x1[:, p]).then_inc(x1_out[p], 16)
                        act.wait_ge(xn1_made, n)
                        act.dma_start(rows(scratch["xn1"], k, p), xn1[:, p]).then_inc(xn1_out[p], 16)
                    if ahead:
                        keep_x(*ahead)
                        n = t_xn.up()
                        act.wait_ge(kept, n)
                        act.wait_ge(xn_made, n)
                        act.sem_inc(x_used, 1)

            keep_x(0, 0)
            act.wait_ge(kept, 1)
            act.wait_ge(xn_made, 1)
            act.sem_inc(x_used, 1)
            all_steps(act, run)
            for p in range(STREAMS):
                act.wait_ge(x1_out[p], 16 * TURNS + 16)
                act.wait_ge(xn1_out[p], 16 * TURNS + 16)

        @block.gpsimd
        def _(pool):
            nc.gpsimd.memset(vE[:], 0.0).then_inc(zeroed, 1)
            nc.gpsimd.memset(vO[:], 0.0).then_inc(zeroed, 1)

            def rsqrt(p, n):
                pool.wait_ge(var_made, n)
                nc.gpsimd.tensor_tensor(veps[:, p], mv[:, p, :, 1], cst[:, C_EPS5:C_EPS5 + 2], ALU.add).then_inc(veps_made, 1)
                pool.wait_ge(veps_made, n)
                nc.gpsimd.tensor_tensor(rstd[:, p], veps[:, p], cst[:, C_HALF:C_HALF + 2], ALU.pow).then_inc(rstd_made, 1)

            def run(g, started, steps):
                t_inv = Tally(g, STREAMS * SLOTS, started * (SLOTS - 2))
                t_var = Tally(g, STREAMS * 2, 1 + started)

                def normalise(p, b, strips):
                    for r in strips:
                        pool.wait_ge(inv_made, t_inv.up())
                        e = pr[:, p, b, r]
                        nc.gpsimd.tensor_tensor(e, e, rinv[:, p, b, r].unsqueeze(2).broadcast_to([P, 4, T]),
                                                ALU.mult).then_inc(norm_made, 1)

                for front, back, ahead in steps:
                    if back:
                        normalise(back[1], 1, (2, 3))
                    if ahead:
                        rsqrt(ahead[1], t_var.up())
                    if back:
                        rsqrt(back[1], t_var.up())
                    if front:
                        normalise(front[1], 0, range(ROWS))
                        normalise(front[1], 1, (0, 1))

            rsqrt(0, 1)
            all_steps(pool, run)

        @block.vector
        def _(dve):
            for s, k in ((x_used, STREAMS), (c_used, STREAMS), (mask_used, STREAMS), (prod_used, 2),
                         (sco_used, ROWS), (pT_made, 2), *((m, 16) for m in x1_out + xn1_out)):
                dve.sem_inc(s, k)
            dve.wait_ge(zeroed, 2)

            def moments(src, p, n):
                for b in range(PAIR):
                    i = nc.vector.bn_stats(stats[:, b], src[:, b])
                i.then_inc(vstep, 1)
                dve.wait_ge(vstep, n)
                nc.vector.memset(after_wait[:], 0.0)
                for b in range(PAIR):
                    i = nc.vector.bn_aggr(mv[:, p, b], stats[:, b])
                i.then_inc(var_made, 1)

            def normal(src, dst, p, n, made):
                dve.wait_ge(rstd_made, n)
                for b in range(PAIR):
                    i = nc.vector.tensor_scalar(dst[:, b], src[:, b], mv[:, p, b, 0:1], rstd[:, p, b:b + 1],
                                                ALU.subtract, ALU.mult)
                i.then_inc(made, 1)

            def run(g, started, steps):
                t_step = Tally(g, STREAMS * 3, 1 + 2 * started)
                t_rstd, t_kept = Tally(g, STREAMS * 2, 1 + started), Tally(g, STREAMS)
                t_exp = Tally(g, STREAMS * SLOTS, started * (SLOTS - 2))
                t_prod, t_sco = Tally(g, PRODS, started * FRONT), Tally(g, STREAMS * SLOTS, started * SLOTS)

                def product():
                    dve.wait_ge(prod, t_prod.up())
                    return M[(started * FRONT + t_prod.n - 1) % 2]

                def masked(p, b, strips):
                    for r in strips:
                        dve.wait_ge(sco, t_sco.up())
                        nc.vector.tensor_tensor(pr[:, p, b, r], S[r][:],
                                                mk[:, p, b].unsqueeze(1).broadcast_to([P, 4, T]),
                                                ALU.add).then_inc(sco_used, 1)
                        dve.wait_ge(sco_used, ROWS + t_sco.now())
                        nc.vector.tensor_reduce(nmax[:, p, b, r], pr[:, p, b, r], AX.X, ALU.max,
                                                negate=True).then_inc(max_made, 1)

                def inverse(p, b, r):
                    dve.wait_ge(exp_made, t_exp.up())
                    nc.vector.reciprocal(rinv[:, p, b, r], rsum[:, p, b, r]).then_inc(inv_made, 1)

                for front, back, ahead in steps:
                    if front:
                        k, p = front
                        m = product()
                        nc.vector.tensor_copy(xT[:, p], m[:]).then_inc(prod_used, 1)
                    if back:
                        k1, p1 = back
                        inverse(p1, 1, 2)
                    if front:
                        m = product()
                        nc.vector.tensor_copy(cT[:, p, 0], m[:, 0])
                        nc.vector.tensor_copy(cT[0:C1, p, 1], m[0:C1, 1]).then_inc(prod_used, 1)
                    if back:
                        inverse(p1, 1, 3)
                    if front:
                        dve.wait_ge(mask_in[p], k * 16 + 16)
                        nc.vector.tensor_scalar(mk[:, p], mku[:, p], 1.0, NEG, ALU.subtract, ALU.mult).then_inc(vstep, 1)
                        n_mask = t_step.up()
                    if ahead:
                        k2, p2 = ahead
                        dve.wait_ge(x_in[p2], k2 * 16 + 16)
                        moments(xt[:, p2], p2, t_step.up())
                    if front:
                        m = product()
                        nc.vector.tensor_scalar(qT[:, p], m[:], 0.25, None, ALU.mult).then_inc(prod_used, 1)
                    if ahead:
                        normal(xt[:, p2], xn[:, p2], p2, t_rstd.up(), xn_made)
                    if front:
                        m = product()
                        nc.vector.tensor_scalar(kE[:, p], m[:], cst[:, C_EVEN:C_EVEN + 1], None, ALU.mult)
                        nc.vector.tensor_scalar(kO[:, p], m[:], cst[:, C_ODD:C_ODD + 1], None, ALU.mult).then_inc(prod_used, 1)
                        dve.wait_ge(vstep, n_mask)
                        dve.sem_inc(mask_used, 1)
                    if back:
                        m = product()
                        nc.vector.tensor_copy(oT[:], m[:]).then_inc(prod_used, 1)
                    if front:
                        masked(p, 0, range(ROWS))
                    if back:
                        m = product()
                        dve.wait_ge(x1_out[p1], k1 * 16 + 16)
                        dve.wait_ge(kept, t_kept.up())
                        nc.vector.tensor_tensor(x1[:, p1], m[:], xr[:, p1], ALU.add).then_inc(prod_used, 1)
                        dve.wait_ge(prod_used, 2 + t_prod.now())
                        dve.sem_inc(x1_made, 1)
                        moments(x1[:, p1], p1, t_step.up())
                    if front:
                        m = product()
                        for v, o in ((vE, 0), (vO, 16)):
                            i = nc.vector.tensor_copy(
                                v[:, p].rearrange("t b (h f) -> t (b h) f", f=32)[:, :, o:o + 16],
                                m[:].rearrange("t b (h f) -> t (b h) f", f=32)[:, :, o:o + 16])
                        i.then_inc(prod_used, 1)
                    if back:
                        dve.wait_ge(xn1_out[p1], k1 * 16 + 16)
                        normal(x1[:, p1], xn1[:, p1], p1, t_rstd.up(), xn1_made)
                    if front:
                        masked(p, 1, (0,))
                        inverse(p, 0, 0)
                        masked(p, 1, (1,))
                        inverse(p, 0, 1)
                    if back:
                        m = product()
                        nc.vector.tensor_copy(xn1T[:], m[:]).then_inc(prod_used, 1)
                    if front:
                        masked(p, 1, (2,))
                        inverse(p, 0, 2)
                    if back:
                        m = product()
                        nc.vector.tensor_copy(keep["logits"][:, bass.ds(k1 * 4 + p1 * 2, 2)],
                                              m[:, :, 0:E]).then_inc(prod_used, 1)
                    if front:
                        masked(p, 1, (3,))
                        inverse(p, 0, 3)
                        inverse(p, 1, 0)
                        inverse(p, 1, 1)

            dve.wait_ge(x_in[0], 16)
            moments(xt[:, 0], 0, 1)
            normal(xt[:, 0], xn[:, 0], 0, 1, xn_made)
            all_steps(dve, run)

        @block.tensor
        def _(pe):
            ident = cst[:, C_ID:C_ID + P]
            pe.wait_ge(w_in, 16 * 7)

            def run(g, started, steps):
                t_prod, t_xn = Tally(g, PRODS, started * FRONT), Tally(g, STREAMS, started)
                t_sfree = Tally(g, STREAMS * SLOTS, started * SLOTS)
                t_norm, t_pt, t_out = Tally(g, STREAMS * SLOTS), Tally(g, STREAMS * SLOTS), Tally(g, STREAMS)

                def bank():
                    pe.wait_ge(prod_used, t_prod.up())
                    return M[(started * FRONT + t_prod.n - 1) % 2]

                def out_of_bank(n):
                    pe.wait_ge(prod_used, 2 + n)

                def turn_rows(src):
                    dst = bank()
                    for b in range(PAIR):
                        for u in range(2):
                            w = min(P, src.shape[2] - u * P)
                            i = nc.tensor.transpose(dst[0:w, u, b * T:(b + 1) * T], src[:, b, u * P:u * P + w], ident)
                    i.then_inc(prod, 1)
                    return t_prod.now()

                def project(w, src, K1=P):
                    m = bank()
                    for u in range(2):
                        nc.tensor.matmul(m[:, u], w[:, 0, u * P:(u + 1) * P], src[:, 0], start=True, stop=False)
                        i = nc.tensor.matmul(m[:, u], w[0:K1, 1, u * P:(u + 1) * P], src[0:K1, 1], start=False, stop=True)
                    i.then_inc(prod, 1)
                    return t_prod.now()

                def project_rows(w, src, K1=P):
                    m = bank()
                    for b in range(PAIR):
                        n = w.shape[2]
                        nc.tensor.matmul(m[:, b, 0:n], src[:, 0, b * T:(b + 1) * T], w[:, 0], start=True, stop=False)
                        i = nc.tensor.matmul(m[:, b, 0:n], src[0:K1, 1, b * T:(b + 1) * T], w[0:K1, 1], start=False, stop=True)
                    i.then_inc(prod, 1)
                    return t_prod.now()

                def scores(p, b):
                    for j in range(4):
                        u, k = j // 2, (kE, kO)[j % 2]
                        for r in range(ROWS):
                            if j == 0:
                                pe.wait_ge(sco_used, t_sfree.up())
                            s = slice(32 * r, 32 * r + 32)
                            i = nc.tensor.matmul(S[r][:, j], qT[s, p, u, b * T:(b + 1) * T],
                                                 k[s, p, u, b * T:(b + 1) * T], start=True, stop=True)
                            if j == 3:
                                i.then_inc(sco, 1)

                def turn_probs(p, b, strips):
                    for r in strips:
                        n = t_norm.up()
                        pe.wait_ge(norm_made, n)
                        pe.wait_ge(pT_made, n)
                        for j in range(4):
                            i = nc.tensor.transpose(TB[r % 2][:, j], pr[:, p, b, r, j], ident)
                        i.then_inc(turned, 1)

                def attend(p):
                    m = bank()
                    for b in range(PAIR):
                        pe.wait_ge(pT_made, 2 + t_pt.up(ROWS))
                        for j in range(4):
                            u, v = j // 2, (vE, vO)[j % 2]
                            for r in range(ROWS):
                                h = 32 * (4 * u + r)
                                i = nc.tensor.matmul(m[32 * r:32 * r + 32, u, b * T:(b + 1) * T],
                                                     v[:, p, b, h:h + 32], pT[:, b, r, j],
                                                     start=j % 2 == 0, stop=j % 2 == 1)
                    i.then_inc(prod, 1)
                    return t_prod.now()

                for front, back, _ in steps:
                    if front:
                        k, p = front
                        pe.wait_ge(xn_made, t_xn.up())
                        n_x = turn_rows(xn[:, p])
                        pe.wait_ge(c_in[p], k * 16 + 16)
                        n_c = turn_rows(ct[:, p])
                    if back:
                        turn_probs(back[1], 0, (0, 1))
                    if front:
                        out_of_bank(n_x)
                        project(wq, xT[:, p])
                    if back:
                        turn_probs(back[1], 0, (2, 3))
                    if front:
                        out_of_bank(n_c)
                        pe.sem_inc(c_used, 1)
                        n_k = project(wk, cT[:, p], C1)
                    if back:
                        turn_probs(back[1], 1, range(ROWS))
                        n_o = attend(back[1])
                    if front:
                        out_of_bank(n_k)
                        scores(p, 0)
                    if back:
                        out_of_bank(n_o)
                        project_rows(wo, oT)
                    if front:
                        n_v = project_rows(wv, cT[:, p], C1)
                        scores(p, 1)
                    if back:
                        pe.wait_ge(xn1_made, t_out.up())
                        n_x1 = turn_rows(xn1[:, back[1]])
                        out_of_bank(n_x1)
                        project_rows(wsw, xn1T)
                    elif front:
                        out_of_bank(n_v)

            all_steps(pe, run)

CAP_FACTOR = 0.5
OUT_OF_BOUNDS = 65536.0


def phase_route(nc, io, scratch, keep, cst):
    NT, T, D = io["x"].shape
    E = io["L0_ffn_b_switch"].shape[0]
    CAP = int(CAP_FACTOR * NT * T / E)
    LOADS = 4
    HALVES = 2
    TURNS = NT // (LOADS * HALVES)
    buf = scratch["buf"]

    with ExitStack() as es:
        def sb(name, shape, dt=F32):
            return es.enter_context(nc.sbuf_tensor("r_" + name, [P] + shape, dt))

        def sem(name):
            return es.enter_context(nc.semaphore("r_" + name))

        bsw = sb("b_switch", [E])
        lg, e, pb = keep["logits"], sb("exp", [NT, E]), sb("probs", [NT, E])
        oh = sb("one_hot", [NT, E])
        i8 = sb("iota_less_E", [E])
        tot = sb("tile_totals", [NT, E])
        run = [sb(f"running{n}", [NT, E]) for n in range(2)]
        mx, sm, pm, route, pos, kept, slot = (sb(n, [NT]) for n in ("mx", "sm", "pm", "route", "pos", "kept", "slotf"))
        zero = sb("zero", [2048])
        rows = sb("rows", [HALVES, LOADS, D])
        idx = sb("idx", [HALVES, LOADS], U32)
        after_wait = sb("after_wait", [1])
        cum = es.enter_context(nc.psum_tensor("r_cum", [P, NT, E], F32))
        all_ = es.enter_context(nc.psum_tensor("r_all", [P, NT, E], F32))

        b_in, zero_made, zeroed, pad_made = sem("b_in"), sem("zero_made"), sem("buf_zeroed"), sem("pad_made")
        step = sem("vector_step")
        shifted, exped, hot, counted = sem("shifted"), sem("exped"), sem("one_hot"), sem("counted")
        slots_made = sem("slots_made")
        rows_in = [sem(f"rows_in{h}") for h in range(HALVES)]
        sent = [sem(f"sent{h}") for h in range(HALVES)]
        idx_made, rows_free = sem("idx_made"), sem("rows_free")
        block = es.enter_context(nc.Block())

        @block.vector
        def _(dve):
            t = Tally()

            def chain(i):
                i.then_inc(step, 1)
                dve.wait_ge(step, t.up())

            def over_e(a):
                return a.unsqueeze(2).broadcast_to([P, NT, E])

            def over_t(a):
                return a.unsqueeze(1).broadcast_to([P, NT, E])

            V = nc.vector
            V.memset(zero[:], 0.0).then_inc(zero_made, 1)
            V.memset(keep["gate"][:, NT:], 0.0)
            V.memset(keep["slots"][:, NT:], 0)
            chain(V.tensor_scalar(i8[:], cst[:, C_IOTA:C_IOTA + E], float(E), None, ALU.subtract))
            dve.wait_ge(b_in, 16)
            chain(V.tensor_tensor(e[:], lg[:], over_t(bsw[:]), ALU.add))
            chain(V.tensor_reduce(mx[:], e[:], AX.X, ALU.max))
            V.tensor_tensor(pb[:], e[:], over_e(mx[:]), ALU.subtract).then_inc(shifted, 1)
            dve.wait_ge(exped, 1)
            chain(V.tensor_reduce(sm[:], e[:], AX.X, ALU.add))
            chain(V.reciprocal(mx[:], sm[:]))
            chain(V.tensor_tensor(pb[:], e[:], over_e(mx[:]), ALU.mult))
            chain(V.tensor_reduce(pm[:], pb[:], AX.X, ALU.max))
            chain(V.reciprocal(mx[:], pm[:]))
            V.tensor_tensor(keep["gate"][:, 0:NT], pm[:], mx[:], ALU.mult)
            chain(V.tensor_tensor(oh[:], pb[:], over_e(pm[:]), ALU.is_equal))
            chain(V.tensor_tensor(e[:], oh[:], over_t(i8[:]), ALU.mult))
            chain(V.tensor_reduce(route[:], e[:], AX.X, ALU.min))
            V.tensor_tensor(oh[:], over_t(i8[:]), over_e(route[:]), ALU.is_equal).then_inc(hot, 1)
            dve.wait_ge(counted, 1)
            chain(V.tensor_copy(tot[:], all_[:]))
            src, n, s = tot, 0, 1
            while s < NT:
                dst = run[n % 2]
                V.tensor_copy(dst[:, 0:s], src[:, 0:s])
                chain(V.tensor_tensor(dst[:, s:NT], src[:, s:NT], src[:, 0:NT - s], ALU.add))
                src, n, s = dst, n + 1, s * 2
            chain(V.tensor_tensor(e[:], src[:], tot[:], ALU.subtract))
            chain(V.tensor_tensor(pb[:], e[:], cum[:], ALU.add))
            chain(V.tensor_tensor(e[:], pb[:], oh[:], ALU.mult))
            chain(V.tensor_reduce(pos[:], e[:], AX.X, ALU.add))
            chain(V.tensor_scalar(kept[:], pos[:], float(CAP), OUT_OF_BOUNDS, ALU.is_gt, ALU.mult))
            chain(V.tensor_scalar(route[:], route[:], float(CAP), float(E * CAP - 1), ALU.mult, ALU.add))
            chain(V.tensor_tensor(slot[:], route[:], pos[:], ALU.add))
            V.tensor_tensor(keep["slots"][:, 0:NT], slot[:], kept[:], ALU.add).then_inc(slots_made, 1)

        @block.scalar
        def _(act):
            act.wait_ge(shifted, 1)
            nc.scalar.activation(e[:], pb[:], ACT.Exp).then_inc(exped, 1)

        @block.tensor
        def _(pe):
            pe.wait_ge(hot, 1)
            nc.tensor.matmul(cum[:], cst[:, C_TRI:C_TRI + P], oh[:], start=True, stop=True)
            nc.tensor.matmul(all_[:], cst[:, C_ONE:C_ONE + P], oh[:], start=True, stop=True).then_inc(counted, 1)

        @block.sync
        def _(sp):
            sp.dma_start(bsw[:], io["L0_ffn_b_switch"].partition_broadcast(P)).then_inc(b_in, 16)
            sp.wait_ge(zero_made, 1)
            parts = buf.rearrange("(n p r) d -> n p (r d)", p=P, r=2048 // D)
            for n in range(parts.shape[0]):
                sp.dma_start(parts[n], zero[:]).then_inc(zeroed, 16)
            src = scratch["xn1"][0:NT].rearrange("(g h n) t d -> g h t n d", h=HALVES, n=LOADS)
            pad = scratch["xn1"].shape[0] - NT
            for n in ("x1", "xn1"):
                spare = scratch[n][NT:NT + pad].rearrange("n t d -> (n t d)").rearrange("(p r) -> p r", p=P)
                sp.dma_start(spare, zero[:, 0:pad * T * D // P]).then_inc(pad_made, 16)
            sp.wait_ge(pad_made, 32)
            with sp.Fori(0, TURNS) as g:
                for h in range(HALVES):
                    sp.wait_ge(rows_free, g * HALVES + h + 1)
                    sp.dma_start(rows[:, h], src[bass.ds(g, 1), h].rearrange("g t n d -> (g t) n d")).then_inc(rows_in[h], 16)

        @block.gpsimd
        def _(pool):
            last_slot = pool.to_reg(E * CAP - 1)
            pool.sem_inc(rows_free, HALVES)
            pool.wait_ge(slots_made, 1)
            pool.wait_ge(zeroed, 16 * (E * CAP * D // (2048 * P)))
            with pool.Fori(0, TURNS) as g:
                for h in range(HALVES):
                    nc.gpsimd.tensor_copy(idx[:, h], keep["slots"][:, bass.ds((g * HALVES + h) * LOADS, LOADS)]).then_inc(idx_made, 1)
                    pool.wait_ge(idx_made, g * HALVES + h + 1)
                    pool.wait_ge(rows_in[h], g * 16 + 16)
                    nc.gpsimd.tensor_tensor(after_wait[:], cst[:, 0:1], cst[:, 0:1], ALU.add)
                    for n in range(LOADS):
                        nc.gpsimd.indirect_dma_start(
                            out=buf, out_offset=bass.IndirectOffsetOnAxis(ap=idx[:, h, n:n + 1], axis=0),
                            in_=rows[:, h, n], in_offset=None, bounds_check=last_slot, oob_is_err=False,
                        ).then_inc(sent[h], 16)
                for h in range(HALVES):
                    pool.wait_ge(sent[h], (g + 1) * 16 * LOADS)
                    pool.sem_inc(rows_free, 1)


def phase_experts(nc, io, scratch, cst):
    w1, w2, b2 = io["L0_ffn_w1"], io["L0_ffn_w2"], io["L0_ffn_b2"]
    E, D, H = w1.shape
    CAP = scratch["buf"].shape[0] // E
    NR = CAP // P
    HC = H // P
    SIDES = 2
    TURNS = E // SIDES
    YB = NR // 2

    with ExitStack() as es:
        def sb(name, shape, dt=F32):
            return es.enter_context(nc.sbuf_tensor("e_" + name, [P] + shape, dt))

        def sem(name):
            return es.enter_context(nc.semaphore("e_" + name))

        w1t = sb("w1", [SIDES, 2, H])
        w2t = sb("w2", [SIDES, HC, D])
        b1t = sb("b1", [SIDES, HC])
        b2t = sb("b2", [SIDES, D])
        xr = sb("rows", [SIDES, NR, D])
        xT = sb("rowsT", [2, CAP])
        hT = sb("hidden", [HC, CAP])
        y = sb("y", [YB, 2, D])
        TB = [es.enter_context(nc.psum_tensor(f"e_turned{r}", [P, CAP], F32)) for r in range(2)]
        HB = [es.enter_context(nc.psum_tensor(f"e_hidden{r}", [P, CAP], F32)) for r in range(4)]
        Y = [es.enter_context(nc.psum_tensor(f"e_out{r}", [P, 2, D], F32)) for r in range(2)]
        got = [sem(f"loaded{s}") for s in range(SIDES)]
        turned, xT_made, done = sem("turned"), sem("xT_made"), sem("expert_done")
        hid, hid_made = sem("hidden"), sem("hidden_made")
        out, y_made = sem("out"), sem("y_made")
        y_out = [sem(f"y_out{i}") for i in range(2)]
        block = es.enter_context(nc.Block())

        def of(ap, g, s):
            v = ap.rearrange("(g s) a n -> g s a n", s=SIDES)[bass.ds(g, 1), s]
            return v.rearrange("g (c p) n -> p (g c) n", p=P)

        @block.sync
        def _(sp):
            buf = scratch["buf"].rearrange("(e r) d -> e r d", e=E)
            with sp.Fori(0, TURNS) as g:
                for s in range(SIDES):
                    sp.wait_ge(done, g * SIDES + s + 1)
                    sp.dma_start(xr[:, s], of(buf, g, s)).then_inc(got[s], 16)
                    sp.dma_start(w1t[:, s], of(w1, g, s)).then_inc(got[s], 16)
                    sp.dma_start(w2t[:, s], of(w2, g, s)).then_inc(got[s], 16)
                    b1 = io["b1_cols"].rearrange("(g s) p c -> g s p c", s=SIDES)[bass.ds(g, 1), s]
                    sp.dma_start(b1t[:, s], b1.rearrange("g p c -> (g p) c")).then_inc(got[s], 16)
                    b = b2.rearrange("(g s) n -> g s n", s=SIDES)[bass.ds(g, 1), s]
                    sp.dma_start(b2t[:, s], b.rearrange("g n -> (g n)").partition_broadcast(P)).then_inc(got[s], 16)

        @block.tensor
        def _(pe):
            with pe.Fori(0, TURNS) as g:
                t_x, t_h, t_y = Tally(g, 2 * SIDES), Tally(g, HC * SIDES), Tally(g, YB * SIDES)
                for s in range(SIDES):
                    pe.wait_ge(got[s], g * 80 + 80)
                    for u in range(2):
                        pe.wait_ge(xT_made, t_x.up())
                        for n in range(NR):
                            i = nc.tensor.transpose(TB[u][:, n * P:(n + 1) * P], xr[:, s, n, u * P:(u + 1) * P],
                                                    cst[:, C_ID:C_ID + P])
                        i.then_inc(turned, 1)
                    pe.wait_ge(xT_made, 2 + t_x.now())
                    for c in range(HC):
                        pe.wait_ge(hid_made, t_h.up())
                        b = HB[c % 4]
                        for u in range(2):
                            i = nc.tensor.matmul(b[:], w1t[:, s, u, c * P:(c + 1) * P], xT[:, u], start=u == 0, stop=u == 1)
                        i.then_inc(hid, 1)
                    for q in range(YB):
                        pe.wait_ge(y_made, t_y.up())
                        for n in range(2):
                            r = (2 * q + n) * P
                            for c in range(HC):
                                if q == 0 and n == 0:
                                    pe.wait_ge(hid_made, 4 + t_h.now() - HC + c + 1)
                                i = nc.tensor.matmul(Y[q % 2][:, n], hT[:, c, r:r + P], w2t[:, s, c],
                                                     start=c == 0, stop=c == HC - 1)
                        i.then_inc(out, 1)

        @block.scalar
        def _(act):
            with act.Fori(0, TURNS) as g:
                t_h, t_y = Tally(g, HC * SIDES), Tally(g, YB * SIDES, YB)
                for s in range(SIDES):
                    act.wait_ge(got[s], g * 80 + 80)
                    for c in range(HC):
                        act.wait_ge(hid, t_h.up())
                        nc.scalar.activation(hT[:, c], HB[c % 4][:], ACT.Relu,
                                             bias=b1t[:, s, c:c + 1]).then_inc(hid_made, 1)
                    dst = scratch["y"].rearrange("(g s q n p) d -> g s q p n d", s=SIDES, q=YB, n=2, p=P)
                    for q in range(YB):
                        act.wait_ge(y_made, t_y.up())
                        act.dma_start(dst[bass.ds(g, 1), s, q].rearrange("g p n d -> (g p) n d"), y[:, q]).then_inc(y_out[q], 16)
            for q in range(YB):
                act.wait_ge(y_out[q], 16 * E + 16)

        @block.vector
        def _(dve):
            for m, k in ((xT_made, 2), (hid_made, 4), (y_made, YB), (done, SIDES), *((m, 16) for m in y_out)):
                dve.sem_inc(m, k)
            with dve.Fori(0, TURNS) as g:
                t_x, t_y = Tally(g, 2 * SIDES), Tally(g, YB * SIDES)
                for s in range(SIDES):
                    for u in range(2):
                        dve.wait_ge(turned, t_x.up())
                        nc.vector.tensor_copy(xT[:, u], TB[u][:]).then_inc(xT_made, 1)
                    dve.wait_ge(got[s], g * 80 + 80)
                    for q in range(YB):
                        dve.wait_ge(out, t_y.up())
                        dve.wait_ge(y_out[q], (g * SIDES + s + 1) * 16)
                        nc.vector.tensor_tensor(y[:, q], Y[q][:], b2t[:, s].unsqueeze(1).broadcast_to([P, 2, D]),
                                                ALU.add).then_inc(y_made, 1)
                    dve.wait_ge(y_made, YB + t_y.now())
                    dve.sem_inc(done, 1)



NODES, MAX_PREV, CELL_HEADS = 6, 5, 8
KINDS = 5
TO_Q, TO_K, TO_V, EDGE, OUT = range(KINDS)


def cell_plan():
    plan, at = [], 0
    for c in range(NODES):
        n = min(c + 1, MAX_PREV)
        plan.append(dict(edge=(at + n - 1, at, at + n // 2), src=(c - 1, c - n, c - n + n // 2)))
        at += n
    return plan


def phase_fuse(nc, io, fw, fb, row5, cst):
    plan = cell_plan()
    D = io["L1_ffn_Wq"].shape[1]
    SCALE = 1.0 / np.sqrt(D // CELL_HEADS)
    NE = io["L1_ffn_We"].shape[0]
    RING = 3
    jobs = [(c, k) for c in range(NODES) for k in (TO_Q, TO_K, TO_V)]
    W = [io["L1_ffn_" + n] for n in ("Wq", "Wk", "Wv")]

    with ExitStack() as es:
        def sb(name, shape, dt=F32):
            return es.enter_context(nc.sbuf_tensor("f_" + name, [P] + shape, dt))

        def sem(name):
            return es.enter_context(nc.semaphore("f_" + name))

        weT = sb("edgeT", [RING, 2, D])
        w = sb("w", [RING, 2, D])
        ew = sb("ew", [NODES, 3])
        aw = sb("act_w", [NODES])
        be = sb("be", [2, NE])
        M = [es.enter_context(nc.psum_tensor(f"f_product{r}", [P, 2, D], F32)) for r in range(2)]
        MB = es.enter_context(nc.psum_tensor("f_biases", [P, NODES, 3, 2], F32))
        small_in, plain_in = sem("small_in"), sem("plain_in")
        job_in = [sem(f"job_in{r}") for r in range(RING)]
        made, used, bias_made = sem("made"), sem("used"), sem("bias_made")
        block = es.enter_context(nc.Block())

        def halves(a):
            return a.rearrange("(c p) n -> p c n", p=P)

        @block.sync
        def _(sp):
            sp.dma_start(ew[:], io["L1_ffn_ew"].rearrange("c k -> (c k)").partition_broadcast(P)
                         .rearrange("p (c k) -> p c k", k=3)).then_inc(small_in, 16)
            sp.dma_start(aw[:], io["L1_ffn_act_w"].partition_broadcast(P)).then_inc(small_in, 16)
            sp.dma_start(be[:], io["be_cols"]).then_inc(small_in, 16)
            last = plan[-1]["edge"][0]
            sp.dma_start(row5[:], io["L1_ffn_be"][last].partition_broadcast(P)).then_inc(small_in, 16)
            for n, (c, k) in enumerate(jobs):
                if n >= RING:
                    sp.wait_ge(made, n - RING + 1)
                sp.dma_start(weT[:, n % RING], halves(io["edgesT"][plan[c]["edge"][k]])).then_inc(job_in[n % RING], 16)
                sp.dma_start(w[:, n % RING], halves(W[k][c])).then_inc(job_in[n % RING], 16)

        @block.scalar
        def _(act):
            for c in range(NODES):
                act.dma_start(fw[:, c, EDGE], halves(io["L1_ffn_We"][plan[c]["edge"][0]])).then_inc(plain_in, 16)
                act.dma_start(fw[:, c, OUT], halves(io["L1_ffn_Wo"][c])).then_inc(plain_in, 16)

        @block.tensor
        def _(pe):
            pe.wait_ge(small_in, 64)
            for n, (c, k) in enumerate(jobs):
                pe.wait_ge(job_in[n % RING], 32 * (n // RING + 1))
                if n >= 2:
                    pe.wait_ge(used, n - 1)
                e = plan[c]["edge"][k]
                for o in range(2):
                    for h in range(2):
                        nc.tensor.matmul(MB[:, c, k, o:o + 1], w[:, n % RING, h, o * P:(o + 1) * P],
                                         be[:, h, e:e + 1], start=h == 0, stop=h == 1)
                for u in range(2):
                    for h in range(2):
                        i = nc.tensor.matmul(M[n % 2][:, u], weT[:, n % RING, h, u * P:(u + 1) * P],
                                             w[:, n % RING, h], start=h == 0, stop=h == 1)
                i.then_inc(made, 1)

        @block.vector
        def _(dve):
            dve.wait_ge(small_in, 64)
            for n, (c, k) in enumerate(jobs):
                dve.wait_ge(made, n + 1)
                nc.vector.tensor_scalar(fw[:, c, k], M[n % 2][:], ew[:, c, k:k + 1], SCALE if k == TO_Q else 1.0,
                                        ALU.mult, ALU.mult).then_inc(used, 1)
            for c, k in jobs:
                nc.vector.tensor_scalar(fb[:, c, k], MB[:, c, k], ew[:, c, k:k + 1], SCALE if k == TO_Q else 1.0,
                                        ALU.mult, ALU.mult)
            dve.wait_ge(plain_in, 32 * NODES)
            for c in range(NODES):
                q = ew[:, c, TO_Q:TO_Q + 1]
                nc.vector.tensor_scalar(fw[:, c, EDGE], fw[:, c, EDGE], q, None, ALU.mult)
                nc.vector.tensor_scalar(fb[:, c, EDGE], be[:, :, plan[c]["edge"][0]], q, None, ALU.mult)
                nc.vector.tensor_scalar(fw[:, c, OUT], fw[:, c, OUT], aw[:, c:c + 1], None, ALU.mult)
            nc.vector.tensor_scalar(row5[:], row5[:], ew[:, NODES - 1, TO_Q:TO_Q + 1], None, ALU.mult)



def phase_second_layer(nc, io, scratch, keep, fw, fb, row5, cst, out):
    ctx = io["ctx_768"]
    B, T, D = io["x"].shape
    C = ctx.shape[2]
    C1 = C - P
    TURNS = B // (PAIR * STREAMS)
    W2 = PAIR * T
    HID = io["L1_xattn_W1"].shape[1] // P
    plan = cell_plan()
    RT = PAIR * STREAMS
    SLOT_OF = {-1: 0, 0: 1, 1: 2, 2: 3, 3: 0, 4: 1}
    STAGES = NODES + 2

    def rows(ap, g, p):
        v = ap.rearrange("(g p b) t d -> g p t b d", p=STREAMS, b=PAIR)
        return v[bass.ds(g, 1), p].rearrange("g t b d -> (g t) b d")

    with ExitStack() as es:
        def sb(name, shape, dt=F32):
            return es.enter_context(nc.sbuf_tensor("c_" + name, [P] + shape, dt))

        def sem(name):
            return es.enter_context(nc.semaphore("c_" + name))

        wq, wk, wv = (sb(n, [2, D]) for n in ("wq", "wk", "wv"))
        w1, w2 = sb("w1", [2, HID * P]), sb("w2", [HID, D])
        bq, bk, bv, b1 = sb("bq", [2]), sb("bk", [2]), sb("bv", [2]), sb("b1", [HID])
        b2, ln_g, ln_b = sb("b2", [D]), sb("ln_g", [D]), sb("ln_b", [D])
        x2 = sb("x2", [STREAMS, PAIR, D])
        xg = sb("routed", [STREAMS, PAIR, D])
        ct = sb("ctx", [STREAMS, PAIR, C])
        mvf = sb("front_mean_var", [STREAMS, PAIR, 2])
        vepsf = sb("front_var_eps", [STREAMS, PAIR])
        rstdf = sb("front_rstd", [STREAMS, PAIR])
        idx = sb("idx", [STREAMS, PAIR], U32)
        gate = sb("gate", [STREAMS, PAIR])
        x3 = sb("x3", [STREAMS, PAIR, D])
        xn = sb("xn", [STREAMS, PAIR, D])
        fin = sb("fin", [STREAMS, PAIR, D])
        stats = sb("stats", [PAIR, 6])
        after_wait = sb("after_wait", [1])
        after_wait_pool = sb("after_wait_pool", [1])
        mv = sb("mean_var", [STREAMS, PAIR, 2])
        veps = sb("var_eps", [STREAMS, PAIR])
        rstd = sb("rstd", [STREAMS, PAIR])
        nd = sb("nodes", [STREAMS, 4, 2, W2])
        hid = sb("hidden", [STREAMS, HID, W2])
        qT = sb("qT", [STREAMS, 2, W2])
        kT = sb("kT", [STREAMS, 2, W2])
        oT = sb("oT", [STREAMS, 2, W2])
        vE = sb("v_even", [STREAMS, PAIR, D])
        vO = sb("v_odd", [STREAMS, PAIR, D])
        va = sb("v", [STREAMS, PAIR, D])
        pr = sb("probs", [STREAMS, PAIR, ROWS, 4, T])
        nmax = sb("neg_max", [STREAMS, PAIR, ROWS, 4])
        rsum = sb("row_sum", [STREAMS, PAIR, ROWS, 4])
        rinv = sb("row_inv", [STREAMS, PAIR, ROWS, 4])
        pT = sb("probsT", [PAIR, ROWS, 4, T])
        kO = oT
        cT = hid

        S = [es.enter_context(nc.psum_tensor(f"c_scores{r}", [P, 4, T], F32)) for r in range(ROWS)]
        TB = [es.enter_context(nc.psum_tensor(f"c_turned{r}", [P, 4, T], F32)) for r in range(2)]
        M = [es.enter_context(nc.psum_tensor(f"c_product{r}", [P, 2, W2], F32)) for r in range(2)]

        w_in = sem("weights_in")
        x_in = [sem(f"x_in{p}") for p in range(STREAMS)]
        c_in = [sem(f"ctx_in{p}") for p in range(STREAMS)]
        r_in = [sem(f"routed_in{p}") for p in range(STREAMS)]
        gathered = [sem(f"gathered{p}") for p in range(STREAMS)]
        idx_made, c_used, xg_used, x2_used = sem("idx_made"), sem("ctx_used"), sem("routed_used"), sem("x2_used")
        zeroed, x3b_made, x3n_made = sem("v_zeroed"), sem("x3_ln_b_made"), sem("x3_normed")
        vstep, pstep = sem("vector_step"), sem("pool_step")
        var_made, veps_made, rstd_made, xn_made = sem("var_made"), sem("veps_made"), sem("rstd_made"), sem("xn_made")
        fvar_made, fveps_made, frstd_made, front_made = \
            sem("front_var_made"), sem("front_veps_made"), sem("front_rstd_made"), sem("front_made")
        normed = sem("cell_normed")
        stored = [sem(f"stored{p}") for p in range(STREAMS)]
        prod, prod_used = sem("product_made"), sem("product_used")
        sco, sco_used = sem("scores_made"), sem("scores_used")
        max_made, inv_made, norm_made = sem("max_made"), sem("inv_made"), sem("norm_made")
        turned, turned_used = sem("turned_made"), sem("turned_used")

        def banks(s):
            return [(b, r) for b in range((2, 1, 1, 1, 1, 1, 1, 0)[s]) for r in range(ROWS)]

        order = [(s, p) for s in range(1, STAGES) for p in range(STREAMS)]
        SLOTS = STREAMS * sum(len(banks(s)) for s in range(STAGES))
        PRODS = STREAMS * (5 + 7 + 4 * (NODES - 1) + 2)
        TURNED = SLOTS + STREAMS * NODES
        LNS = 2 * STREAMS
        VSTEPS = STREAMS * (3 + 2)
        assert PRODS % 2 == 0 and TURNED % 2 == 0

        def left_over(n):
            return [(1, (1, r)) for r in range(ROWS)] if n == 0 else \
                [(order[n - 1][1], k) for k in banks(order[n - 1][0])]

        def ahead(n):
            return [(order[n + 1][1], k) for k in banks(order[n + 1][0] - 1)] if n + 1 < len(order) else []

        block = es.enter_context(nc.Block())

        @block.sync
        def _(sp):
            def halves(a):
                return a.rearrange("(c p) n -> p c n", p=P)

            for t, a in ((wq[:], halves(io["L1_xattn_Wq"])), (w1[:], halves(io["L1_xattn_W1"])),
                         (w2[:], halves(io["L1_xattn_W2"])), (wk[:, 0], io["L1_xattn_Wk"][0:P]),
                         (wk[0:C1, 1], io["L1_xattn_Wk"][P:C]), (wv[:, 0], io["L1_xattn_Wv"][0:P]),
                         (wv[0:C1, 1], io["L1_xattn_Wv"][P:C]), (bq[:], io["L1_xattn_bq_cols"]),
                         (bk[:], io["L1_xattn_bk_cols"]), (bv[:], io["L1_xattn_bv_cols"]),
                         (b1[:], io["L1_xattn_b1_cols"]), (b2[:], io["L1_xattn_b2"].partition_broadcast(P)),
                         (ln_g[:], io["L1_ffn_ln_g"].partition_broadcast(P)),
                         (ln_b[:], io["L1_ffn_ln_b"].partition_broadcast(P))):
                sp.dma_start(t, a).then_inc(w_in, 16)
            for p in range(STREAMS):
                sp.dma_start(xg[:, p], rows(scratch["xn1"], 0, p)).then_inc(r_in[p], 16)
                sp.dma_start(x2[:, p], rows(scratch["x1"], 0, p)).then_inc(x_in[p], 16)
            with sp.Fori(0, TURNS) as g:
                for p in range(STREAMS):
                    sp.wait_ge(c_used, g * STREAMS + p + 1)
                    sp.dma_start(ct[:, p], rows(ctx, g, p)).then_inc(c_in[p], 16)
                for p in range(STREAMS):
                    sp.wait_ge(xg_used, g * STREAMS + p + 1)
                    sp.dma_start(xg[:, p], rows(scratch["xn1"][RT:], g, p)).then_inc(r_in[p], 16)
                for p in range(STREAMS):
                    sp.wait_ge(x2_used, g * STREAMS + p + 1)
                    sp.dma_start(x2[:, p], rows(scratch["x1"][RT:], g, p)).then_inc(x_in[p], 16)

        @block.gpsimd
        def _(pool):
            def gather(g, p):
                at = bass.ds(g * RT + p * PAIR, PAIR)
                nc.gpsimd.tensor_copy(idx[:, p], keep["slots"][:, at]).then_inc(idx_made, 1)
                pool.wait_ge(idx_made, g * 2 * STREAMS + 2 * p + 1)
                nc.gpsimd.tensor_copy(gate[:, p], keep["gate"][:, at]).then_inc(idx_made, 1)
                pool.wait_ge(idx_made, g * 2 * STREAMS + 2 * p + 2)
                pool.wait_ge(r_in[p], g * 16 + 16)
                nc.gpsimd.tensor_tensor(after_wait_pool[:], cst[:, 0:1], cst[:, 0:1], ALU.add)
                for b in range(PAIR):
                    nc.gpsimd.indirect_dma_start(
                        out=xg[:, p, b], out_offset=None, in_=scratch["y"],
                        in_offset=bass.IndirectOffsetOnAxis(ap=idx[:, p, b:b + 1], axis=0),
                        bounds_check=last_slot, oob_is_err=False).then_inc(gathered[p], 16)

            last_slot = pool.to_reg(scratch["y"].shape[0] - 1)
            nc.gpsimd.memset(vE[:], 0.0).then_inc(zeroed, 1)
            nc.gpsimd.memset(vO[:], 0.0).then_inc(zeroed, 1)
            for p in range(STREAMS):
                gather(0, p)
            pool.wait_ge(w_in, 16 * 14)

            def rsqrt_front(g, p):
                pool.wait_ge(fvar_made, g * STREAMS + p + 1)
                nc.gpsimd.tensor_tensor(vepsf[:, p], mvf[:, p, :, 1], cst[:, C_EPS5:C_EPS5 + 2], ALU.add).then_inc(fveps_made, 1)
                pool.wait_ge(fveps_made, g * STREAMS + p + 1)
                nc.gpsimd.tensor_tensor(rstdf[:, p], vepsf[:, p], cst[:, C_HALF:C_HALF + 2], ALU.pow).then_inc(frstd_made, 1)

            for p in range(STREAMS):
                rsqrt_front(0, p)
            with pool.Fori(0, TURNS) as g:
                t_var, t_inv = Tally(g, LNS), Tally(g, SLOTS)

                def rsqrt(p, eps):
                    n = t_var.up()
                    pool.wait_ge(var_made, n)
                    nc.gpsimd.tensor_tensor(veps[:, p], mv[:, p, :, 1], cst[:, eps:eps + 2], ALU.add).then_inc(veps_made, 1)
                    pool.wait_ge(veps_made, n)
                    nc.gpsimd.tensor_tensor(rstd[:, p], veps[:, p], cst[:, C_HALF:C_HALF + 2], ALU.pow).then_inc(rstd_made, 1)

                def wide(a):
                    return a.unsqueeze(1).broadcast_to([P, PAIR, D])

                def norms(some):
                    for p, (b, r) in some:
                        pool.wait_ge(inv_made, t_inv.up())
                        e = pr[:, p, b, r]
                        nc.gpsimd.tensor_tensor(e, e, rinv[:, p, b, r].unsqueeze(2).broadcast_to([P, 4, T]),
                                                ALU.mult).then_inc(norm_made, 1)

                norms([(p, k) for p in range(STREAMS) for k in banks(0)][:-ROWS])
                for n, (s, p) in enumerate(order):
                    norms(left_over(n))
                    if s == 1:
                        rsqrt(p, C_EPS5)
                    if s == 2:
                        pool.wait_ge(x3n_made, g * STREAMS + p + 1)
                        nc.gpsimd.tensor_tensor(x3[:, p], x3[:, p], wide(ln_b[:]), ALU.add).then_inc(x3b_made, 1)
                    if s == 3:
                        gather(g + 1, p)
                    if s == 5:
                        rsqrt_front(g + 1, p)
                    if s == STAGES - 1:
                        rsqrt(p, C_EPS6)
                        pool.wait_ge(normed, g * STREAMS + p + 1)
                        pool.wait_ge(stored[p], g * 16 + 16)
                        nc.gpsimd.tensor_tensor(fin[:, p], xn[:, p], wide(ln_g[:]), ALU.mult).then_inc(pstep, 1)
                        pool.wait_ge(pstep, 2 * STREAMS + g * 2 * STREAMS + 2 * p + 1)
                        pool.wait_ge(x3b_made, g * STREAMS + p + 1)
                        nc.gpsimd.tensor_tensor(fin[:, p], fin[:, p], x3[:, p], ALU.add).then_inc(pstep, 1)
            for p in range(STREAMS):
                pool.wait_ge(gathered[p], 16 * PAIR * (TURNS + 1))

        @block.scalar
        def _(act):
            with act.Fori(0, TURNS) as g:
                t_max, t_turn = Tally(g, SLOTS), Tally(g, TURNED)

                def evacuate(dst):
                    act.wait_ge(turned, t_turn.up())
                    nc.scalar.copy(dst, TB[(t_turn.n - 1) % 2][:]).then_inc(turned_used, 1)

                def turned_probs(some):
                    for _, (b, r) in some:
                        evacuate(pT[:, b, r])

                def exponentials(p, some):
                    for b, r in some:
                        act.wait_ge(max_made, t_max.up())
                        for j in range(4):
                            i = nc.scalar.activation(pr[:, p, b, r, j], S[r][:, j], ACT.Exp,
                                                     bias=nmax[:, p, b, r, j:j + 1],
                                                     accum_out=rsum[:, p, b, r, j:j + 1])
                        i.then_inc(sco_used, 1)

                def v(p):
                    evacuate(va[:, p].rearrange("t b (h f) -> t (b h) f", f=T))

                exponentials(0, banks(0))
                first = [(0, k) for k in banks(0)]
                turned_probs(first[:ROWS])
                exponentials(1, banks(0)[:ROWS])
                turned_probs(first[ROWS:])
                exponentials(1, banks(0)[ROWS:])
                for n, (s, p) in enumerate(order):
                    if s == 1:
                        turned_probs(ahead(n))
                        v(p)
                    elif s < STAGES - 1:
                        v(p)
                        turned_probs(ahead(n))
                    else:
                        turned_probs(ahead(n))
                    exponentials(p, banks(s))
                for p in range(STREAMS):
                    act.wait_ge(pstep, 2 * STREAMS + g * 2 * STREAMS + 2 * p + 2)
                    act.dma_start(rows(out, g, p), fin[:, p]).then_inc(stored[p], 16)
            for p in range(STREAMS):
                act.wait_ge(stored[p], 16 * TURNS + 16)

        @block.vector
        def _(dve):
            V = nc.vector
            for m, k in ((c_used, STREAMS), (prod_used, 2), (sco_used, ROWS), (turned_used, 2), (pstep, 2 * STREAMS),
                         *((m, 16) for m in stored)):
                dve.sem_inc(m, k)
            dve.wait_ge(zeroed, 2)
            dve.wait_ge(w_in, 16 * 14)

            def statistics(src, dst, made, stepped):
                for b in range(PAIR):
                    i = V.bn_stats(stats[:, b], src[:, b])
                i.then_inc(vstep, 1)
                dve.wait_ge(vstep, stepped)
                V.memset(after_wait[:], 0.0)
                for b in range(PAIR):
                    i = V.bn_aggr(dst[:, b], stats[:, b])
                i.then_inc(made, 1)

            def front_statistics(g, p, step):
                dve.wait_ge(x_in[p], g * 16 + 16)
                dve.wait_ge(gathered[p], g * 16 * PAIR + 16 * PAIR)
                for b in range(PAIR):
                    i = V.scalar_tensor_tensor(out=x2[:, p, b], in0=xg[:, p, b], scalar=gate[:, p, b:b + 1],
                                               in1=x2[:, p, b], op0=ALU.mult, op1=ALU.add)
                i.then_inc(vstep, 1)
                dve.wait_ge(vstep, step())
                statistics(x2[:, p], mvf[:, p], fvar_made, step())

            def front_norm(g, p):
                dve.wait_ge(frstd_made, g * STREAMS + p + 1)
                for b in range(PAIR):
                    i = V.tensor_scalar(xg[:, p, b], x2[:, p, b], mvf[:, p, b, 0:1], rstdf[:, p, b:b + 1],
                                        ALU.subtract, ALU.mult)
                i.then_inc(front_made, 1)

            before = Tally()
            for p in range(STREAMS):
                front_statistics(0, p, before.up)
            for p in range(STREAMS):
                front_norm(0, p)
            with dve.Fori(0, TURNS) as g:
                t_step, t_prod, t_sco = Tally(g, VSTEPS, 2 * STREAMS), Tally(g, PRODS), Tally(g, SLOTS)
                t_exp, t_rstd = Tally(g, SLOTS), Tally(g, LNS)

                def product():
                    dve.wait_ge(prod, t_prod.up())
                    return M[(t_prod.n - 1) % 2]

                def layer_norm(src, dst, p, made):
                    statistics(src, mv[:, p], var_made, t_step.up())
                    dve.wait_ge(rstd_made, t_rstd.up())
                    for b in range(PAIR):
                        i = V.tensor_scalar(dst[:, b], src[:, b], mv[:, p, b, 0:1], rstd[:, p, b:b + 1],
                                            ALU.subtract, ALU.mult)
                    i.then_inc(made, 1)

                def biased(dst, bias, then=None, scalar=None):
                    m = product()
                    for u in range(2):
                        i = V.tensor_scalar(dst[:, u], m[:, u], bias[:, u:u + 1], scalar,
                                            ALU.add, *([then] if then else []))
                    i.then_inc(prod_used, 1)

                def copied(dst):
                    m = product()
                    V.tensor_copy(dst, m[:]).then_inc(prod_used, 1)

                def maxima(p, some):
                    for b, r in some:
                        dve.wait_ge(sco, t_sco.up())
                        V.tensor_reduce(nmax[:, p, b, r], S[r][:], AX.X, ALU.max, negate=True).then_inc(max_made, 1)

                def inverses(some):
                    for p, (b, r) in some:
                        dve.wait_ge(sco_used, ROWS + t_exp.up())
                        V.reciprocal(rinv[:, p, b, r], rsum[:, p, b, r]).then_inc(inv_made, 1)

                def wide(a):
                    return a.unsqueeze(1).broadcast_to([P, PAIR, D])

                def front(p):
                    copied(nd[:, p, 1])
                    dve.sem_inc(xg_used, 1)
                    m = product()
                    V.tensor_copy(cT[:, p, 0], m[:, 0])
                    V.tensor_copy(cT[0:C1, p, 1], m[0:C1, 1]).then_inc(prod_used, 1)
                    biased(qT[:, p], bq, ALU.mult, 0.25)
                    m = product()
                    for u in range(2):
                        V.tensor_scalar(kT[:, p, u], m[:, u], bk[:, u:u + 1], cst[:, C_EVEN:C_EVEN + 1], ALU.add, ALU.mult)
                        i = V.tensor_scalar(kO[:, p, u], m[:, u], bk[:, u:u + 1], cst[:, C_ODD:C_ODD + 1], ALU.add, ALU.mult)
                    i.then_inc(prod_used, 1)
                    m = product()
                    for v, o in ((vE, 0), (vO, 16)):
                        i = V.tensor_copy(v[:, p].rearrange("t b (h f) -> t (b h) f", f=32)[:, :, o:o + 16],
                                          m[:].rearrange("t b (h f) -> t (b h) f", f=32)[:, :, o:o + 16])
                    i.then_inc(prod_used, 1)

                rounds = [(p, banks(0)[b * ROWS:(b + 1) * ROWS]) for p in range(STREAMS) for b in range(PAIR)]
                front(0)
                maxima(*rounds[0])
                front(1)
                for n in range(1, len(rounds)):
                    inverses([(rounds[n - 1][0], k) for k in rounds[n - 1][1]])
                    maxima(*rounds[n])
                for n, (s, p) in enumerate(order):
                    late = left_over(n)
                    if s == 1:
                        biased(oT[:, p], bv)
                        for h in range(HID // 2):
                            m = product()
                            for u in range(2):
                                i = V.tensor_scalar(hid[:, p, 2 * h + u], m[:, u], b1[:, 2 * h + u:2 * h + u + 1], 0.0,
                                                    ALU.add, ALU.max)
                            i.then_inc(prod_used, 1)
                            if h == 0:
                                inverses(late)
                        m = product()
                        V.tensor_tensor(xn[:, p], m[:], wide(b2[:]), ALU.add).then_inc(prod_used, 1)
                        dve.wait_ge(prod_used, 2 + t_prod.now())
                        dve.wait_ge(pstep, g * 2 * STREAMS + 2 * p + 2)
                        V.tensor_tensor(x3[:, p], xn[:, p], x2[:, p], ALU.add).then_inc(vstep, 1)
                        dve.wait_ge(vstep, t_step.up())
                        dve.sem_inc(x2_used, 1)
                        layer_norm(x3[:, p], xn[:, p], p, xn_made)
                        dve.wait_ge(xn_made, g * STREAMS + p + 1)
                        dve.sem_inc(x3n_made, 1)
                        copied(nd[:, p, SLOT_OF[-1]])
                        biased(qT[:, p], fb[:, 0, TO_Q])
                        biased(kT[:, p], fb[:, 0, TO_K])
                        maxima(p, banks(s))
                    elif s < STAGES - 1:
                        c = s - 1
                        biased(oT[:, p], fb[:, c - 1, TO_V])
                        biased(kT[:, p], fb[:, c, TO_K])
                        inverses(late[:2])
                        biased(nd[:, p, SLOT_OF[c - 1]], fb[:, c - 1, EDGE])
                        inverses(late[2:])
                        biased(qT[:, p], fb[:, c, TO_Q])
                        maxima(p, banks(s))
                        if s == 4:
                            front_statistics(g + 1, p, t_step.up)
                        if s == 5:
                            front_norm(g + 1, p)
                    else:
                        biased(oT[:, p], fb[:, NODES - 1, TO_V])
                        inverses(late)
                        m = product()
                        V.tensor_tensor(xn[:, p], m[:], wide(row5[:]), ALU.add).then_inc(prod_used, 1)
                        dve.wait_ge(prod_used, 2 + t_prod.now())
                        layer_norm(xn[:, p], xn[:, p], p, normed)
                assert (t_step.n, t_prod.n, t_sco.n, t_rstd.n) == (VSTEPS, PRODS, SLOTS, LNS), (t_step.n, t_prod.n, t_sco.n, t_rstd.n)

        @block.tensor
        def _(pe):
            ident = cst[:, C_ID:C_ID + P]
            T_ = nc.tensor
            pe.wait_ge(w_in, 16 * 14)
            with pe.Fori(0, TURNS) as g:
                t_free, t_sfree, t_norm = Tally(g, PRODS), Tally(g, SLOTS), Tally(g, SLOTS)
                t_turn = Tally(g, TURNED)

                def bank():
                    pe.wait_ge(prod_used, t_free.up())
                    return M[(t_free.n - 1) % 2]

                def turn_bank():
                    pe.wait_ge(turned_used, t_turn.up())
                    return TB[(t_turn.n - 1) % 2]

                def landed(back=0):
                    pe.wait_ge(prod_used, 2 + t_free.now() - back)

                def turn_rows(src):
                    m = bank()
                    for b in range(PAIR):
                        for u in range(2):
                            w = min(P, src.shape[2] - u * P)
                            i = T_.transpose(m[0:w, u, b * T:(b + 1) * T], src[:, b, u * P:u * P + w], ident)
                    i.then_inc(prod, 1)

                def project(*terms, K1=P):
                    m = bank()
                    last = len(terms) * 2 - 1
                    for u in range(2):
                        n = 0
                        for w, src in terms:
                            for k in range(2):
                                K = K1 if k else P
                                i = T_.matmul(m[:, u], w[0:K, k, u * P:(u + 1) * P], src[0:K, k], start=n == 0, stop=n == last)
                                n += 1
                    i.then_inc(prod, 1)

                def rows_of(m, b, terms, K1=P):
                    steps = [(w, src, k) for w, src in terms for k in range(w.shape[1])]
                    for n, (w, src, k) in enumerate(steps):
                        K = K1 if k == 1 else P
                        i = T_.matmul(m, src[0:K, k, b * T:(b + 1) * T], w[0:K, k], start=n == 0, stop=n == len(steps) - 1)
                    return i

                def project_rows(*terms, K1=P):
                    m = bank()
                    for b in range(PAIR):
                        i = rows_of(m[:, b], b, terms, K1)
                    i.then_inc(prod, 1)

                def scores(p, j, u, b, k):
                    for r in range(ROWS):
                        if j == 0:
                            pe.wait_ge(sco_used, t_sfree.up())
                        q = slice(32 * r, 32 * r + 32)
                        i = T_.matmul(S[r][:, j], qT[q, p, u, b * T:(b + 1) * T], k[q, p, u, b * T:(b + 1) * T],
                                      start=True, stop=True)
                        if j == 3:
                            i.then_inc(sco, 1)

                def turn_probs(some):
                    for p, (b, r) in some:
                        pe.wait_ge(norm_made, t_norm.up())
                        m = turn_bank()
                        for j in range(4):
                            i = T_.transpose(m[:, j], pr[:, p, b, r, j], ident)
                        i.then_inc(turned, 1)

                def v_of(p, c, between=lambda: None):
                    m = turn_bank()
                    src = nd[:, p, SLOT_OF[plan[c]["src"][TO_V]]]
                    for b in range(PAIR):
                        i = rows_of(m[:, 2 * b:2 * b + 2].rearrange("t a f -> t (a f)"), b, [(fw[:, c, TO_V], src)])
                        if b == 0:
                            between()
                    i.then_inc(turned, 1)

                def node_scores(p, js):
                    for j in js:
                        scores(p, j, j % 2, j // 2, kT)

                def attend(p, pairs):
                    pe.wait_ge(turned_used, 2 + t_turn.now())
                    m = bank()
                    for b, u, v, start, stop, row, j in pairs:
                        for r in range(ROWS):
                            h = 32 * (4 * u + r)
                            i = T_.matmul(m[32 * r:32 * r + 32, u, b * T:(b + 1) * T], v[:, p, b, h:h + 32],
                                          pT[:, row, r, j], start=start, stop=stop)
                    i.then_inc(prod, 1)

                def front(p):
                    pe.wait_ge(front_made, g * STREAMS + p + 1)
                    turn_rows(xg[:, p])
                    pe.wait_ge(c_in[p], g * 16 + 16)
                    turn_rows(ct[:, p])
                    landed(1)
                    project((wq, nd[:, p, 1]))
                    landed(1)
                    pe.sem_inc(c_used, 1)
                    project((wk, cT[:, p]), K1=C1)
                    project_rows((wv, cT[:, p]), K1=C1)
                    landed(1)

                def layer_scores(p, b):
                    for j in range(4):
                        scores(p, j, j // 2, b, (kT, kO)[j % 2])

                front(0)
                layer_scores(0, 0)
                front(1)
                layer_scores(0, 1)
                first = [(0, k) for k in banks(0)]
                turn_probs(first[:ROWS])
                layer_scores(1, 0)
                turn_probs(first[ROWS:])
                layer_scores(1, 1)
                for n, (s, p) in enumerate(order):
                    some = ahead(n)
                    if s == 1:
                        attend(p, [(b, j // 2, (vE, vO)[j % 2], j % 2 == 0, j % 2 == 1, b, j)
                                         for b in range(PAIR) for j in range(4)])
                        turn_probs(some[:-ROWS])
                        landed()
                        for h in range(HID // 2):
                            project((w1[:, :, 2 * h * P:(2 * h + 2) * P], oT[:, p]))
                        landed()
                        project_rows((w2, hid[:, p]))
                        turn_probs(some[-ROWS:])
                        pe.wait_ge(xn_made, g * STREAMS + p + 1)
                        turn_rows(xn[:, p])
                        landed()
                        project((fw[:, 0, TO_Q], nd[:, p, SLOT_OF[-1]]))
                        project((fw[:, 0, TO_K], nd[:, p, SLOT_OF[-1]]))

                        def half():
                            landed()
                            node_scores(p, (0, 1))

                        v_of(p, 0, half)
                        node_scores(p, (2, 3))
                    elif s < STAGES - 1:
                        c = s - 1
                        attend(p, [(j // 2, j % 2, va, True, True, 0, j) for j in range(4)])
                        project((fw[:, c, TO_K], nd[:, p, SLOT_OF[plan[c]["src"][TO_K]]]))
                        landed(1)
                        project((fw[:, c - 1, OUT], oT[:, p]), (fw[:, c - 1, EDGE], nd[:, p, SLOT_OF[c - 2]]))
                        if c >= 2:
                            v_of(p, c)
                        landed()
                        project((fw[:, c, TO_Q], nd[:, p, SLOT_OF[c - 1]]))
                        if c == 1:
                            v_of(p, c)
                        turn_probs(some[:2])
                        landed()
                        node_scores(p, (0, 1))
                        turn_probs(some[2:])
                        node_scores(p, (2, 3))
                    else:
                        last = NODES - 1
                        attend(p, [(j // 2, j % 2, va, True, True, 0, j) for j in range(4)])
                        landed()
                        project_rows((fw[:, last, OUT], oT[:, p]), (fw[:, last, EDGE], nd[:, p, SLOT_OF[last - 1]]))
                        turn_probs(some)

def build(nc, io, out):
    B, T, D = io["x"].shape
    E = io["L0_ffn_w_switch"].shape[1]
    CAP = int(CAP_FACTOR * B * T / E)
    AHEAD = PAIR * STREAMS
    scratch = {n: nc.dram_tensor(n, s, F32, kind="Internal").ap() for n, s in (
        ("x1", (B + AHEAD, T, D)), ("xn1", (B + AHEAD, T, D)), ("buf", (E * CAP, D)), ("y", (E * CAP, D)))}
    with ExitStack() as es:
        def sb(name, shape, dt=F32):
            return es.enter_context(nc.sbuf_tensor(name, [P] + shape, dt))

        cst = sb("consts_sb", [C_END])
        keep = {"logits": sb("logits", [B, E]), "gate": sb("gates", [B + AHEAD]), "slots": sb("slots", [B + AHEAD], U32)}
        consts_in = es.enter_context(nc.semaphore("consts_in"))
        with nc.Block() as block:
            @block.sync
            def _(sp):
                sp.dma_start(cst[:], io["consts"]).then_inc(consts_in, 16)
                sp.wait_ge(consts_in, 16)
        phase_first_attention(nc, io, scratch, keep, cst)
        phase_route(nc, io, scratch, keep, cst)
        phase_experts(nc, io, scratch, cst)
        fw = sb("cell_w", [NODES, KINDS, 2, D])
        fb = sb("cell_b", [NODES, KINDS - 1, 2])
        row5 = sb("last_edge_b", [D])
        phase_fuse(nc, io, fw, fb, row5, cst)
        phase_second_layer(nc, io, scratch, keep, fw, fb, row5, cst, out)


_PLAIN = ["x", "ctx_768", "L0_xattn_Wq", "L0_xattn_Wk", "L0_xattn_Wv", "L0_xattn_Wo", "L0_ffn_w_switch",
          "L0_ffn_b_switch", "L0_ffn_w1", "L0_ffn_w2", "L0_ffn_b2",
          "L1_xattn_Wq", "L1_xattn_Wk", "L1_xattn_Wv", "L1_xattn_W1", "L1_xattn_W2", "L1_xattn_b2",
          "L1_ffn_ew", "L1_ffn_act_w", "L1_ffn_We", "L1_ffn_be", "L1_ffn_Wq", "L1_ffn_Wk", "L1_ffn_Wv",
          "L1_ffn_Wo", "L1_ffn_ln_g", "L1_ffn_ln_b"]


def lay_out(inputs):
    arrays = {n: np.ascontiguousarray(inputs[n]) for n in _PLAIN}
    arrays["mask_BxS2_bf1"] = np.ascontiguousarray(inputs["mask_BxS2_bf1"]).view(np.uint8)
    b1 = np.asarray(inputs["L0_ffn_b1"])
    arrays["b1_cols"] = np.ascontiguousarray(b1.reshape(b1.shape[0], -1, P).transpose(0, 2, 1))
    for n in ("bq", "bk", "bv", "b1"):
        arrays[f"L1_xattn_{n}_cols"] = np.ascontiguousarray(np.asarray(inputs[f"L1_xattn_{n}"]).reshape(-1, P).T)
    be = np.asarray(inputs["L1_ffn_be"])
    arrays["be_cols"] = np.ascontiguousarray(be.reshape(be.shape[0], -1, P).transpose(2, 1, 0))
    arrays["edgesT"] = np.ascontiguousarray(np.asarray(inputs["L1_ffn_We"]).transpose(0, 2, 1))
    arrays["consts"] = consts_array()
    return arrays


def kernel(**inputs):
    import concourse.bacc as bacc
    from concourse.bass_utils import run_bass_kernel_spmd

    nc = bacc.Bacc("TRN2", target_bir_lowering=False, num_devices=1)
    arrays = {f"in_{n}": a for n, a in lay_out(inputs).items()}
    io = {n[3:]: nc.dram_tensor(n, a.shape, mybir.dt.from_np(a.dtype), kind="ExternalInput").ap()
          for n, a in arrays.items()}
    out = nc.dram_tensor("out", io["x"].shape, F32, kind="ExternalOutput").ap()
    build(nc, io, out)
    return run_bass_kernel_spmd(nc, [arrays], core_ids=[0]).results[0]["out"]
```
